# Optimizing a Trainium2 kernel written in Bass

```python
import numpy as np
import jax
import jax.numpy as jnp

def _softmax(x, axis=-1):
    return jax.nn.softmax(x, axis=axis)
def _gelu(x):
    return jax.nn.gelu(x, approximate=True)
def _silu(x):
    return jax.nn.silu(x)
def _sigmoid(x):
    return jax.nn.sigmoid(x)
def _layernorm(x, axis=-1, eps=1e-5):
    m = jnp.mean(x, axis=axis, keepdims=True)
    v = jnp.var(x, axis=axis, keepdims=True)
    return (x - m) / jnp.sqrt(v + eps)
def _scatter_add(tgt, idx, src, axis=0):
    return tgt.at[idx].add(src)
def _segment_sum(src, seg, n):
    return jax.ops.segment_sum(src, seg, n)

kernel_name = 'mk_conv_seq_d4_conv_nhwc128_7061f4'

def setup_inputs(seed: int = 0):
    np.random.seed(seed)
    _w = jnp.asarray
    def _rec_inputs():
        import jax
        import jax.numpy as jnp
        _gk = jax.random.key(seed)
        x = -0.0005207 + 1.001 * jax.random.normal(jax.random.fold_in(_gk, 1), (4, 64, 64, 128), jnp.float32)
        return x
    x = _rec_inputs()
    def _L0_conv_setup():
        import jax, jax.numpy as jnp
        import numpy as np
        B, H, W, C = (4, 64, 64, 128)
        DI, N, R, K = (256, 16, 8, 4)

        def _ln(x, w, b):
            mu = x.mean(-1, keepdims=True)
            var = ((x - mu) ** 2).mean(-1, keepdims=True)
            return (x - mu) * jax.lax.rsqrt(var + 1e-05) * w + b

        def _silu(x):
            return x * jax.nn.sigmoid(x)

        def _forward(input, ln1_w, ln1_b, in_proj_w, conv_w, conv_b, x_proj_w, dt_w, dt_b, A_log, Ds, onorm_w, onorm_b, out_proj_w, ln2_w, ln2_b, fc1_w, fc1_b, fc2_w, fc2_b):
            Bn, Hh, Ww, Cc = input.shape
            L = Hh * Ww
            xn = _ln(input, ln1_w, ln1_b)
            xz = xn @ in_proj_w
            x_, z = jnp.split(xz, 2, axis=-1)
            xc = jnp.transpose(x_, (0, 3, 1, 2))
            xc = jax.lax.conv_general_dilated(xc, conv_w, (1, 1), 'SAME', feature_group_count=DI, dimension_numbers=('NCHW', 'OIHW', 'NCHW')) + conv_b[None, :, None, None]
            xc = _silu(xc)
            x0 = xc.reshape(Bn, DI, L)
            x1 = jnp.transpose(xc, (0, 1, 3, 2)).reshape(Bn, DI, L)
            xs = jnp.stack([x0, x1, x0[..., ::-1], x1[..., ::-1]], axis=1)
            x_dbl = jnp.einsum('bkdl,kcd->bkcl', xs, x_proj_w)
            dts, Bs, Cs = jnp.split(x_dbl, [R, R + N], axis=2)
            dts = jnp.einsum('bkrl,kdr->bkdl', dts, dt_w)
            delta = jax.nn.softplus(dts + dt_b[None, :, :, None])
            A = -jnp.exp(A_log).reshape(K, DI, N)

            def step(h, t):
                x_t, d_t, B_t, C_t = t
                h = jnp.exp(d_t[..., None] * A) * h + (d_t * x_t)[..., None] * B_t[:, :, None, :]
                return (h, jnp.einsum('bkdn,bkn->bkd', h, C_t))
            scan_in = (jnp.moveaxis(xs, -1, 0), jnp.moveaxis(delta, -1, 0), jnp.moveaxis(Bs, -1, 0), jnp.moveaxis(Cs, -1, 0))
            h0 = jnp.zeros((Bn, K, DI, N), input.dtype)
            _, ys_l = jax.lax.scan(step, h0, scan_in)
            ys = jnp.moveaxis(ys_l, 0, -1) + Ds.reshape(K, DI)[None, :, :, None] * xs
            ym = ys[:, :2] + ys[:, 2:, :, ::-1]
            y = ym[:, 0] + jnp.transpose(ym[:, 1].reshape(Bn, DI, Ww, Hh), (0, 1, 3, 2)).reshape(Bn, DI, L)
            y = _ln(jnp.transpose(y, (0, 2, 1)), onorm_w, onorm_b).reshape(Bn, Hh, Ww, DI)
            y = y * _silu(z)
            x = input + y @ out_proj_w
            h2 = _ln(x, ln2_w, ln2_b)
            h2 = jax.nn.gelu(h2 @ fc1_w + fc1_b, approximate=False) @ fc2_w + fc2_b
            return x + h2
        key = jax.random.key(seed)
        ks = jax.random.split(key, 16)
        g = lambda i, shape, s=0.02: jax.random.normal(ks[i], shape, jnp.float32) * s
        return {'input': jax.random.normal(ks[0], (B, H, W, C), jnp.float32), 'ln1_w': jnp.ones((C,), jnp.float32), 'ln1_b': jnp.zeros((C,), jnp.float32), 'in_proj_w': g(1, (C, 2 * DI)), 'conv_w': g(2, (DI, 1, 3, 3), 0.1), 'conv_b': jnp.zeros((DI,), jnp.float32), 'x_proj_w': g(3, (K, R + 2 * N, DI)), 'dt_w': g(4, (K, DI, R), 0.1), 'dt_b': g(5, (K, DI), 0.1), 'A_log': jnp.tile(jnp.log(jnp.arange(1, N + 1, dtype=jnp.float32)), (K * DI, 1)), 'Ds': jnp.ones((K * DI,), jnp.float32), 'onorm_w': jnp.ones((DI,), jnp.float32), 'onorm_b': jnp.zeros((DI,), jnp.float32), 'out_proj_w': g(6, (DI, C)), 'ln2_w': jnp.ones((C,), jnp.float32), 'ln2_b': jnp.zeros((C,), jnp.float32), 'fc1_w': g(7, (C, 4 * C)), 'fc1_b': jnp.zeros((4 * C,), jnp.float32), 'fc2_w': g(8, (4 * C, C)), 'fc2_b': jnp.zeros((C,), jnp.float32)}
    _L0_conv_all = _L0_conv_setup()
    _L0_conv_in = {k: v for k, v in _L0_conv_all.items() if k in ('ln1_w', 'ln1_b', 'in_proj_w', 'conv_w', 'conv_b', 'x_proj_w', 'dt_w', 'dt_b', 'A_log', 'Ds', 'onorm_w', 'onorm_b', 'out_proj_w', 'ln2_w', 'ln2_b', 'fc1_w', 'fc1_b', 'fc2_w', 'fc2_b', )}
    del _L0_conv_all

    def _L1_conv_setup():
        import jax, jax.numpy as jnp
        import numpy as np

        def _ln(x, w, b, eps=1e-05):
            mu = jnp.mean(x, axis=-1, keepdims=True)
            var = jnp.var(x, axis=-1, keepdims=True)
            return (x - mu) * jax.lax.rsqrt(var + eps) * w + b

        def _vss_forward(x, norm1_w, norm1_b, in_proj_w, conv_w, conv_b, x_proj_w, dt_projs_w, dt_projs_b, A_logs, Ds, out_norm_w, out_norm_b, out_proj_w, norm2_w, norm2_b, fc1_w, fc1_b, fc2_w, fc2_b):
            B, H, W, C = x.shape
            Di = in_proj_w.shape[0] // 2
            K = x_proj_w.shape[0]
            R = dt_projs_w.shape[2]
            N = A_logs.shape[1]
            L = H * W
            xn = _ln(x, norm1_w, norm1_b)
            xz = jnp.einsum('bhwc,ec->bhwe', xn, in_proj_w)
            xx, z = jnp.split(xz, 2, axis=-1)
            xb = xx.transpose(0, 3, 1, 2)
            xb = jax.lax.conv_general_dilated(xb, conv_w, window_strides=(1, 1), padding=((1, 1), (1, 1)), dimension_numbers=('NCHW', 'OIHW', 'NCHW'), feature_group_count=Di)
            xb = jax.nn.silu(xb + conv_b[None, :, None, None])
            x0 = xb.reshape(B, Di, L)
            x1 = xb.transpose(0, 1, 3, 2).reshape(B, Di, L)
            xs = jnp.stack([x0, x1, x0[..., ::-1], x1[..., ::-1]], axis=1)
            x_dbl = jnp.einsum('bkdl,kcd->bkcl', xs, x_proj_w)
            dts, Bsm, Csm = jnp.split(x_dbl, [R, R + N], axis=2)
            dt = jnp.einsum('bkrl,kdr->bkdl', dts, dt_projs_w)
            dt = jax.nn.softplus(dt + dt_projs_b[None, :, :, None])
            A = -jnp.exp(A_logs).reshape(K, Di, N)

            def step(h, t):
                dt_t, u_t, B_t, C_t = t
                h = h * jnp.exp(dt_t[..., None] * A) + (dt_t * u_t)[..., None] * B_t[:, :, None, :]
                y = jnp.einsum('bkdn,bkn->bkd', h, C_t)
                return (h, y)
            ts = (dt.transpose(3, 0, 1, 2), xs.transpose(3, 0, 1, 2), Bsm.transpose(3, 0, 1, 2), Csm.transpose(3, 0, 1, 2))
            h0 = jnp.zeros((B, K, Di, N), dtype=x.dtype)
            _, ys = jax.lax.scan(step, h0, ts)
            ys = ys.transpose(1, 2, 3, 0)
            ys = ys + Ds.reshape(K, Di)[None, :, :, None] * xs
            y = ys[:, 0] + ys[:, 2, :, ::-1]
            yw = ys[:, 1] + ys[:, 3, :, ::-1]
            y = y + yw.reshape(B, Di, W, H).transpose(0, 1, 3, 2).reshape(B, Di, L)
            y = y.transpose(0, 2, 1).reshape(B, H, W, Di)
            y = _ln(y, out_norm_w, out_norm_b)
            y = y * jax.nn.silu(z)
            y = jnp.einsum('bhwd,cd->bhwc', y, out_proj_w)
            x = x + y
            xm = _ln(x, norm2_w, norm2_b)
            h = jax.nn.gelu(jnp.einsum('bhwc,fc->bhwf', xm, fc1_w) + fc1_b)
            x = x + jnp.einsum('bhwf,cf->bhwc', h, fc2_w) + fc2_b
            return x
        key = jax.random.key(seed)
        ks = jax.random.split(key, 12)
        B, H, W, C = (4, 64, 64, 128)
        Di, N, R, K = (256, 16, 8, 4)
        Cm = 4 * C
        w = lambda i, shape, s=0.02: jax.random.normal(ks[i], shape, jnp.float32) * s
        return {'x': jax.random.normal(ks[0], (B, H, W, C), jnp.float32), 'norm1_w': jnp.ones((C,), jnp.float32), 'norm1_b': jnp.zeros((C,), jnp.float32), 'in_proj_w': w(1, (2 * Di, C)), 'conv_w': w(2, (Di, 1, 3, 3), 0.1), 'conv_b': jnp.zeros((Di,), jnp.float32), 'x_proj_w': w(3, (K, R + 2 * N, Di)), 'dt_projs_w': w(4, (K, Di, R), 0.1), 'dt_projs_b': w(5, (K, Di), 0.1), 'A_logs': jnp.log(jnp.tile(jnp.arange(1, N + 1, dtype=jnp.float32), (K * Di, 1))), 'Ds': jnp.ones((K * Di,), jnp.float32), 'out_norm_w': jnp.ones((Di,), jnp.float32), 'out_norm_b': jnp.zeros((Di,), jnp.float32), 'out_proj_w': w(6, (C, Di)), 'norm2_w': jnp.ones((C,), jnp.float32), 'norm2_b': jnp.zeros((C,), jnp.float32), 'fc1_w': w(7, (Cm, C)), 'fc1_b': jnp.zeros((Cm,), jnp.float32), 'fc2_w': w(8, (C, Cm)), 'fc2_b': jnp.zeros((C,), jnp.float32)}
    _L1_conv_all = _L1_conv_setup()
    _L1_conv_in = {k: v for k, v in _L1_conv_all.items() if k in ('norm1_w', 'norm1_b', 'in_proj_w', 'conv_w', 'conv_b', 'x_proj_w', 'dt_projs_w', 'dt_projs_b', 'A_logs', 'Ds', 'out_norm_w', 'out_norm_b', 'out_proj_w', 'norm2_w', 'norm2_b', 'fc1_w', 'fc1_b', 'fc2_w', 'fc2_b', )}
    del _L1_conv_all

    def _L2_conv_setup():
        import jax, jax.numpy as jnp
        import numpy as np
        C = 128
        DW = 2 * C
        FF = 2 * C
        EPS = 1e-06

        def _layernorm(x, scale, bias):
            mu = jnp.mean(x, axis=-1, keepdims=True)
            var = jnp.mean(jnp.square(x - mu), axis=-1, keepdims=True)
            return (x - mu) * jax.lax.rsqrt(var + EPS) * scale + bias
        key = jax.random.key(seed)
        ks = jax.random.split(key, 20)
        s = 0.05
        return {'x': jax.random.normal(ks[0], (8, 192, 192, C), jnp.float32), 'ln1_scale': jnp.ones((C,), jnp.float32), 'ln1_bias': jnp.zeros((C,), jnp.float32), 'w1': jax.random.normal(ks[1], (C, DW), jnp.float32) * s, 'b1': jax.random.normal(ks[2], (DW,), jnp.float32) * s, 'wdw': jax.random.normal(ks[3], (DW,), jnp.float32) * s, 'bdw': jax.random.normal(ks[4], (DW,), jnp.float32) * s, 'wse': jax.random.normal(ks[5], (C, C), jnp.float32) * s, 'bse': jax.random.normal(ks[6], (C,), jnp.float32) * s, 'w2': jax.random.normal(ks[7], (C, C), jnp.float32) * s, 'b2': jax.random.normal(ks[8], (C,), jnp.float32) * s, 'ln2_scale': jnp.ones((C,), jnp.float32), 'ln2_bias': jnp.zeros((C,), jnp.float32), 'wf1': jax.random.normal(ks[9], (C, FF), jnp.float32) * s, 'bf1': jax.random.normal(ks[10], (FF,), jnp.float32) * s, 'wf2': jax.random.normal(ks[11], (C, C), jnp.float32) * s, 'bf2': jax.random.normal(ks[12], (C,), jnp.float32) * s, 'beta': jax.random.normal(ks[13], (1, 1, 1, C), jnp.float32) * s, 'gamma': jax.random.normal(ks[14], (1, 1, 1, C), jnp.float32) * s}
    _L2_conv_all = _L2_conv_setup()
    _L2_conv_in = {k: v for k, v in _L2_conv_all.items() if k in ('ln1_scale', 'ln1_bias', 'w1', 'b1', 'wdw', 'bdw', 'wse', 'bse', 'w2', 'b2', 'ln2_scale', 'ln2_bias', 'wf1', 'bf1', 'wf2', 'bf2', 'beta', 'gamma', )}
    del _L2_conv_all

    def _L3_conv_setup():
        import jax, jax.numpy as jnp
        import numpy as np

        def _ln(x, w, b, eps=1e-05):
            mu = jnp.mean(x, axis=-1, keepdims=True)
            var = jnp.var(x, axis=-1, keepdims=True)
            return (x - mu) * jax.lax.rsqrt(var + eps) * w + b

        def _vss_forward(x, norm1_w, norm1_b, in_proj_w, conv_w, conv_b, x_proj_w, dt_projs_w, dt_projs_b, A_logs, Ds, out_norm_w, out_norm_b, out_proj_w, norm2_w, norm2_b, fc1_w, fc1_b, fc2_w, fc2_b):
            B, H, W, C = x.shape
            Di = in_proj_w.shape[0] // 2
            K = x_proj_w.shape[0]
            R = dt_projs_w.shape[2]
            N = A_logs.shape[1]
            L = H * W
            xn = _ln(x, norm1_w, norm1_b)
            xz = jnp.einsum('bhwc,ec->bhwe', xn, in_proj_w)
            xx, z = jnp.split(xz, 2, axis=-1)
            xb = xx.transpose(0, 3, 1, 2)
            xb = jax.lax.conv_general_dilated(xb, conv_w, window_strides=(1, 1), padding=((1, 1), (1, 1)), dimension_numbers=('NCHW', 'OIHW', 'NCHW'), feature_group_count=Di)
            xb = jax.nn.silu(xb + conv_b[None, :, None, None])
            x0 = xb.reshape(B, Di, L)
            x1 = xb.transpose(0, 1, 3, 2).reshape(B, Di, L)
            xs = jnp.stack([x0, x1, x0[..., ::-1], x1[..., ::-1]], axis=1)
            x_dbl = jnp.einsum('bkdl,kcd->bkcl', xs, x_proj_w)
            dts, Bsm, Csm = jnp.split(x_dbl, [R, R + N], axis=2)
            dt = jnp.einsum('bkrl,kdr->bkdl', dts, dt_projs_w)
            dt = jax.nn.softplus(dt + dt_projs_b[None, :, :, None])
            A = -jnp.exp(A_logs).reshape(K, Di, N)

            def step(h, t):
                dt_t, u_t, B_t, C_t = t
                h = h * jnp.exp(dt_t[..., None] * A) + (dt_t * u_t)[..., None] * B_t[:, :, None, :]
                y = jnp.einsum('bkdn,bkn->bkd', h, C_t)
                return (h, y)
            ts = (dt.transpose(3, 0, 1, 2), xs.transpose(3, 0, 1, 2), Bsm.transpose(3, 0, 1, 2), Csm.transpose(3, 0, 1, 2))
            h0 = jnp.zeros((B, K, Di, N), dtype=x.dtype)
            _, ys = jax.lax.scan(step, h0, ts)
            ys = ys.transpose(1, 2, 3, 0)
            ys = ys + Ds.reshape(K, Di)[None, :, :, None] * xs
            y = ys[:, 0] + ys[:, 2, :, ::-1]
            yw = ys[:, 1] + ys[:, 3, :, ::-1]
            y = y + yw.reshape(B, Di, W, H).transpose(0, 1, 3, 2).reshape(B, Di, L)
            y = y.transpose(0, 2, 1).reshape(B, H, W, Di)
            y = _ln(y, out_norm_w, out_norm_b)
            y = y * jax.nn.silu(z)
            y = jnp.einsum('bhwd,cd->bhwc', y, out_proj_w)
            x = x + y
            xm = _ln(x, norm2_w, norm2_b)
            h = jax.nn.gelu(jnp.einsum('bhwc,fc->bhwf', xm, fc1_w) + fc1_b)
            x = x + jnp.einsum('bhwf,cf->bhwc', h, fc2_w) + fc2_b
            return x
        key = jax.random.key(seed)
        ks = jax.random.split(key, 12)
        B, H, W, C = (4, 64, 64, 128)
        Di, N, R, K = (256, 16, 8, 4)
        Cm = 4 * C
        w = lambda i, shape, s=0.02: jax.random.normal(ks[i], shape, jnp.float32) * s
        return {'x': jax.random.normal(ks[0], (B, H, W, C), jnp.float32), 'norm1_w': jnp.ones((C,), jnp.float32), 'norm1_b': jnp.zeros((C,), jnp.float32), 'in_proj_w': w(1, (2 * Di, C)), 'conv_w': w(2, (Di, 1, 3, 3), 0.1), 'conv_b': jnp.zeros((Di,), jnp.float32), 'x_proj_w': w(3, (K, R + 2 * N, Di)), 'dt_projs_w': w(4, (K, Di, R), 0.1), 'dt_projs_b': w(5, (K, Di), 0.1), 'A_logs': jnp.log(jnp.tile(jnp.arange(1, N + 1, dtype=jnp.float32), (K * Di, 1))), 'Ds': jnp.ones((K * Di,), jnp.float32), 'out_norm_w': jnp.ones((Di,), jnp.float32), 'out_norm_b': jnp.zeros((Di,), jnp.float32), 'out_proj_w': w(6, (C, Di)), 'norm2_w': jnp.ones((C,), jnp.float32), 'norm2_b': jnp.zeros((C,), jnp.float32), 'fc1_w': w(7, (Cm, C)), 'fc1_b': jnp.zeros((Cm,), jnp.float32), 'fc2_w': w(8, (C, Cm)), 'fc2_b': jnp.zeros((C,), jnp.float32)}
    _L3_conv_all = _L3_conv_setup()
    _L3_conv_in = {k: v for k, v in _L3_conv_all.items() if k in ('norm1_w', 'norm1_b', 'in_proj_w', 'conv_w', 'conv_b', 'x_proj_w', 'dt_projs_w', 'dt_projs_b', 'A_logs', 'Ds', 'out_norm_w', 'out_norm_b', 'out_proj_w', 'norm2_w', 'norm2_b', 'fc1_w', 'fc1_b', 'fc2_w', 'fc2_b', )}
    del _L3_conv_all

    return {
        "x": x,
        "L0_conv_ln1_w": _L0_conv_in["ln1_w"],
        "L0_conv_ln1_b": _L0_conv_in["ln1_b"],
        "L0_conv_in_proj_w": _L0_conv_in["in_proj_w"],
        "L0_conv_conv_w": _L0_conv_in["conv_w"],
        "L0_conv_conv_b": _L0_conv_in["conv_b"],
        "L0_conv_x_proj_w": _L0_conv_in["x_proj_w"],
        "L0_conv_dt_w": _L0_conv_in["dt_w"],
        "L0_conv_dt_b": _L0_conv_in["dt_b"],
        "L0_conv_A_log": _L0_conv_in["A_log"],
        "L0_conv_Ds": _L0_conv_in["Ds"],
        "L0_conv_onorm_w": _L0_conv_in["onorm_w"],
        "L0_conv_onorm_b": _L0_conv_in["onorm_b"],
        "L0_conv_out_proj_w": _L0_conv_in["out_proj_w"],
        "L0_conv_ln2_w": _L0_conv_in["ln2_w"],
        "L0_conv_ln2_b": _L0_conv_in["ln2_b"],
        "L0_conv_fc1_w": _L0_conv_in["fc1_w"],
        "L0_conv_fc1_b": _L0_conv_in["fc1_b"],
        "L0_conv_fc2_w": _L0_conv_in["fc2_w"],
        "L0_conv_fc2_b": _L0_conv_in["fc2_b"],
        "L1_conv_norm1_w": _L1_conv_in["norm1_w"],
        "L1_conv_norm1_b": _L1_conv_in["norm1_b"],
        "L1_conv_in_proj_w": _L1_conv_in["in_proj_w"],
        "L1_conv_conv_w": _L1_conv_in["conv_w"],
        "L1_conv_conv_b": _L1_conv_in["conv_b"],
        "L1_conv_x_proj_w": _L1_conv_in["x_proj_w"],
        "L1_conv_dt_projs_w": _L1_conv_in["dt_projs_w"],
        "L1_conv_dt_projs_b": _L1_conv_in["dt_projs_b"],
        "L1_conv_A_logs": _L1_conv_in["A_logs"],
        "L1_conv_Ds": _L1_conv_in["Ds"],
        "L1_conv_out_norm_w": _L1_conv_in["out_norm_w"],
        "L1_conv_out_norm_b": _L1_conv_in["out_norm_b"],
        "L1_conv_out_proj_w": _L1_conv_in["out_proj_w"],
        "L1_conv_norm2_w": _L1_conv_in["norm2_w"],
        "L1_conv_norm2_b": _L1_conv_in["norm2_b"],
        "L1_conv_fc1_w": _L1_conv_in["fc1_w"],
        "L1_conv_fc1_b": _L1_conv_in["fc1_b"],
        "L1_conv_fc2_w": _L1_conv_in["fc2_w"],
        "L1_conv_fc2_b": _L1_conv_in["fc2_b"],
        "L2_conv_ln1_scale": _L2_conv_in["ln1_scale"],
        "L2_conv_ln1_bias": _L2_conv_in["ln1_bias"],
        "L2_conv_w1": _L2_conv_in["w1"],
        "L2_conv_b1": _L2_conv_in["b1"],
        "L2_conv_wdw": _L2_conv_in["wdw"],
        "L2_conv_bdw": _L2_conv_in["bdw"],
        "L2_conv_wse": _L2_conv_in["wse"],
        "L2_conv_bse": _L2_conv_in["bse"],
        "L2_conv_w2": _L2_conv_in["w2"],
        "L2_conv_b2": _L2_conv_in["b2"],
        "L2_conv_ln2_scale": _L2_conv_in["ln2_scale"],
        "L2_conv_ln2_bias": _L2_conv_in["ln2_bias"],
        "L2_conv_wf1": _L2_conv_in["wf1"],
        "L2_conv_bf1": _L2_conv_in["bf1"],
        "L2_conv_wf2": _L2_conv_in["wf2"],
        "L2_conv_bf2": _L2_conv_in["bf2"],
        "L2_conv_beta": _L2_conv_in["beta"],
        "L2_conv_gamma": _L2_conv_in["gamma"],
        "L3_conv_norm1_w": _L3_conv_in["norm1_w"],
        "L3_conv_norm1_b": _L3_conv_in["norm1_b"],
        "L3_conv_in_proj_w": _L3_conv_in["in_proj_w"],
        "L3_conv_conv_w": _L3_conv_in["conv_w"],
        "L3_conv_conv_b": _L3_conv_in["conv_b"],
        "L3_conv_x_proj_w": _L3_conv_in["x_proj_w"],
        "L3_conv_dt_projs_w": _L3_conv_in["dt_projs_w"],
        "L3_conv_dt_projs_b": _L3_conv_in["dt_projs_b"],
        "L3_conv_A_logs": _L3_conv_in["A_logs"],
        "L3_conv_Ds": _L3_conv_in["Ds"],
        "L3_conv_out_norm_w": _L3_conv_in["out_norm_w"],
        "L3_conv_out_norm_b": _L3_conv_in["out_norm_b"],
        "L3_conv_out_proj_w": _L3_conv_in["out_proj_w"],
        "L3_conv_norm2_w": _L3_conv_in["norm2_w"],
        "L3_conv_norm2_b": _L3_conv_in["norm2_b"],
        "L3_conv_fc1_w": _L3_conv_in["fc1_w"],
        "L3_conv_fc1_b": _L3_conv_in["fc1_b"],
        "L3_conv_fc2_w": _L3_conv_in["fc2_w"],
        "L3_conv_fc2_b": _L3_conv_in["fc2_b"],
    }

def reference(x, L0_conv_ln1_w, L0_conv_ln1_b, L0_conv_in_proj_w, L0_conv_conv_w, L0_conv_conv_b, L0_conv_x_proj_w, L0_conv_dt_w, L0_conv_dt_b, L0_conv_A_log, L0_conv_Ds, L0_conv_onorm_w, L0_conv_onorm_b, L0_conv_out_proj_w, L0_conv_ln2_w, L0_conv_ln2_b, L0_conv_fc1_w, L0_conv_fc1_b, L0_conv_fc2_w, L0_conv_fc2_b, L1_conv_norm1_w, L1_conv_norm1_b, L1_conv_in_proj_w, L1_conv_conv_w, L1_conv_conv_b, L1_conv_x_proj_w, L1_conv_dt_projs_w, L1_conv_dt_projs_b, L1_conv_A_logs, L1_conv_Ds, L1_conv_out_norm_w, L1_conv_out_norm_b, L1_conv_out_proj_w, L1_conv_norm2_w, L1_conv_norm2_b, L1_conv_fc1_w, L1_conv_fc1_b, L1_conv_fc2_w, L1_conv_fc2_b, L2_conv_ln1_scale, L2_conv_ln1_bias, L2_conv_w1, L2_conv_b1, L2_conv_wdw, L2_conv_bdw, L2_conv_wse, L2_conv_bse, L2_conv_w2, L2_conv_b2, L2_conv_ln2_scale, L2_conv_ln2_bias, L2_conv_wf1, L2_conv_bf1, L2_conv_wf2, L2_conv_bf2, L2_conv_beta, L2_conv_gamma, L3_conv_norm1_w, L3_conv_norm1_b, L3_conv_in_proj_w, L3_conv_conv_w, L3_conv_conv_b, L3_conv_x_proj_w, L3_conv_dt_projs_w, L3_conv_dt_projs_b, L3_conv_A_logs, L3_conv_Ds, L3_conv_out_norm_w, L3_conv_out_norm_b, L3_conv_out_proj_w, L3_conv_norm2_w, L3_conv_norm2_b, L3_conv_fc1_w, L3_conv_fc1_b, L3_conv_fc2_w, L3_conv_fc2_b):
    import jax
    import jax.numpy as jnp
    def _L0_conv_ref(input, ln1_w, ln1_b, in_proj_w, conv_w, conv_b, x_proj_w, dt_w, dt_b, A_log, Ds, onorm_w, onorm_b, out_proj_w, ln2_w, ln2_b, fc1_w, fc1_b, fc2_w, fc2_b):
        import jax, jax.numpy as jnp
        import numpy as np
        B, H, W, C = (4, 64, 64, 128)
        DI, N, R, K = (256, 16, 8, 4)

        def _ln(x, w, b):
            mu = x.mean(-1, keepdims=True)
            var = ((x - mu) ** 2).mean(-1, keepdims=True)
            return (x - mu) * jax.lax.rsqrt(var + 1e-05) * w + b

        def _silu(x):
            return x * jax.nn.sigmoid(x)

        def _forward(input, ln1_w, ln1_b, in_proj_w, conv_w, conv_b, x_proj_w, dt_w, dt_b, A_log, Ds, onorm_w, onorm_b, out_proj_w, ln2_w, ln2_b, fc1_w, fc1_b, fc2_w, fc2_b):
            Bn, Hh, Ww, Cc = input.shape
            L = Hh * Ww
            xn = _ln(input, ln1_w, ln1_b)
            xz = xn @ in_proj_w
            x_, z = jnp.split(xz, 2, axis=-1)
            xc = jnp.transpose(x_, (0, 3, 1, 2))
            xc = jax.lax.conv_general_dilated(xc, conv_w, (1, 1), 'SAME', feature_group_count=DI, dimension_numbers=('NCHW', 'OIHW', 'NCHW')) + conv_b[None, :, None, None]
            xc = _silu(xc)
            x0 = xc.reshape(Bn, DI, L)
            x1 = jnp.transpose(xc, (0, 1, 3, 2)).reshape(Bn, DI, L)
            xs = jnp.stack([x0, x1, x0[..., ::-1], x1[..., ::-1]], axis=1)
            x_dbl = jnp.einsum('bkdl,kcd->bkcl', xs, x_proj_w)
            dts, Bs, Cs = jnp.split(x_dbl, [R, R + N], axis=2)
            dts = jnp.einsum('bkrl,kdr->bkdl', dts, dt_w)
            delta = jax.nn.softplus(dts + dt_b[None, :, :, None])
            A = -jnp.exp(A_log).reshape(K, DI, N)

            def step(h, t):
                x_t, d_t, B_t, C_t = t
                h = jnp.exp(d_t[..., None] * A) * h + (d_t * x_t)[..., None] * B_t[:, :, None, :]
                return (h, jnp.einsum('bkdn,bkn->bkd', h, C_t))
            scan_in = (jnp.moveaxis(xs, -1, 0), jnp.moveaxis(delta, -1, 0), jnp.moveaxis(Bs, -1, 0), jnp.moveaxis(Cs, -1, 0))
            h0 = jnp.zeros((Bn, K, DI, N), input.dtype)
            _, ys_l = jax.lax.scan(step, h0, scan_in)
            ys = jnp.moveaxis(ys_l, 0, -1) + Ds.reshape(K, DI)[None, :, :, None] * xs
            ym = ys[:, :2] + ys[:, 2:, :, ::-1]
            y = ym[:, 0] + jnp.transpose(ym[:, 1].reshape(Bn, DI, Ww, Hh), (0, 1, 3, 2)).reshape(Bn, DI, L)
            y = _ln(jnp.transpose(y, (0, 2, 1)), onorm_w, onorm_b).reshape(Bn, Hh, Ww, DI)
            y = y * _silu(z)
            x = input + y @ out_proj_w
            h2 = _ln(x, ln2_w, ln2_b)
            h2 = jax.nn.gelu(h2 @ fc1_w + fc1_b, approximate=False) @ fc2_w + fc2_b
            return x + h2
        return _forward(input, ln1_w, ln1_b, in_proj_w, conv_w, conv_b, x_proj_w, dt_w, dt_b, A_log, Ds, onorm_w, onorm_b, out_proj_w, ln2_w, ln2_b, fc1_w, fc1_b, fc2_w, fc2_b)

    def _L1_conv_ref(x, norm1_w, norm1_b, in_proj_w, conv_w, conv_b, x_proj_w, dt_projs_w, dt_projs_b, A_logs, Ds, out_norm_w, out_norm_b, out_proj_w, norm2_w, norm2_b, fc1_w, fc1_b, fc2_w, fc2_b):
        import jax, jax.numpy as jnp
        import numpy as np

        def _ln(x, w, b, eps=1e-05):
            mu = jnp.mean(x, axis=-1, keepdims=True)
            var = jnp.var(x, axis=-1, keepdims=True)
            return (x - mu) * jax.lax.rsqrt(var + eps) * w + b

        def _vss_forward(x, norm1_w, norm1_b, in_proj_w, conv_w, conv_b, x_proj_w, dt_projs_w, dt_projs_b, A_logs, Ds, out_norm_w, out_norm_b, out_proj_w, norm2_w, norm2_b, fc1_w, fc1_b, fc2_w, fc2_b):
            B, H, W, C = x.shape
            Di = in_proj_w.shape[0] // 2
            K = x_proj_w.shape[0]
            R = dt_projs_w.shape[2]
            N = A_logs.shape[1]
            L = H * W
            xn = _ln(x, norm1_w, norm1_b)
            xz = jnp.einsum('bhwc,ec->bhwe', xn, in_proj_w)
            xx, z = jnp.split(xz, 2, axis=-1)
            xb = xx.transpose(0, 3, 1, 2)
            xb = jax.lax.conv_general_dilated(xb, conv_w, window_strides=(1, 1), padding=((1, 1), (1, 1)), dimension_numbers=('NCHW', 'OIHW', 'NCHW'), feature_group_count=Di)
            xb = jax.nn.silu(xb + conv_b[None, :, None, None])
            x0 = xb.reshape(B, Di, L)
            x1 = xb.transpose(0, 1, 3, 2).reshape(B, Di, L)
            xs = jnp.stack([x0, x1, x0[..., ::-1], x1[..., ::-1]], axis=1)
            x_dbl = jnp.einsum('bkdl,kcd->bkcl', xs, x_proj_w)
            dts, Bsm, Csm = jnp.split(x_dbl, [R, R + N], axis=2)
            dt = jnp.einsum('bkrl,kdr->bkdl', dts, dt_projs_w)
            dt = jax.nn.softplus(dt + dt_projs_b[None, :, :, None])
            A = -jnp.exp(A_logs).reshape(K, Di, N)

            def step(h, t):
                dt_t, u_t, B_t, C_t = t
                h = h * jnp.exp(dt_t[..., None] * A) + (dt_t * u_t)[..., None] * B_t[:, :, None, :]
                y = jnp.einsum('bkdn,bkn->bkd', h, C_t)
                return (h, y)
            ts = (dt.transpose(3, 0, 1, 2), xs.transpose(3, 0, 1, 2), Bsm.transpose(3, 0, 1, 2), Csm.transpose(3, 0, 1, 2))
            h0 = jnp.zeros((B, K, Di, N), dtype=x.dtype)
            _, ys = jax.lax.scan(step, h0, ts)
            ys = ys.transpose(1, 2, 3, 0)
            ys = ys + Ds.reshape(K, Di)[None, :, :, None] * xs
            y = ys[:, 0] + ys[:, 2, :, ::-1]
            yw = ys[:, 1] + ys[:, 3, :, ::-1]
            y = y + yw.reshape(B, Di, W, H).transpose(0, 1, 3, 2).reshape(B, Di, L)
            y = y.transpose(0, 2, 1).reshape(B, H, W, Di)
            y = _ln(y, out_norm_w, out_norm_b)
            y = y * jax.nn.silu(z)
            y = jnp.einsum('bhwd,cd->bhwc', y, out_proj_w)
            x = x + y
            xm = _ln(x, norm2_w, norm2_b)
            h = jax.nn.gelu(jnp.einsum('bhwc,fc->bhwf', xm, fc1_w) + fc1_b)
            x = x + jnp.einsum('bhwf,cf->bhwc', h, fc2_w) + fc2_b
            return x
        return _vss_forward(x, norm1_w, norm1_b, in_proj_w, conv_w, conv_b, x_proj_w, dt_projs_w, dt_projs_b, A_logs, Ds, out_norm_w, out_norm_b, out_proj_w, norm2_w, norm2_b, fc1_w, fc1_b, fc2_w, fc2_b)

    def _L2_conv_ref(x, ln1_scale, ln1_bias, w1, b1, wdw, bdw, wse, bse, w2, b2, ln2_scale, ln2_bias, wf1, bf1, wf2, bf2, beta, gamma):
        import jax, jax.numpy as jnp
        import numpy as np
        C = 128
        DW = 2 * C
        FF = 2 * C
        EPS = 1e-06

        def _layernorm(x, scale, bias):
            mu = jnp.mean(x, axis=-1, keepdims=True)
            var = jnp.mean(jnp.square(x - mu), axis=-1, keepdims=True)
            return (x - mu) * jax.lax.rsqrt(var + EPS) * scale + bias
        s = _layernorm(x, ln1_scale, ln1_bias)
        s = jnp.einsum('bhwc,cd->bhwd', s, w1) + b1
        s = s * wdw + bdw
        g1, g2 = jnp.split(s, 2, axis=-1)
        s = g1 * g2
        gap = jnp.mean(s, axis=(1, 2), keepdims=True)
        att = jnp.einsum('bijc,cd->bijd', gap, wse) + bse
        s = s * att
        s = jnp.einsum('bhwc,cd->bhwd', s, w2) + b2
        x = x + beta * s
        c = _layernorm(x, ln2_scale, ln2_bias)
        c = jnp.einsum('bhwc,cd->bhwd', c, wf1) + bf1
        c1, c2 = jnp.split(c, 2, axis=-1)
        c = c1 * c2
        c = jnp.einsum('bhwc,cd->bhwd', c, wf2) + bf2
        return x + gamma * c

    def _L3_conv_ref(x, norm1_w, norm1_b, in_proj_w, conv_w, conv_b, x_proj_w, dt_projs_w, dt_projs_b, A_logs, Ds, out_norm_w, out_norm_b, out_proj_w, norm2_w, norm2_b, fc1_w, fc1_b, fc2_w, fc2_b):
        import jax, jax.numpy as jnp
        import numpy as np

        def _ln(x, w, b, eps=1e-05):
            mu = jnp.mean(x, axis=-1, keepdims=True)
            var = jnp.var(x, axis=-1, keepdims=True)
            return (x - mu) * jax.lax.rsqrt(var + eps) * w + b

        def _vss_forward(x, norm1_w, norm1_b, in_proj_w, conv_w, conv_b, x_proj_w, dt_projs_w, dt_projs_b, A_logs, Ds, out_norm_w, out_norm_b, out_proj_w, norm2_w, norm2_b, fc1_w, fc1_b, fc2_w, fc2_b):
            B, H, W, C = x.shape
            Di = in_proj_w.shape[0] // 2
            K = x_proj_w.shape[0]
            R = dt_projs_w.shape[2]
            N = A_logs.shape[1]
            L = H * W
            xn = _ln(x, norm1_w, norm1_b)
            xz = jnp.einsum('bhwc,ec->bhwe', xn, in_proj_w)
            xx, z = jnp.split(xz, 2, axis=-1)
            xb = xx.transpose(0, 3, 1, 2)
            xb = jax.lax.conv_general_dilated(xb, conv_w, window_strides=(1, 1), padding=((1, 1), (1, 1)), dimension_numbers=('NCHW', 'OIHW', 'NCHW'), feature_group_count=Di)
            xb = jax.nn.silu(xb + conv_b[None, :, None, None])
            x0 = xb.reshape(B, Di, L)
            x1 = xb.transpose(0, 1, 3, 2).reshape(B, Di, L)
            xs = jnp.stack([x0, x1, x0[..., ::-1], x1[..., ::-1]], axis=1)
            x_dbl = jnp.einsum('bkdl,kcd->bkcl', xs, x_proj_w)
            dts, Bsm, Csm = jnp.split(x_dbl, [R, R + N], axis=2)
            dt = jnp.einsum('bkrl,kdr->bkdl', dts, dt_projs_w)
            dt = jax.nn.softplus(dt + dt_projs_b[None, :, :, None])
            A = -jnp.exp(A_logs).reshape(K, Di, N)

            def step(h, t):
                dt_t, u_t, B_t, C_t = t
                h = h * jnp.exp(dt_t[..., None] * A) + (dt_t * u_t)[..., None] * B_t[:, :, None, :]
                y = jnp.einsum('bkdn,bkn->bkd', h, C_t)
                return (h, y)
            ts = (dt.transpose(3, 0, 1, 2), xs.transpose(3, 0, 1, 2), Bsm.transpose(3, 0, 1, 2), Csm.transpose(3, 0, 1, 2))
            h0 = jnp.zeros((B, K, Di, N), dtype=x.dtype)
            _, ys = jax.lax.scan(step, h0, ts)
            ys = ys.transpose(1, 2, 3, 0)
            ys = ys + Ds.reshape(K, Di)[None, :, :, None] * xs
            y = ys[:, 0] + ys[:, 2, :, ::-1]
            yw = ys[:, 1] + ys[:, 3, :, ::-1]
            y = y + yw.reshape(B, Di, W, H).transpose(0, 1, 3, 2).reshape(B, Di, L)
            y = y.transpose(0, 2, 1).reshape(B, H, W, Di)
            y = _ln(y, out_norm_w, out_norm_b)
            y = y * jax.nn.silu(z)
            y = jnp.einsum('bhwd,cd->bhwc', y, out_proj_w)
            x = x + y
            xm = _ln(x, norm2_w, norm2_b)
            h = jax.nn.gelu(jnp.einsum('bhwc,fc->bhwf', xm, fc1_w) + fc1_b)
            x = x + jnp.einsum('bhwf,cf->bhwc', h, fc2_w) + fc2_b
            return x
        return _vss_forward(x, norm1_w, norm1_b, in_proj_w, conv_w, conv_b, x_proj_w, dt_projs_w, dt_projs_b, A_logs, Ds, out_norm_w, out_norm_b, out_proj_w, norm2_w, norm2_b, fc1_w, fc1_b, fc2_w, fc2_b)

    def _gn(v, G=32, eps=1e-5):
        B_, H_, W_, C_ = v.shape
        g = v.reshape(B_, H_, W_, G, C_ // G)
        m = jnp.mean(g, axis=(1, 2, 4), keepdims=True)
        s = jnp.var(g, axis=(1, 2, 4), keepdims=True)
        return ((g - m) / jnp.sqrt(s + eps)).reshape(v.shape)

    def _ln_c(v, eps=1e-6):
        m = jnp.mean(v, axis=-1, keepdims=True)
        s = jnp.var(v, axis=-1, keepdims=True)
        return (v - m) / jnp.sqrt(s + eps)

    def _ln_t(v, eps=1e-5):
        m = jnp.mean(v, axis=-1, keepdims=True)
        s = jnp.var(v, axis=-1, keepdims=True)
        return (v - m) / jnp.sqrt(s + eps)

    def _to_tokens(v):
        B_, H_, W_, C_ = v.shape
        return v.reshape(B_, H_ * W_, C_)
    def _from_tokens(t, like):
        return t.reshape(like.shape)

    x = _L0_conv_ref(x, L0_conv_ln1_w, L0_conv_ln1_b, L0_conv_in_proj_w, L0_conv_conv_w, L0_conv_conv_b, L0_conv_x_proj_w, L0_conv_dt_w, L0_conv_dt_b, L0_conv_A_log, L0_conv_Ds, L0_conv_onorm_w, L0_conv_onorm_b, L0_conv_out_proj_w, L0_conv_ln2_w, L0_conv_ln2_b, L0_conv_fc1_w, L0_conv_fc1_b, L0_conv_fc2_w, L0_conv_fc2_b)
    x = _L1_conv_ref(x, L1_conv_norm1_w, L1_conv_norm1_b, L1_conv_in_proj_w, L1_conv_conv_w, L1_conv_conv_b, L1_conv_x_proj_w, L1_conv_dt_projs_w, L1_conv_dt_projs_b, L1_conv_A_logs, L1_conv_Ds, L1_conv_out_norm_w, L1_conv_out_norm_b, L1_conv_out_proj_w, L1_conv_norm2_w, L1_conv_norm2_b, L1_conv_fc1_w, L1_conv_fc1_b, L1_conv_fc2_w, L1_conv_fc2_b)
    x = _L2_conv_ref(x, L2_conv_ln1_scale, L2_conv_ln1_bias, L2_conv_w1, L2_conv_b1, L2_conv_wdw, L2_conv_bdw, L2_conv_wse, L2_conv_bse, L2_conv_w2, L2_conv_b2, L2_conv_ln2_scale, L2_conv_ln2_bias, L2_conv_wf1, L2_conv_bf1, L2_conv_wf2, L2_conv_bf2, L2_conv_beta, L2_conv_gamma)
    x = _L3_conv_ref(x, L3_conv_norm1_w, L3_conv_norm1_b, L3_conv_in_proj_w, L3_conv_conv_w, L3_conv_conv_b, L3_conv_x_proj_w, L3_conv_dt_projs_w, L3_conv_dt_projs_b, L3_conv_A_logs, L3_conv_Ds, L3_conv_out_norm_w, L3_conv_out_norm_b, L3_conv_out_proj_w, L3_conv_norm2_w, L3_conv_norm2_b, L3_conv_fc1_w, L3_conv_fc1_b, L3_conv_fc2_w, L3_conv_fc2_b)
    return x


_drawn_inputs = setup_inputs


def setup_inputs(seed=0):
    import zlib

    import numpy as np

    out = dict(_drawn_inputs(seed))
    spreads = {'L0_conv_ln1_w': (1.0, 0.6),
     'L0_conv_ln1_b': (0.0, 0.8),
     'L0_conv_conv_b': (0.0, 0.1),
     'L0_conv_Ds': (1.0, 0.6),
     'L0_conv_onorm_w': (1.0, 0.6),
     'L0_conv_onorm_b': (0.0, 0.8),
     'L0_conv_ln2_w': (1.0, 0.6),
     'L0_conv_ln2_b': (0.0, 0.8),
     'L0_conv_fc1_b': (0.0, 0.331),
     'L0_conv_fc2_b': (0.0, 0.1),
     'L1_conv_norm1_w': (1.0, 0.6),
     'L1_conv_norm1_b': (0.0, 0.8),
     'L1_conv_conv_b': (0.0, 0.1),
     'L1_conv_Ds': (1.0, 0.6),
     'L1_conv_out_norm_w': (1.0, 0.6),
     'L1_conv_out_norm_b': (0.0, 0.8),
     'L1_conv_norm2_w': (1.0, 0.6),
     'L1_conv_norm2_b': (0.0, 0.8),
     'L1_conv_fc1_b': (0.0, 0.346),
     'L1_conv_fc2_b': (0.0, 0.1),
     'L2_conv_ln1_scale': (1.0, 0.6),
     'L2_conv_ln1_bias': (0.0, 0.8),
     'L2_conv_ln2_scale': (1.0, 0.6),
     'L2_conv_ln2_bias': (0.0, 0.8),
     'L3_conv_norm1_w': (1.0, 0.6),
     'L3_conv_norm1_b': (0.0, 0.8),
     'L3_conv_conv_b': (0.0, 0.1),
     'L3_conv_Ds': (1.0, 0.6),
     'L3_conv_out_norm_w': (1.0, 0.6),
     'L3_conv_out_norm_b': (0.0, 0.8),
     'L3_conv_norm2_w': (1.0, 0.6),
     'L3_conv_norm2_b': (0.0, 0.8),
     'L3_conv_fc1_b': (0.0, 0.38),
     'L3_conv_fc2_b': (0.0, 0.1)}
    factors = {'L0_conv_x_proj_w': 8.0,
     'L0_conv_dt_w': 8.0,
     'L0_conv_dt_b': 8.0,
     'L0_conv_A_log': 8.0,
     'L1_conv_x_proj_w': 8.0,
     'L1_conv_dt_projs_w': 8.0,
     'L1_conv_dt_projs_b': 8.0,
     'L1_conv_A_logs': 8.0,
     'L2_conv_w1': 8.0,
     'L2_conv_b1': 8.0,
     'L2_conv_wdw': 8.0,
     'L2_conv_bdw': 8.0,
     'L2_conv_wse': 8.0,
     'L2_conv_bse': 8.0,
     'L2_conv_w2': 8.0,
     'L2_conv_b2': 8.0,
     'L2_conv_wf1': 6.019,
     'L2_conv_bf1': 8.0,
     'L2_conv_wf2': 5.868,
     'L2_conv_bf2': 8.0,
     'L2_conv_beta': 8.0,
     'L2_conv_gamma': 5.791,
     'L3_conv_x_proj_w': 8.0,
     'L3_conv_dt_projs_w': 8.0,
     'L3_conv_dt_projs_b': 8.0,
     'L3_conv_A_logs': 8.0}
    for name, (base, spread) in spreads.items():
        noise = np.random.default_rng([zlib.crc32(name.encode()), seed]).standard_normal(out[name].shape)
        drawn = base * np.exp(spread * noise) if base else spread * noise
        out[name] = jnp.asarray(drawn.astype(out[name].dtype))
    for name, factor in factors.items():
        out[name] = (out[name] * factor).astype(out[name].dtype)
    return out
```

```python
from contextlib import ExitStack

import numpy as np
import concourse.bass as bass
from concourse import mybir

F32 = mybir.dt.float32
BF16 = mybir.dt.bfloat16
ALU = mybir.AluOpType
ACT = mybir.ActivationFunctionType
AX_X = mybir.AxisListType.X

P = 128
NB, HW, C = 4, 64, 128
L = HW * HW
DH = 2
N, R, K = 16, 8, 4
CH = 512
NCH = L // CH
ROWS = CH // HW
PW = HW + 2
FF = 4
DIRS = (0, 2, 1, 3)
STEPS = N * NCH * K
CHUNKS = NCH * K
DT0 = 32

V_COLS = {}
_at = 0
for _name, _n in (("in_proj", 4 * C), ("conv_w", DH * 9), ("x_proj", K * DH * P), ("dt_w", K * DH * P),
                  ("A_log", K * DH * N), ("Ds", K * DH), ("onorm_w", DH), ("onorm_b", DH), ("out_proj", DH * C),
                  ("ln1_w", 1), ("ln1_b", 1), ("ln2_w", 1), ("ln2_b", 1), ("fc1", FF * C), ("fc1_b", FF),
                  ("fc2", FF * C), ("fc2_b", 1), ("conv_b", DH)):
    V_COLS[_name] = (_at, _at + _n)
    _at += _n
VW = _at
G_COLS = {}
_at = 0
for _name, _n in (("w1", 2 * C), ("wse", C), ("w2", C), ("wf1", 2 * C), ("wf2", C), ("b1", 2), ("wdw", 2), ("bdw", 2),
                  ("bse", 1), ("b2", 1), ("bf1", 2), ("bf2", 1), ("beta", 1), ("gamma", 1),
                  ("ln1_w", 1), ("ln1_b", 1), ("ln2_w", 1), ("ln2_b", 1)):
    G_COLS[_name] = (_at, _at + _n)
    _at += _n
GW = _at
K_ID, K_128, K_256, K_EPS5, K_EPS6, K_ROW = 0, P, 2 * P, 3 * P, 3 * P + 1, 3 * P + 2
KW = 3 * P + 3


def program(nc, x_in, consts, sel_in, w0, w1, wg, w3, out):
    ctx = ExitStack()
    with ctx:
        def sb(name, shape, dt=F32):
            return ctx.enter_context(nc.sbuf_tensor(name, shape, dt))

        def sem(name):
            return ctx.enter_context(nc.semaphore(name))

        layers = [("scan", w0, ACT.Gelu), ("scan", w1, ACT.Gelu_apprx_tanh), ("gated", wg, None),
                  ("scan", w3, ACT.Gelu_apprx_tanh)]
        hidden = [nc.dram_tensor(f"hidden{i}", [NB, P, L], F32).ap() for i in range(3)]
        gates = nc.dram_tensor("gates", [P, DH, L], F32).ap()
        sources = [x_in, *hidden]
        targets = [*hidden, out]

        X0 = sb("X0", [P, DH, L])
        X1 = sb("X1", [P, DH, L])
        YP = sb("YP", [P, DH * PW * PW])
        W = sb("W", [P, VW])
        KC = sb("KC", [P, KW])
        SEL = sb("SEL", [P, 2 * N, P], BF16)
        DIAG = sb("DIAG", [P, 9, P])
        ANEG = sb("ANEG", [P, K * DH * N])
        DTOT = sb("DTOT", [P, DH])
        SMALL = sb("SMALL", [P, 16])
        WK = sb("WK", [P, 13 * 2 * CH])
        HC = sb("HC", [P, 2, DH, CH])
        CS = sb("CS", [P, 2, CH])
        PARTS = sb("PARTS", [P, 2, CH], BF16)
        REST = sb("REST", [P, CH])
        DTS = sb("DTS", [P, CH])
        CARRY = sb("CARRY", [P, N, DH])
        ZERO = sb("ZERO", [P, DH])
        PS = ctx.enter_context(nc.psum_tensor("PS", [P, 8, CH], F32))

        def work(i):
            return WK[:, 2 * CH * i:2 * CH * (i + 1)].rearrange("p (h l) -> p h l", h=DH)

        DELTA = [work(0), work(1)]
        DX = [work(2), work(3)]
        EXPV, LOGV, RELU = work(4), work(5), work(6)
        DBX = [work(7), work(8)]
        HS = [work(9), work(10), work(11), work(12)]
        ROUND = HC[:, 0]
        ROUND = sb("ROUND", [P, DH, CH])
        PAD = YP[:, :].rearrange("p (h r c) -> p h r c", h=DH, r=PW)
        Y = YP[:, 0:DH * L].rearrange("p (h l) -> p h l", h=DH)
        YT = YP[:, 0:DH * L].rearrange("p (h r c) -> p h c r", h=DH, r=HW)
        SQ8 = WK[:, 0:NCH * 2 * CH].rearrange("p (t h l) -> p t h l", t=NCH, h=DH)
        SQ4 = WK[:, 0:L].rearrange("p (t l) -> p t l", t=NCH)
        RSTD = WK[:, 2 * L:3 * L].rearrange("p (t l) -> p t l", t=NCH)
        GL = WK[:, 0:2 * FF * CH].rearrange("p (s f l) -> p s f l", s=2, f=FF)
        OT = WK[:, 4 * CH * FF:4 * CH * FF + 2 * CH].rearrange("p (s l) -> p s l", s=2)
        SZT = [work(0), work(1)]
        XI, XN = X1[:, 0, :], X1[:, 1, :]
        YB, DAB, BB, CB, PB = PS[:, 0:2], PS[:, 2:4], PS[:, 4:6], PS[:, 6], PS[:, 7]

        ident, ones128, ones256 = KC[:, K_ID:K_ID + P], KC[:, K_128:K_128 + P], KC[:, K_256:K_256 + P]

        def col(i):
            return KC[:, i:i + 1]

        def wv(name, a=0, n=None):
            lo, hi = V_COLS[name]
            return W[:, lo + a:hi if n is None else lo + a + n]

        def wg_(name, a=0, n=None):
            lo, hi = G_COLS[name]
            return W[:, lo + a:hi if n is None else lo + a + n]

        def tok(t):
            return slice(t * CH, (t + 1) * CH)

        def both(ap):
            return ap.rearrange("p (o l) -> p o l", o=1).to_broadcast([P, DH, CH])

        s = {name: sem(name) for name in (
            "consts_loaded", "weights_loaded", "x_loaded", "gates_loaded", "residual_loaded",
            "gate_stored0", "gate_stored1", "out_stored0", "out_stored1",
            "derived", "carry_cleared", "a_exp",
            "ln_mean", "ln_cent", "ln_sq", "ln_var", "ln_log", "ln_rstd", "ln_norm", "ln_out",
            "border_zero", "xx_ready", "z_ready", "gate_ready", "padded", "conv0_ready", "x_half0", "taps_done",
            "x_half1", "turned",
            "proj_ready", "hi_ready", "dts_ready", "rest_ready", "mid_ready", "parts_ready", "v_ready", "v_used",
            "abs_done", "e_ready", "ln_ready", "round_ready", "err_ready", "log1p_ready", "delta_ready", "dx_ready",
            "b_ready", "c_ready", "decay_ready", "c_copied", "input_ready", "state_ready", "carry_ready",
            "readout_ready", "ysum_done", "y_merged",
            "on_mean", "on_cent", "on_sq", "on_var", "on_log", "on_rstd", "on_norm", "on_aff", "gated", "oproj",
            "res_done", "fc1_done", "gelu_done", "fc2_done", "out_ready",
            "g_small", "g_w1", "g_branch", "g_mult", "g_gap", "g_att_ps", "g_att", "g_w2s", "g_w2", "g_scaled",
            "g_res", "g_wf1", "g_c1", "g_c", "g_wf2", "g_o")}

        class Image:

            def __init__(self, layer, b):
                self.layer, self.b = layer, b
                self.scan_layer = {0: 0, 1: 1, 3: 2}.get(layer, 0)

            def all(self, per):
                return self.b * per + self.layer * NB * per

            def scan(self, per):
                return self.b * per + self.scan_layer * NB * per

            def own(self, per):
                return self.b * per

        class Chunk:

            def __init__(self, img, ki, j):
                self.k = DIRS[ki]
                self.o, self.back = self.k % 2, self.k // 2
                self.pos = j * -1 + (NCH - 1) if self.back else j
                self.i = img.scan(CHUNKS) + ki * NCH + j
                self.step = img.scan(STEPS) + (ki * NCH + j) * N
                self.X = X1 if self.o else X0

            def tokens(self):
                if isinstance(self.pos, int):
                    return slice(self.pos * CH, (self.pos + 1) * CH)
                return bass.ds(self.pos * CH, CH)

            def last(self):
                return 0 if self.back else CH - 1

            def run(self, ap):
                return ap[:, ::-1] if self.back else ap

            def out(self):
                if not self.o:
                    return Y[:, :, self.tokens()], YB
                cols = (slice(self.pos * ROWS, (self.pos + 1) * ROWS) if isinstance(self.pos, int)
                        else bass.ds(self.pos * ROWS, ROWS))
                return YT[:, :, cols, :], YB.rearrange("p h (c r) -> p h c r", r=HW)

        def scans(engine, img, body):
            for ki in range(K):
                before = Chunk(img, ki - 1, NCH - 1) if ki else None
                after = Chunk(img, ki + 1, 0) if ki + 1 < K else None
                body(Chunk(img, ki, 0), before, Chunk(img, ki, 1), 0)
                with engine.Fori(0, NCH // 2 - 1) as j:
                    for u in (1, 2):
                        body(Chunk(img, ki, 2 * j + u), Chunk(img, ki, 2 * j + (u - 1)),
                             Chunk(img, ki, 2 * j + (u + 1)), u % 2)
                body(Chunk(img, ki, NCH - 1), Chunk(img, ki, NCH - 2), after, 1)

        block = ctx.enter_context(nc.Block())

        @block.sync
        def _(sp):
            sp.dma_start(KC[:, :], consts).then_inc(s["consts_loaded"], 16)
            sp.dma_start(SEL[:, :, :], sel_in).then_inc(s["consts_loaded"], 16)
            for layer, (kind, weights, _) in enumerate(layers):
                if layer:
                    for q in range(2):
                        sp.wait_ge(s[f"out_stored{q}"], 16 * layer * NB * NCH // 2)
                sp.dma_start(W[:, 0:VW if kind == "scan" else GW], weights).then_inc(s["weights_loaded"], 16)
                src, dst = sources[layer], targets[layer]
                with sp.Fori(0, NB) as b:
                    img = Image(layer, b)
                    sp.dma_start(XI, src[bass.ds(b, 1)].rearrange("o p l -> p (o l)")).then_inc(s["x_loaded"], 16)
                    if kind == "scan":
                        for t in range(NCH):
                            sp.wait_ge(s["gate_ready"], img.scan(NCH) + (t + 1))
                            sp.dma_start(gates[:, :, tok(t)], SZT[t % 2]).then_inc(s[f"gate_stored{t % 2}"], 16)
                        for q in range(2):
                            sp.wait_ge(s[f"gate_stored{q}"], (img.scan(NCH // 2) + NCH // 2) * 16)
                        sp.wait_ge(s["y_merged"], img.scan(CHUNKS) + 2 * NCH)
                        sp.dma_start(X0[:, :, :], gates).then_inc(s["gates_loaded"], 16)
                        sp.wait_ge(s["y_merged"], img.scan(CHUNKS) + CHUNKS)
                        sp.dma_start(XI, src[bass.ds(b, 1)].rearrange("o p l -> p (o l)")).then_inc(s["residual_loaded"], 16)
                    for t in range(NCH):
                        sp.wait_ge(s["out_ready"], img.all(NCH) + (t + 1))
                        sp.dma_start(dst[bass.ds(b, 1), :, tok(t)].rearrange("o p l -> p (o l)"),
                                     OT[:, t % 2]).then_inc(s[f"out_stored{t % 2}"], 16)
            for q in range(2):
                sp.wait_ge(s[f"out_stored{q}"], 16 * len(layers) * NB * NCH // 2)

        @block.tensor
        def _(pe):
            def layernorm(img, which, ready, per, count):
                base = img.all(2 * NCH) + which * NCH
                for t in range(NCH):
                    pe.wait_ge(s[ready], per + count(t))
                    pe.matmul(PS[:, t], ones128, XI[:, tok(t)], start=True, stop=True).then_inc(s["ln_mean"], 1)
                for t in range(NCH):
                    pe.wait_ge(s["ln_sq"], base + (t + 1))
                    pe.matmul(PS[:, t], ones128, SQ4[:, t], start=True, stop=True).then_inc(s["ln_var"], 1)

            def project(nxt):
                for h in range(DH):
                    mm = pe.matmul(PB, wv("x_proj", (nxt.k * DH + h) * P, P), nxt.X[:, h, nxt.tokens()],
                                   start=(h == 0), stop=(h == 1))
                mm.then_inc(s["proj_ready"], 1)

            def step_size(nxt, h):
                pe.matmul(PB, wv("dt_w", (nxt.k * DH + h) * P, P)[DT0:DT0 + R + 1], DTS[DT0:DT0 + R + 1],
                          start=True, stop=True).then_inc(s["v_ready"], 1)

            def spread(bank, row, parity):
                return pe.matmul(bank, SEL[:, row], PARTS[:, parity], start=True, stop=True)

            def sum_states(n, half_bank, slot):
                for h in range(DH):
                    mm = pe.matmul(half_bank[:, h], ident, HC[:, slot, h], start=(n == 0), stop=(n == N - 1))
                mm.then_inc(s["ysum_done"], 1)

            def chunk(c, prev, nxt, par):
                for n in range(N):
                    st = c.step + n
                    if n + 2 < N or nxt:
                        pe.wait_ge(s["input_ready"], st + 1)
                        if n + 2 == N:
                            pe.wait_ge(s["parts_ready"], c.i + 2)
                        m = (n + 2) % N
                        spread(BB[:, n % 2], m, par if n + 2 < N else 1 - par).then_inc(s["b_ready"], 1)
                    if n + 1 < N or nxt:
                        pe.wait_ge(s["c_copied"], st + 1)
                        m = (n + 1) % N
                        spread(CB, N + m, par if n + 1 < N else 1 - par).then_inc(s["c_ready"], 1)
                    if n >= 2 or prev:
                        pe.wait_ge(s["readout_ready"], st - 1)
                        if n == 2 and prev:
                            pe.wait_ge(s["y_merged"], c.i)
                        sum_states((n - 2) % N, YB, n % 2)
                    if nxt:
                        if n == 2:
                            if nxt.o and not c.o:
                                pe.wait_ge(s["turned"], DH * (c.i // CHUNKS) + DH if isinstance(c.i, int) else turned)
                            pe.wait_ge(s["v_used"], c.i * DH + DH)
                            project(nxt)
                        if n == 6:
                            pe.wait_ge(s["rest_ready"], c.i + 2)
                            pe.wait_ge(s["dts_ready"], c.i + 2)
                            step_size(nxt, 0)
                        if n == 8:
                            pe.wait_ge(s["v_used"], c.i * DH + (DH + 1))
                            step_size(nxt, 1)

            pe.wait_ge(s["consts_loaded"], 32)
            for layer, (kind, _, _) in enumerate(layers):
                pe.wait_ge(s["weights_loaded"], 16 * (layer + 1))
                with pe.Fori(0, NB) as b:
                    img = Image(layer, b)
                    layernorm(img, 0, "x_loaded", img.all(16) + 16, lambda t: 0)
                    ln0 = img.all(2 * NCH)
                    if kind == "scan":
                        a = img.scan(NCH)
                        for t in range(NCH):
                            pe.wait_ge(s["ln_out"], ln0 + (t + 1))
                            if t < 2:
                                pe.wait_ge(s["ln_log"], ln0 + 4 * (t + 1))
                            else:
                                pe.wait_ge(s["padded"], a + (t - 1))
                                pe.wait_ge(s["gate_ready"], a + (t - 1))
                            for e in range(4):
                                mm = pe.matmul(PS[:, 4 * (t % 2) + e], wv("in_proj", e * C, C), XN[:, tok(t)],
                                               start=True, stop=True)
                                if e == 1:
                                    mm.then_inc(s["xx_ready"], 1)
                            mm.then_inc(s["z_ready"], 1)
                        pe.wait_ge(s["padded"], a + NCH)
                        pe.wait_ge(s["gate_ready"], a + NCH)
                        pe.wait_ge(s["border_zero"], img.scan(1) + 1)
                        pe.wait_ge(s["derived"], img.scan_layer + 1)
                        for t in range(NCH):
                            for tap in range(9):
                                dy, dx = divmod(tap, 3)
                                mm = pe.matmul(PS[:, t], DIAG[:, tap],
                                               PAD[:, 0, ROWS * t + dy:ROWS * (t + 1) + dy, dx:dx + HW],
                                               start=(tap == 0), stop=(tap == 8))
                            mm.then_inc(s["conv0_ready"], 1)
                        first = Chunk(img, 0, 0)
                        turned = img.scan(DH) + DH
                        pe.wait_ge(s["x_half0"], a + NCH)
                        pe.wait_ge(s["x_half1"], img.scan(2) + 2)
                        project(first)
                        pe.wait_ge(s["rest_ready"], first.i + 1)
                        pe.wait_ge(s["dts_ready"], first.i + 1)
                        step_size(first, 0)
                        pe.wait_ge(s["v_used"], first.i * DH + 1)
                        step_size(first, 1)
                        pe.wait_ge(s["parts_ready"], first.i + 1)
                        spread(BB[:, 0], 0, 0).then_inc(s["b_ready"], 1)
                        spread(BB[:, 1], 1, 0).then_inc(s["b_ready"], 1)
                        spread(CB, N, 0).then_inc(s["c_ready"], 1)
                        scans(pe, img, chunk)
                        end = img.scan(STEPS) + STEPS
                        for n in (N - 2, N - 1):
                            pe.wait_ge(s["readout_ready"], end - (N - 1 - n))
                            sum_states(n, YB, n % 2)
                        pe.wait_ge(s["y_merged"], img.scan(CHUNKS) + CHUNKS)
                        for t in range(NCH):
                            for h in range(DH):
                                mm = pe.matmul(PS[:, t], ones256, Y[:, h, tok(t)], start=(h == 0), stop=(h == 1))
                            mm.then_inc(s["on_mean"], 1)
                        for t in range(NCH):
                            pe.wait_ge(s["on_sq"], a + (t + 1))
                            for h in range(DH):
                                mm = pe.matmul(PS[:, t], ones256, SQ8[:, t, h], start=(h == 0), stop=(h == 1))
                            mm.then_inc(s["on_var"], 1)
                        for t in range(NCH):
                            pe.wait_ge(s["gated"], a + (t + 1))
                            for h in range(DH):
                                mm = pe.matmul(PS[:, t], wv("out_proj", h * C, C), Y[:, h, tok(t)],
                                               start=(h == 0), stop=(h == 1))
                            mm.then_inc(s["oproj"], 1)
                        layernorm(img, 1, "res_done", a, lambda t: t + 1)
                        ln1 = img.all(2 * NCH) + NCH
                        pe.wait_ge(s["ln_log"], ln1 + NCH)

                        def fc2(t):
                            pe.wait_ge(s["gelu_done"], img.scan(2 * NCH) + (2 * t + 2))
                            if t >= 2:
                                pe.wait_ge(s["out_ready"], img.all(NCH) + (t - 1))
                            for f in range(FF):
                                mm = pe.matmul(PS[:, 6 + t % 2], wv("fc2", f * C, C), GL[:, t % 2, f],
                                               start=(f == 0), stop=(f == FF - 1))
                            mm.then_inc(s["fc2_done"], 1)

                        for t in range(NCH):
                            pe.wait_ge(s["ln_out"], ln1 + (t + 1))
                            for p in range(2):
                                q = 2 * t + p
                                if q >= 3:
                                    pe.wait_ge(s["gelu_done"], img.scan(2 * NCH) + (q - 2))
                                for i in range(2):
                                    mm = pe.matmul(PS[:, 2 * (q % 3) + i], wv("fc1", (2 * p + i) * C, C), XN[:, tok(t)],
                                                   start=True, stop=True)
                                mm.then_inc(s["fc1_done"], 1)
                            if t:
                                fc2(t - 1)
                        fc2(NCH - 1)
                    else:
                        g = img.own(NCH)
                        for t in range(NCH):
                            pe.wait_ge(s["ln_out"], ln0 + (t + 1))
                            if t < 4:
                                pe.wait_ge(s["ln_log"], ln0 + 2 * (t + 1))
                            else:
                                pe.wait_ge(s["g_branch"], img.own(2 * NCH) + 2 * (t - 3))
                            for e in range(2):
                                mm = pe.matmul(PS[:, 2 * (t % 4) + e], wg_("w1", e * C, C), XN[:, tok(t)],
                                               start=True, stop=True)
                            mm.then_inc(s["g_w1"], 1)
                        pe.wait_ge(s["g_gap"], img.own(1) + 1)
                        pe.matmul(PS[:, 0, 0:1], wg_("wse"), SMALL[:, 8:9], start=True, stop=True).then_inc(s["g_att_ps"], 1)
                        pe.wait_ge(s["g_w2s"], img.own(1) + 1)
                        for t in range(NCH):
                            pe.matmul(PS[:, t], DIAG[:, 0], X0[:, 0, tok(t)], start=True, stop=True).then_inc(s["g_w2"], 1)
                        layernorm(img, 1, "g_res", g, lambda t: t + 1)
                        ln1 = img.all(2 * NCH) + NCH
                        pe.wait_ge(s["ln_log"], ln1 + NCH)

                        def wf2(t):
                            pe.wait_ge(s["g_c"], g + (t + 1))
                            if t >= 2:
                                pe.wait_ge(s["g_o"], g + (t - 1))
                            pe.matmul(PS[:, 6 + t % 2], wg_("wf2"), GL[:, t % 2, 1], start=True, stop=True).then_inc(s["g_wf2"], 1)

                        for t in range(NCH):
                            pe.wait_ge(s["ln_out"], ln1 + (t + 1))
                            if t >= 3:
                                pe.wait_ge(s["g_c"], g + (t - 2))
                            for e in range(2):
                                mm = pe.matmul(PS[:, 2 * (t % 3) + e], wg_("wf1", e * C, C), XN[:, tok(t)],
                                               start=True, stop=True)
                            mm.then_inc(s["g_wf1"], 1)
                            if t:
                                wf2(t - 1)
                        wf2(NCH - 1)

        @block.vector
        def _(dve):
            def layernorm(img, which, w, bias):
                base = img.all(2 * NCH) + which * NCH
                for t in range(NCH):
                    dve.wait_ge(s["ln_mean"], base + (t + 1))
                    dve.tensor_tensor(XN[:, tok(t)], XI[:, tok(t)], PS[:, t], ALU.subtract).then_inc(s["ln_cent"], 1)
                for t in range(NCH):
                    dve.wait_ge(s["ln_rstd"], base + (t + 1))
                    dve.tensor_tensor(XN[:, tok(t)], XN[:, tok(t)], RSTD[:, t], ALU.mult).then_inc(s["ln_norm"], 1)
                    dve.wait_ge(s["ln_norm"], base + (t + 1))
                    dve.tensor_scalar(XN[:, tok(t)], XN[:, tok(t)], w, bias, ALU.mult, ALU.add).then_inc(s["ln_out"], 1)

            def leave_rest(i):
                dve.wait_ge(s["hi_ready"], i + 1)
                dve.tensor_tensor(REST[64:128], PB[64:128], PARTS[64:128, rest_par[0]], ALU.subtract)\
                   .then_inc(s["rest_ready"], 1)

            rest_par = [0]

            def split_rest(i, par):
                rest_par[0] = par
                leave_rest(i)

            def split_low(i, par):
                dve.wait_ge(s["mid_ready"], i + 1)
                dve.tensor_tensor(PARTS[96:128, par], REST[96:128], PARTS[96:128, par], ALU.subtract)\
                   .then_inc(s["parts_ready"], 1)

            def round_one(i):
                dve.wait_ge(s["e_ready"], i + 1)
                dve.tensor_scalar(ROUND[:, :, :], EXPV, 1.0, -1.0, ALU.add, ALU.add).then_inc(s["round_ready"], 1)

            def delta(i, par):
                dve.wait_ge(s["log1p_ready"], i + 1)
                dve.tensor_tensor(DELTA[par], LOGV, RELU, ALU.add).then_inc(s["delta_ready"], 1)

            def delta_x(nxt, par):
                dve.wait_ge(s["delta_ready"], nxt.i + 1)
                dve.tensor_tensor(DX[par], DELTA[par], nxt.X[:, :, nxt.tokens()], ALU.mult).then_inc(s["dx_ready"], 1)

            def scan_input(st, slot, par):
                dve.wait_ge(s["b_ready"], st + 1)
                dve.tensor_tensor(DBX[slot], DX[par], both(BB[:, slot]), ALU.mult).then_inc(s["input_ready"], 1)

            def merge(c, first):
                dve.wait_ge(s["ysum_done"], c.step + N)
                to, sums = c.out()
                if first:
                    for h in range(DH):
                        ins = dve.scalar_tensor_tensor(to[:, h], c.X[:, h, c.tokens()], DTOT[:, h:h + 1], sums[:, h],
                                                       ALU.mult, ALU.add)
                else:
                    for h in range(DH):
                        ins = dve.tensor_tensor(to[:, h], to[:, h], sums[:, h], ALU.add)
                ins.then_inc(s["y_merged"], 1)

            def chunk(c, prev, nxt, par):
                for n in range(N):
                    st = c.step + n
                    if n + 1 < N or nxt:
                        if n + 1 == N:
                            dve.wait_ge(s["dx_ready"], nxt.i + 1)
                        if prev or n >= 1:
                            dve.wait_ge(s["state_ready"], st * DH)
                        scan_input(st + 1, (n + 1) % 2, par if n + 1 < N else 1 - par)
                    dve.wait_ge(s["input_ready"], st + 1)
                    if prev or n >= 4:
                        dve.wait_ge(s["carry_ready"], st - 3)
                        dve.wait_ge(s["readout_ready"], st - 3)
                    for h in range(DH):
                        dve.wait_ge(s["decay_ready"], st * DH + (h + 1))
                        dve.tensor_tensor_scan(c.run(HS[n % 4][:, h]), c.run(DAB[:, h]), c.run(DBX[n % 2][:, h]),
                                               CARRY[:, n, h:h + 1], ALU.mult, ALU.add).then_inc(s["state_ready"], 1)
                    if n == 1 and prev:
                        merge(prev, prev.k == DIRS[0])
                    if nxt:
                        if n == 4:
                            split_rest(nxt.i, 1 - par)
                        if n == 6:
                            split_low(nxt.i, 1 - par)
                        if n == 11:
                            round_one(nxt.i)
                        if n == 13:
                            delta(nxt.i, 1 - par)
                        if n == 14:
                            delta_x(nxt, 1 - par)

            dve.memset(ZERO[:, :], 0.0).then_inc(s["carry_cleared"], 1)
            dve.memset(CARRY[:, :, :], 0.0).then_inc(s["carry_cleared"], 1)
            dve.wait_ge(s["consts_loaded"], 32)
            for layer, (kind, _, _) in enumerate(layers):
                dve.wait_ge(s["weights_loaded"], 16 * (layer + 1))
                lay = Image(layer, 0)
                if kind == "scan":
                    for tap in range(9):
                        dve.tensor_scalar(DIAG[:, tap], ident, wv("conv_w", tap, 1), None, ALU.mult)
                    dve.tensor_reduce(DTOT[:, :], wv("Ds").rearrange("p (k h) -> p h k", h=DH), AX_X, ALU.add)\
                       .then_inc(s["derived"], 1)
                    dve.wait_ge(s["a_exp"], lay.scan_layer + 1)
                    dve.tensor_scalar(ANEG[:, :], ANEG[:, :], -1.0, None, ALU.mult).then_inc(s["derived"], 0 + 1)
                else:
                    dve.tensor_tensor(SMALL[:, 0:2], wg_("b1"), wg_("wdw"), ALU.mult).then_inc(s["g_small"], 1)
                    dve.wait_ge(s["g_small"], 1)
                    dve.tensor_tensor(SMALL[:, 0:2], SMALL[:, 0:2], wg_("bdw"), ALU.add)
                    dve.tensor_tensor(SMALL[:, 2:3], wg_("beta"), wg_("b2"), ALU.mult)
                    dve.tensor_tensor(SMALL[:, 3:4], wg_("gamma"), wg_("bf2"), ALU.mult).then_inc(s["g_small"], 1)
                with dve.Fori(0, NB) as b:
                    img = Image(layer, b)
                    layernorm_w = wv if kind == "scan" else wg_
                    if kind == "scan":
                        dve.wait_ge(s["x_loaded"], img.all(16) + 16)
                        dve.memset(PAD[:, :, 0:PW:PW - 1, :], 0.0)
                        dve.memset(PAD[:, :, 1:PW - 1, 0:PW:PW - 1], 0.0).then_inc(s["border_zero"], 1)
                    layernorm(img, 0, layernorm_w("ln1_w"), layernorm_w("ln1_b"))
                    if kind == "scan":
                        a = img.scan(NCH)
                        for t in range(NCH):
                            dve.wait_ge(s["xx_ready"], a + (t + 1))
                            dve.tensor_copy(PAD[:, :, 1 + ROWS * t:1 + ROWS * (t + 1), 1:1 + HW],
                                            PS[:, 4 * (t % 2):4 * (t % 2) + 2].rearrange("p h (r c) -> p h r c", c=HW))\
                               .then_inc(s["padded"], 1)
                        conv = X0[:, 1].rearrange("p (r c) -> p r c", c=HW)
                        dve.wait_ge(s["padded"], a + NCH)
                        dve.wait_ge(s["border_zero"], img.scan(1) + 1)
                        for tap in range(9):
                            dy, dx = divmod(tap, 3)
                            window = PAD[:, 1, dy:dy + HW, dx:dx + HW]
                            w = wv("conv_w", 9 + tap, 1)
                            if tap:
                                dve.wait_ge(s["taps_done"], img.scan(9) + tap)
                                ins = dve.scalar_tensor_tensor(conv, window, w, conv, ALU.mult, ALU.add)
                            else:
                                ins = dve.tensor_scalar(conv, window, w, None, ALU.mult)
                            ins.then_inc(s["taps_done"], 1)
                        first = Chunk(img, 0, 0)
                        split_rest(first.i, 0)
                        split_low(first.i, 0)
                        dve.wait_ge(s["x_half0"], a + NCH)
                        dve.wait_ge(s["x_half1"], img.scan(2) + 2)
                        for h in range(DH):
                            dve.tensor_copy(X1[:, h].rearrange("p (c r) -> p c r", r=HW),
                                            X0[:, h].rearrange("p (r c) -> p c r", c=HW)).then_inc(s["turned"], 1)
                        round_one(first.i)
                        delta(first.i, 0)
                        delta_x(first, 0)
                        dve.wait_ge(s["dx_ready"], first.i + 1)
                        scan_input(first.step, 0, 0)
                        scans(dve, img, chunk)
                        merge(Chunk(img, K - 1, NCH - 1), False)
                        dve.wait_ge(s["y_merged"], img.scan(CHUNKS) + CHUNKS)
                        for t in range(NCH):
                            dve.wait_ge(s["on_mean"], a + (t + 1))
                            dve.tensor_tensor(Y[:, :, tok(t)], Y[:, :, tok(t)], both(PS[:, t]), ALU.subtract)\
                               .then_inc(s["on_cent"], 1)
                        for t in range(NCH):
                            dve.wait_ge(s["on_rstd"], a + (t + 1))
                            dve.tensor_tensor(Y[:, :, tok(t)], Y[:, :, tok(t)], both(RSTD[:, t]), ALU.mult)\
                               .then_inc(s["on_norm"], 1)
                        dve.wait_ge(s["residual_loaded"], img.scan(16) + 16)
                        for t in range(NCH):
                            dve.wait_ge(s["oproj"], a + (t + 1))
                            dve.tensor_tensor(XI[:, tok(t)], XI[:, tok(t)], PS[:, t], ALU.add).then_inc(s["res_done"], 1)
                        layernorm(img, 1, wv("ln2_w"), wv("ln2_b"))
                        for t in range(NCH):
                            dve.wait_ge(s["fc2_done"], a + (t + 1))
                            if t >= 2:
                                dve.wait_ge(s[f"out_stored{t % 2}"], (img.all(NCH // 2) + t // 2) * 16)
                            dve.scalar_tensor_tensor(OT[:, t % 2], PS[:, 6 + t % 2], wv("fc2_b"), XI[:, tok(t)],
                                                     ALU.add, ALU.add).then_inc(s["out_ready"], 1)
                    else:
                        g = img.own(NCH)
                        for t in range(NCH):
                            dve.wait_ge(s["g_branch"], img.own(2 * NCH) + (2 * t + 2))
                            dve.tensor_tensor(X0[:, 0, tok(t)], X0[:, 0, tok(t)], X0[:, 1, tok(t)], ALU.mult)\
                               .then_inc(s["g_mult"], 1)
                        dve.wait_ge(s["g_mult"], g + NCH)
                        dve.tensor_reduce(SMALL[:, 8:9], X0[:, 0], AX_X, ALU.add).then_inc(s["g_gap"], 1)
                        dve.wait_ge(s["g_att"], img.own(1) + 1)
                        dve.tensor_scalar(DIAG[:, 0], wg_("w2"), SMALL[:, 9:10], None, ALU.mult).then_inc(s["g_w2s"], 1)
                        for t in range(NCH):
                            dve.wait_ge(s["g_scaled"], g + (t + 1))
                            dve.tensor_tensor(XI[:, tok(t)], XI[:, tok(t)], X0[:, 1, tok(t)], ALU.add).then_inc(s["g_res"], 1)
                        layernorm(img, 1, wg_("ln2_w"), wg_("ln2_b"))

                        def result(t):
                            dve.wait_ge(s["g_o"], g + (t + 1))
                            if t >= 2:
                                dve.wait_ge(s[f"out_stored{t % 2}"], (img.all(NCH // 2) + t // 2) * 16)
                            dve.tensor_tensor(OT[:, t % 2], GL[:, t % 2, 2], XI[:, tok(t)], ALU.add).then_inc(s["out_ready"], 1)

                        for t in range(NCH):
                            dve.wait_ge(s["g_c1"], g + (t + 1))
                            if t >= 2:
                                dve.wait_ge(s["g_wf2"], g + (t - 1))
                            dve.scalar_tensor_tensor(GL[:, t % 2, 1], PS[:, 2 * (t % 3) + 1], wg_("bf1", 1, 1), GL[:, t % 2, 0],
                                                     ALU.add, ALU.mult).then_inc(s["g_c"], 1)
                            if t:
                                result(t - 1)
                        result(NCH - 1)

        @block.scalar
        def _(act):
            def layernorm(img, which, eps):
                base = img.all(2 * NCH) + which * NCH
                for t in range(NCH):
                    act.wait_ge(s["ln_cent"], base + (t + 1))
                    act.activation(SQ4[:, t], XN[:, tok(t)], ACT.Square).then_inc(s["ln_sq"], 1)
                for t in range(NCH):
                    act.wait_ge(s["ln_var"], base + (t + 1))
                    act.activation(RSTD[:, t], PS[:, t], ACT.Ln, bias=col(eps)).then_inc(s["ln_log"], 1)
                    act.wait_ge(s["ln_log"], base + (t + 1))
                    act.activation(RSTD[:, t], RSTD[:, t], ACT.Exp, scale=-0.5).then_inc(s["ln_rstd"], 1)

            def lead(i, par):
                act.wait_ge(s["proj_ready"], i + 1)
                act.activation(PARTS[:, par], PB, ACT.Copy).then_inc(s["hi_ready"], 1)
                act.activation(DTS[DT0:DT0 + 32], PB[DT0:DT0 + 32], ACT.Identity, bias=col(K_ROW)[DT0:DT0 + 32])\
                   .then_inc(s["dts_ready"], 1)

            def middle(i, par):
                act.wait_ge(s["rest_ready"], i + 1)
                act.activation(PARTS[64:128, par], REST[64:128], ACT.Copy).then_inc(s["mid_ready"], 1)

            def take_v(i, h, first=False):
                act.wait_ge(s["v_ready"], i * DH + (h + 1))
                if h == 0 and not first:
                    act.wait_ge(s["log1p_ready"], i)
                act.activation(EXPV[:, h], PB, ACT.Abs).then_inc(s["abs_done"], 1)
                act.activation(RELU[:, h], PB, ACT.Relu).then_inc(s["v_used"], 1)

            def exp_v(i):
                act.wait_ge(s["abs_done"], i * DH + DH)
                act.activation(EXPV, EXPV, ACT.Exp, scale=-1.0).then_inc(s["e_ready"], 1)

            def log_v(i):
                act.wait_ge(s["e_ready"], i + 1)
                act.activation(LOGV, EXPV, ACT.Ln, bias=1.0).then_inc(s["ln_ready"], 1)

            def save(c, n, last_chunk):
                source = ZERO[:, :] if last_chunk else HS[n % 4][:, :, c.last()]
                act.activation(CARRY[:, n], source, ACT.Copy).then_inc(s["carry_ready"], 1)

            def chunk(c, prev, nxt, par):
                final = nxt is None or nxt.k != c.k
                for n in range(N):
                    st = c.step + n
                    if n == 0:
                        act.wait_ge(s["delta_ready"], c.i + 1)
                    for h in range(DH):
                        if prev or n:
                            act.wait_ge(s["state_ready"], st * DH + (h - 1))
                        a = (c.k * DH + h) * N + n
                        act.activation(DAB[:, h], DELTA[par][:, h], ACT.Exp, scale=ANEG[:, a:a + 1])\
                           .then_inc(s["decay_ready"], 1)
                    act.wait_ge(s["c_ready"], st + 1)
                    if prev or n >= 2:
                        act.wait_ge(s["readout_ready"], st - 1)
                    act.activation(CS[:, n % 2], CB, ACT.Copy).then_inc(s["c_copied"], 1)
                    if n:
                        save(c, n - 1, final)
                    elif prev:
                        save(prev, N - 1, prev.k != c.k)
                    if nxt:
                        if n == 3:
                            lead(nxt.i, 1 - par)
                        if n == 5:
                            middle(nxt.i, 1 - par)
                        if n == 7:
                            take_v(nxt.i, 0)
                        if n == 9:
                            take_v(nxt.i, 1)
                            exp_v(nxt.i)
                        if n == 10:
                            log_v(nxt.i)

            act.wait_ge(s["consts_loaded"], 32)
            act.wait_ge(s["carry_cleared"], 2)
            for layer, (kind, _, gelu) in enumerate(layers):
                act.wait_ge(s["weights_loaded"], 16 * (layer + 1))
                lay = Image(layer, 0)
                if kind == "scan":
                    act.activation(ANEG[:, :], wv("A_log"), ACT.Exp).then_inc(s["a_exp"], 1)
                else:
                    act.wait_ge(s["g_small"], 2)
                with act.Fori(0, NB) as b:
                    img = Image(layer, b)
                    layernorm(img, 0, K_EPS5 if kind == "scan" else K_EPS6)
                    if kind == "scan":
                        a = img.scan(NCH)
                        for t in range(NCH):
                            act.wait_ge(s["z_ready"], a + (t + 1))
                            if t >= 2:
                                act.wait_ge(s[f"gate_stored{t % 2}"], (img.scan(NCH // 2) + t // 2) * 16)
                            act.activation(SZT[t % 2], PS[:, 4 * (t % 2) + 2:4 * (t % 2) + 4], ACT.Silu)\
                               .then_inc(s["gate_ready"], 1)
                        for t in range(NCH):
                            act.wait_ge(s["conv0_ready"], a + (t + 1))
                            act.activation(X0[:, 0, tok(t)], PS[:, t], ACT.Silu, bias=wv("conv_b", 0, 1))\
                               .then_inc(s["x_half0"], 1)
                            if t == NCH - 3:
                                act.wait_ge(s["taps_done"], img.scan(9) + 9)
                                for i in range(2):
                                    part = X0[:, 1, i * L // 2:(i + 1) * L // 2]
                                    act.activation(part, part, ACT.Silu, bias=wv("conv_b", 1, 1)).then_inc(s["x_half1"], 1)
                        first = Chunk(img, 0, 0)
                        for q in range(2):
                            act.wait_ge(s[f"gate_stored{q}"], (img.scan(NCH // 2) + NCH // 2) * 16)
                        lead(first.i, 0)
                        middle(first.i, 0)
                        take_v(first.i, 0, True)
                        take_v(first.i, 1, True)
                        exp_v(first.i)
                        log_v(first.i)
                        act.wait_ge(s["derived"], img.scan_layer * 2 + 2)
                        scans(act, img, chunk)
                        end = img.scan(STEPS) + STEPS
                        act.wait_ge(s["state_ready"], end * DH)
                        save(Chunk(img, K - 1, NCH - 1), N - 1, True)
                        for t in range(NCH):
                            act.wait_ge(s["on_cent"], a + (t + 1))
                            act.activation(SQ8[:, t], Y[:, :, tok(t)], ACT.Square).then_inc(s["on_sq"], 1)
                        for t in range(NCH):
                            act.wait_ge(s["on_var"], a + (t + 1))
                            act.activation(RSTD[:, t], PS[:, t], ACT.Ln, bias=col(K_EPS5)).then_inc(s["on_log"], 1)
                            act.wait_ge(s["on_log"], a + (t + 1))
                            act.activation(RSTD[:, t], RSTD[:, t], ACT.Exp, scale=-0.5).then_inc(s["on_rstd"], 1)
                        for t in range(NCH):
                            act.wait_ge(s["on_norm"], a + (t + 1))
                            for h in range(DH):
                                ins = act.activation(Y[:, h, tok(t)], Y[:, h, tok(t)], ACT.Identity,
                                                     bias=wv("onorm_b", h, 1), scale=wv("onorm_w", h, 1))
                            ins.then_inc(s["on_aff"], 1)
                        layernorm(img, 1, K_EPS5)
                        for t in range(NCH):
                            if t >= 2:
                                act.wait_ge(s["fc2_done"], a + (t - 1))
                            for p in range(2):
                                act.wait_ge(s["fc1_done"], img.scan(2 * NCH) + (2 * t + p + 1))
                                for i in range(2):
                                    f = 2 * p + i
                                    ins = act.activation(GL[:, t % 2, f], PS[:, 2 * ((2 * t + p) % 3) + i], gelu,
                                                         bias=wv("fc1_b", f, 1))
                                ins.then_inc(s["gelu_done"], 1)
                    else:
                        g = img.own(NCH)
                        for t in range(NCH):
                            act.wait_ge(s["g_w1"], g + (t + 1))
                            for e in range(2):
                                act.activation(X0[:, e, tok(t)], PS[:, 2 * (t % 4) + e], ACT.Identity,
                                               bias=SMALL[:, e:e + 1], scale=wg_("wdw", e, 1)).then_inc(s["g_branch"], 1)
                        act.wait_ge(s["g_att_ps"], img.own(1) + 1)
                        act.activation(SMALL[:, 9:10], PS[:, 0, 0:1], ACT.Identity, bias=wg_("bse"), scale=1.0 / L)\
                           .then_inc(s["g_att"], 1)
                        for t in range(NCH):
                            act.wait_ge(s["g_w2"], g + (t + 1))
                            act.activation(X0[:, 1, tok(t)], PS[:, t], ACT.Identity, bias=SMALL[:, 2:3], scale=wg_("beta"))\
                               .then_inc(s["g_scaled"], 1)
                        layernorm(img, 1, K_EPS6)

                        def scaled(t):
                            act.wait_ge(s["g_wf2"], g + (t + 1))
                            if t >= 2:
                                act.wait_ge(s["out_ready"], img.all(NCH) + (t - 1))
                            act.activation(GL[:, t % 2, 2], PS[:, 6 + t % 2], ACT.Identity, bias=SMALL[:, 3:4], scale=wg_("gamma"))\
                               .then_inc(s["g_o"], 1)

                        for t in range(NCH):
                            act.wait_ge(s["g_wf1"], g + (t + 1))
                            if t >= 2:
                                act.wait_ge(s["g_c"], g + (t - 1))
                            act.activation(GL[:, t % 2, 0], PS[:, 2 * (t % 3)], ACT.Identity, bias=wg_("bf1", 0, 1))\
                               .then_inc(s["g_c1"], 1)
                            if t:
                                scaled(t - 1)
                        scaled(NCH - 1)

        @block.gpsimd
        def _(pool):
            def log1p(i):
                pool.wait_ge(s["round_ready"], i + 1)
                pool.tensor_tensor(ROUND[:, :, :], EXPV, ROUND[:, :, :], ALU.subtract).then_inc(s["err_ready"], 1)
                pool.wait_ge(s["ln_ready"], i + 1)
                pool.wait_ge(s["err_ready"], i + 1)
                pool.tensor_tensor(LOGV, LOGV, ROUND[:, :, :], ALU.add).then_inc(s["log1p_ready"], 1)

            def chunk(c, prev, nxt, par):
                for n in range(N):
                    st = c.step + n
                    pool.wait_ge(s["c_copied"], st + 1)
                    if prev or n >= 2:
                        pool.wait_ge(s["ysum_done"], st - 1)
                    pool.wait_ge(s["state_ready"], st * DH + DH)
                    pool.tensor_tensor(HC[:, n % 2], HS[n % 4], both(CS[:, n % 2]), ALU.mult).then_inc(s["readout_ready"], 1)
                    if nxt and n == 11:
                        log1p(nxt.i)

            for layer, (kind, _, _) in enumerate(layers):
                if kind != "scan":
                    continue
                with pool.Fori(0, NB) as b:
                    img = Image(layer, b)
                    a = img.scan(NCH)
                    log1p(Chunk(img, 0, 0).i)
                    scans(pool, img, chunk)
                    pool.wait_ge(s["gates_loaded"], img.scan(16) + 16)
                    for t in range(NCH):
                        pool.wait_ge(s["on_aff"], a + (t + 1))
                        pool.tensor_tensor(Y[:, :, tok(t)], Y[:, :, tok(t)], X0[:, :, tok(t)], ALU.mult).then_inc(s["gated"], 1)


_V_NAMES = {0: ("ln1_w", "ln1_b", "dt_w", "dt_b", "A_log", "onorm_w", "onorm_b", "ln2_w", "ln2_b"),
            1: ("norm1_w", "norm1_b", "dt_projs_w", "dt_projs_b", "A_logs", "out_norm_w", "out_norm_b", "norm2_w", "norm2_b")}


def _cols(v):
    return np.ascontiguousarray(v.reshape(-1, P).T)


def _scan_weights(inputs, layer):
    names = _V_NAMES[min(layer, 1)]
    ln1w, ln1b, dtw, dtb, alog, onw, onb, ln2w, ln2b = (inputs[f"L{layer}_conv_{n}"] for n in names)
    g = {n: inputs[f"L{layer}_conv_{n}"] for n in ("in_proj_w", "conv_w", "conv_b", "x_proj_w", "Ds", "out_proj_w",
                                                   "fc1_w", "fc1_b", "fc2_w", "fc2_b")}
    flip = (lambda a: a) if layer == 0 else (lambda a: a.T)
    xp = g["x_proj_w"].reshape(K, R + 2 * N, DH, P).transpose(3, 0, 2, 1)
    dt, bc = xp[..., :R], xp[..., R:]
    gap = np.zeros((P, K, DH, 2 * N - R), np.float32)
    x_proj = np.concatenate([bc, dt, gap, bc, bc], axis=-1).reshape(P, -1)
    step = np.zeros((P, K, DH * P), np.float32)
    step[DT0:DT0 + R] = dtw.transpose(2, 0, 1)
    step[DT0 + R] = dtb
    parts = dict(
        in_proj=flip(g["in_proj_w"]), conv_w=g["conv_w"].reshape(DH, P, 9).transpose(1, 0, 2).reshape(P, -1),
        x_proj=x_proj, dt_w=step.reshape(P, -1),
        A_log=alog.reshape(K, DH, P, N).transpose(2, 0, 1, 3).reshape(P, -1),
        Ds=g["Ds"].reshape(K, DH, P).transpose(2, 0, 1).reshape(P, -1),
        onorm_w=_cols(onw), onorm_b=_cols(onb),
        out_proj=flip(g["out_proj_w"]).reshape(DH, P, C).transpose(1, 0, 2).reshape(P, -1),
        ln1_w=_cols(ln1w), ln1_b=_cols(ln1b), ln2_w=_cols(ln2w), ln2_b=_cols(ln2b),
        fc1=flip(g["fc1_w"]), fc1_b=_cols(g["fc1_b"]),
        fc2=flip(g["fc2_w"]).reshape(FF, P, C).transpose(1, 0, 2).reshape(P, -1), fc2_b=_cols(g["fc2_b"]),
        conv_b=_cols(g["conv_b"]))
    return np.ascontiguousarray(np.concatenate([parts[n] for n in V_COLS], axis=1))


def _gated_weights(inputs):
    g = {n: inputs[f"L2_conv_{n}"] for n in ("w1", "wse", "w2", "wf1", "wf2", "b1", "wdw", "bdw", "bse", "b2", "bf1", "bf2",
                                             "beta", "gamma", "ln1_scale", "ln1_bias", "ln2_scale", "ln2_bias")}
    g.update(ln1_w=g["ln1_scale"], ln1_b=g["ln1_bias"], ln2_w=g["ln2_scale"], ln2_b=g["ln2_bias"])
    mats = ("w1", "wse", "w2", "wf1", "wf2")
    return np.ascontiguousarray(np.concatenate([g[n] if n in mats else _cols(g[n]) for n in G_COLS], axis=1))


def _constants():
    c = np.zeros((P, KW), np.float32)
    c[:, K_ID:K_ID + P] = np.eye(P)
    c[:, K_128:K_128 + P] = 1.0 / P
    c[:, K_256:K_256 + P] = 1.0 / (DH * P)
    c[:, K_EPS5], c[:, K_EPS6] = 1e-5, 1e-6
    c[DT0 + R, K_ROW] = 1.0
    sel = np.zeros((P, 2 * N, P), np.float32)
    for row in range(2 * N):
        for part in (0, 64, 96):
            sel[part + row, row, :] = 1.0
    return c, sel


def kernel(**inputs):
    import concourse.bacc as _bacc
    from concourse.bass_utils import run_bass_kernel_spmd as _run
    inputs = {n: np.asarray(a) for n, a in inputs.items()}
    consts, sel = _constants()
    x = np.ascontiguousarray(inputs["x"].reshape(NB, L, C).transpose(0, 2, 1))
    arrays = {"in_x": x, "consts": consts, "sel": sel.astype(mybir.dt.np(BF16)),
              "w0": _scan_weights(inputs, 0), "w1": _scan_weights(inputs, 1), "wg": _gated_weights(inputs),
              "w3": _scan_weights(inputs, 3)}
    nc = _bacc.Bacc("TRN2", target_bir_lowering=False, num_devices=1)
    args = [nc.dram_tensor(n, a.shape, mybir.dt.from_np(a.dtype), kind="ExternalInput").ap() for n, a in arrays.items()]
    args.append(nc.dram_tensor("out_0", (NB, C, L), F32, kind="ExternalOutput").ap())
    program(nc, *args)
    r = _run(nc, [arrays], core_ids=[0])
    return np.ascontiguousarray(r.results[0]["out_0"].transpose(0, 2, 1)).reshape(NB, HW, HW, C)
```

```python
from contextlib import ExitStack

import numpy as np
import concourse.bass as bass
from concourse import mybir

F32 = mybir.dt.float32
BF16 = mybir.dt.bfloat16
ALU = mybir.AluOpType
ACT = mybir.ActivationFunctionType
AX_X = mybir.AxisListType.X

P = 128
NB, HW, C = 4, 64, 128
L = HW * HW
DH = 2
N, R, K = 16, 8, 4
CH = 512
NCH = L // CH
ROWS = CH // HW
PW = HW + 2
FF = 4
DIRS = (0, 2, 1, 3)
STEPS = N * NCH * K
CHUNKS = NCH * K
RING = 4
LAG = 3
PE_SLOTS = {0: "project", 3: "step0", 5: "step1"}
ACT_SLOTS = {1: ("raw",), 2: ("hi",), 4: ("abs0", "relu0"), 5: ("exp0",), 6: ("abs1", "relu1"), 7: ("exp1",),
             8: ("log0",), 9: ("log1",), 10: ("mid",)}
DVE_SLOTS = {4: "rest", 8: "round", 12: "low", 13: "delta", 14: "input"}
POOL_SLOTS = {8: "error", 10: "log1p"}
MERGE = 2
LN_EXP = "natural_log_exp_and_others"
DT0 = 32

V_COLS = {}
_at = 0
for _name, _n in (("in_proj", 4 * C), ("conv_w", DH * 9), ("x_proj", K * DH * P), ("dt_w", K * DH * P),
                  ("A_log", K * DH * N), ("Ds", K * DH), ("onorm_w", DH), ("onorm_b", DH), ("out_proj", DH * C),
                  ("ln1_w", 1), ("ln1_b", 1), ("ln2_w", 1), ("ln2_b", 1), ("fc1", FF * C), ("fc1_b", FF),
                  ("fc2", FF * C), ("fc2_b", 1), ("conv_b", DH)):
    V_COLS[_name] = (_at, _at + _n)
    _at += _n
VW = _at
G_COLS = {}
_at = 0
for _name, _n in (("w1", 2 * C), ("wse", C), ("w2", C), ("wf1", 2 * C), ("wf2", C), ("b1", 2), ("wdw", 2), ("bdw", 2),
                  ("bse", 1), ("b2", 1), ("bf1", 2), ("bf2", 1), ("beta", 1), ("gamma", 1),
                  ("ln1_w", 1), ("ln1_b", 1), ("ln2_w", 1), ("ln2_b", 1)):
    G_COLS[_name] = (_at, _at + _n)
    _at += _n
GW = _at
K_ID, K_128, K_256, K_EPS5, K_EPS6, K_ROW = 0, P, 2 * P, 3 * P, 3 * P + 1, 3 * P + 2
KW = 3 * P + 3


def program(nc, x_in, consts, sel_in, w0, w1, wg, w3, out):
    ctx = ExitStack()
    with ctx:
        def sb(name, shape, dt=F32):
            return ctx.enter_context(nc.sbuf_tensor(name, shape, dt))

        def sem(name):
            return ctx.enter_context(nc.semaphore(name))

        layers = [("scan", w0, ACT.Gelu), ("scan", w1, ACT.Gelu_apprx_tanh), ("gated", wg, None),
                  ("scan", w3, ACT.Gelu_apprx_tanh)]
        hidden = [nc.dram_tensor(f"hidden{i}", [NB, P, L], F32).ap() for i in range(3)]
        gates = nc.dram_tensor("gates", [P, DH, L], F32).ap()
        sources = [x_in, *hidden]
        targets = [*hidden, out]

        X0 = sb("X0", [P, DH, L])
        X1 = sb("X1", [P, DH, L])
        YP = sb("YP", [P, DH * PW * PW])
        W = sb("W", [P, VW])
        KC = sb("KC", [P, KW])
        SEL = sb("SEL", [P, 2 * N, P], BF16)
        ANEG = sb("ANEG", [P, K * DH * N])
        DTOT = sb("DTOT", [P, DH])
        SMALL = sb("SMALL", [P, 16])
        WK = sb("WK", [P, 12 * 2 * CH])
        HC = sb("HC", [P, RING, DH, CH])
        CS = sb("CS", [P, RING, CH])
        DIAG = CS[:, :, :].rearrange("p s (t c) -> p (s t) c", c=P)
        PARTS = sb("PARTS", [P, 2, CH], BF16)
        RAW = sb("RAW", [P, CH])
        CARRY = sb("CARRY", [P, N, DH])
        ZERO = sb("ZERO", [P, DH])
        PS = ctx.enter_context(nc.psum_tensor("PS", [P, 8, CH], F32))

        def work(i):
            return WK[:, 2 * CH * i:2 * CH * (i + 1)].rearrange("p (h l) -> p h l", h=DH)

        DELTA = [work(0), work(1)]
        DX = [work(2), work(3)]
        EXPV, LOGV = work(4), work(5)
        DBX = [work(6), work(7)]
        HS = [work(8 + i) for i in range(RING)]
        ROUND = DX
        PAD = YP[:, :].rearrange("p (h r c) -> p h r c", h=DH, r=PW)
        Y = YP[:, 0:DH * L].rearrange("p (h l) -> p h l", h=DH)
        YT = YP[:, 0:DH * L].rearrange("p (h r c) -> p h c r", h=DH, r=HW)
        SQ8 = WK[:, 0:NCH * 2 * CH].rearrange("p (t h l) -> p t h l", t=NCH, h=DH)
        SQ4 = WK[:, 0:L].rearrange("p (t l) -> p t l", t=NCH)
        RSTD = WK[:, 2 * L:3 * L].rearrange("p (t l) -> p t l", t=NCH)
        GL = WK[:, 0:2 * FF * CH].rearrange("p (s f l) -> p s f l", s=2, f=FF)
        OT = WK[:, 4 * CH * FF:4 * CH * FF + 2 * CH].rearrange("p (s l) -> p s l", s=2)
        SZT = [work(0), work(1)]
        XI, XN = X1[:, 0, :], X1[:, 1, :]
        YB, DAB, BB, CB, PB = PS[:, 0:2], PS[:, 2:4], PS[:, 4:6], PS[:, 6], PS[:, 7]

        ident, ones128, ones256 = KC[:, K_ID:K_ID + P], KC[:, K_128:K_128 + P], KC[:, K_256:K_256 + P]

        def col(i):
            return KC[:, i:i + 1]

        def wv(name, a=0, n=None):
            lo, hi = V_COLS[name]
            return W[:, lo + a:hi if n is None else lo + a + n]

        def wg_(name, a=0, n=None):
            lo, hi = G_COLS[name]
            return W[:, lo + a:hi if n is None else lo + a + n]

        def tok(t):
            return slice(t * CH, (t + 1) * CH)

        def both(ap):
            return ap.rearrange("p (o l) -> p o l", o=1).to_broadcast([P, DH, CH])

        s = {name: sem(name) for name in (
            "consts_loaded", "weights_loaded", "x_loaded", "gates_loaded", "residual_loaded",
            "gate_stored0", "gate_stored1", "out_stored0", "out_stored1",
            "derived", "diagonals", "carry_cleared", "a_exp",
            "ln_mean", "ln_cent", "ln_sq", "ln_var", "ln_log", "ln_rstd", "ln_norm", "ln_out",
            "border_zero", "xx_ready", "z_ready", "gate_ready", "padded", "conv0_ready", "x_half0", "taps_done",
            "x_half1", "turned",
            "proj_ready", "raw_ready", "hi_ready", "rest_ready", "mid_ready", "parts_ready", "v_ready", "v_used",
            "abs_done", "e_ready", "ln_ready", "round_ready", "err_ready", "log1p_ready", "delta_ready", "dx_ready",
            "b_ready", "c_ready", "decay_ready", "c_copied", "input_ready", "state_ready", "carry_ready",
            "readout_ready", "ysum_done", "y_merged",
            "on_mean", "on_cent", "on_sq", "on_var", "on_log", "on_rstd", "on_norm", "on_aff", "gated", "oproj",
            "res_done", "fc1_done", "gelu_done", "fc2_done", "out_ready",
            "g_small", "g_w1", "g_branch", "g_mult", "g_gap", "g_att_ps", "g_att", "g_w2s", "g_w2", "g_scaled",
            "g_res", "g_wf1", "g_c1", "g_c", "g_wf2", "g_o")}

        class Image:

            def __init__(self, layer, b):
                self.layer, self.b = layer, b
                self.scan_layer = {0: 0, 1: 1, 3: 2}.get(layer, 0)

            def all(self, per):
                return self.b * per + self.layer * NB * per

            def scan(self, per):
                return self.b * per + self.scan_layer * NB * per

            def own(self, per):
                return self.b * per

        class Chunk:

            def __init__(self, img, ki, j):
                self.k = DIRS[ki]
                self.o, self.back = self.k % 2, self.k // 2
                self.pos = j * -1 + (NCH - 1) if self.back else j
                self.i = img.scan(CHUNKS) + ki * NCH + j
                self.step = img.scan(STEPS) + (ki * NCH + j) * N
                self.X = X1 if self.o else X0
                self.turned = img.scan(DH) + DH

            def tokens(self):
                if isinstance(self.pos, int):
                    return slice(self.pos * CH, (self.pos + 1) * CH)
                return bass.ds(self.pos * CH, CH)

            def last(self):
                return 0 if self.back else CH - 1

            def run(self, ap):
                return ap[:, ::-1] if self.back else ap

            def out(self):
                if not self.o:
                    return Y[:, :, self.tokens()], YB
                cols = (slice(self.pos * ROWS, (self.pos + 1) * ROWS) if isinstance(self.pos, int)
                        else bass.ds(self.pos * ROWS, ROWS))
                return YT[:, :, cols, :], YB.rearrange("p h (c r) -> p h c r", r=HW)

        def scans(engine, img, body):
            for ki in range(K):
                before = Chunk(img, ki - 1, NCH - 1) if ki else None
                after = Chunk(img, ki + 1, 0) if ki + 1 < K else None
                body(Chunk(img, ki, 0), before, Chunk(img, ki, 1), 0)
                with engine.Fori(0, NCH // 2 - 1) as j:
                    for u in (1, 2):
                        body(Chunk(img, ki, 2 * j + u), Chunk(img, ki, 2 * j + (u - 1)),
                             Chunk(img, ki, 2 * j + (u + 1)), u % 2)
                body(Chunk(img, ki, NCH - 1), Chunk(img, ki, NCH - 2), after, 1)

        block = ctx.enter_context(nc.Block())

        @block.sync
        def _(sp):
            sp.dma_start(KC[:, :], consts).then_inc(s["consts_loaded"], 16)
            sp.dma_start(SEL[:, :, :], sel_in).then_inc(s["consts_loaded"], 16)
            for layer, (kind, weights, _) in enumerate(layers):
                if layer:
                    for q in range(2):
                        sp.wait_ge(s[f"out_stored{q}"], 16 * layer * NB * NCH // 2)
                sp.dma_start(W[:, 0:VW if kind == "scan" else GW], weights).then_inc(s["weights_loaded"], 16)
                src, dst = sources[layer], targets[layer]
                with sp.Fori(0, NB) as b:
                    img = Image(layer, b)
                    sp.dma_start(XI, src[bass.ds(b, 1)].rearrange("o p l -> p (o l)")).then_inc(s["x_loaded"], 16)
                    if kind == "scan":
                        for t in range(NCH):
                            sp.wait_ge(s["gate_ready"], img.scan(NCH) + (t + 1))
                            sp.dma_start(gates[:, :, tok(t)], SZT[t % 2]).then_inc(s[f"gate_stored{t % 2}"], 16)
                        for q in range(2):
                            sp.wait_ge(s[f"gate_stored{q}"], (img.scan(NCH // 2) + NCH // 2) * 16)
                        sp.wait_ge(s["y_merged"], img.scan(CHUNKS) + 2 * NCH)
                        sp.dma_start(X0[:, :, :], gates).then_inc(s["gates_loaded"], 16)
                        sp.wait_ge(s["y_merged"], img.scan(CHUNKS) + CHUNKS)
                        sp.dma_start(XI, src[bass.ds(b, 1)].rearrange("o p l -> p (o l)")).then_inc(s["residual_loaded"], 16)
                    for t in range(NCH):
                        sp.wait_ge(s["out_ready"], img.all(NCH) + (t + 1))
                        sp.dma_start(dst[bass.ds(b, 1), :, tok(t)].rearrange("o p l -> p (o l)"),
                                     OT[:, t % 2]).then_inc(s[f"out_stored{t % 2}"], 16)
            for q in range(2):
                sp.wait_ge(s[f"out_stored{q}"], 16 * len(layers) * NB * NCH // 2)

        @block.tensor
        def _(pe):
            def layernorm(img, which, ready, per, count):
                base = img.all(2 * NCH) + which * NCH
                for t in range(NCH):
                    pe.wait_ge(s[ready], per + count(t))
                    pe.matmul(PS[:, t], ones128, XI[:, tok(t)], start=True, stop=True).then_inc(s["ln_mean"], 1)
                for t in range(NCH):
                    pe.wait_ge(s["ln_sq"], base + (t + 1))
                    pe.matmul(PS[:, t], ones128, SQ4[:, t], start=True, stop=True).then_inc(s["ln_var"], 1)

            def project(nxt):
                for h in range(DH):
                    mm = pe.matmul(PB, wv("x_proj", (nxt.k * DH + h) * P, P), nxt.X[:, h, nxt.tokens()],
                                   start=(h == 0), stop=(h == 1))
                mm.then_inc(s["proj_ready"], 1)

            def prepare(nxt, op):
                if op == "project":
                    project(nxt)
                if op == "step0":
                    pe.wait_ge(s["raw_ready"], nxt.i + 1)
                    step_size(nxt, 0)
                if op == "step1":
                    pe.wait_ge(s["v_used"], nxt.i * DH + 1)
                    step_size(nxt, 1)

            def step_size(nxt, h):
                pe.matmul(PB, wv("dt_w", (nxt.k * DH + h) * P, P)[DT0:DT0 + R + 1], RAW[DT0:DT0 + R + 1],
                          start=True, stop=True).then_inc(s["v_ready"], 1)

            def spread(bank, row, parity):
                return pe.matmul(bank, SEL[:, row], PARTS[:, parity], start=True, stop=True)

            def sum_states(n, half_bank, slot):
                for h in range(DH):
                    mm = pe.matmul(half_bank[:, h], ident, HC[:, slot, h], start=(n == 0), stop=(n == N - 1))
                mm.then_inc(s["ysum_done"], 1)

            def chunk(c, prev, nxt, par):
                for n in range(N):
                    st = c.step + n
                    if n + 2 < N or nxt:
                        pe.wait_ge(s["input_ready"], st + 1)
                        if n + 2 == N:
                            pe.wait_ge(s["parts_ready"], c.i + 2)
                        m = (n + 2) % N
                        spread(BB[:, n % 2], m, par if n + 2 < N else 1 - par).then_inc(s["b_ready"], 1)
                    if n + 1 < N or nxt:
                        pe.wait_ge(s["c_copied"], st + 1)
                        m = (n + 1) % N
                        spread(CB, N + m, par if n + 1 < N else 1 - par).then_inc(s["c_ready"], 1)
                    if n >= LAG or prev:
                        pe.wait_ge(s["readout_ready"], st - (LAG - 1))
                        if n == LAG and prev:
                            pe.wait_ge(s["y_merged"], c.i)
                        sum_states((n - LAG) % N, YB, (n - LAG) % RING)
                    if nxt and n in PE_SLOTS:
                        if PE_SLOTS[n] == "project":
                            if nxt.o and not c.o:
                                pe.wait_ge(s["turned"], c.turned)
                            pe.wait_ge(s["v_used"], c.i * DH + DH)
                        prepare(nxt, PE_SLOTS[n])

            pe.wait_ge(s["consts_loaded"], 32)
            for layer, (kind, _, _) in enumerate(layers):
                pe.wait_ge(s["weights_loaded"], 16 * (layer + 1))
                with pe.Fori(0, NB) as b:
                    img = Image(layer, b)
                    layernorm(img, 0, "x_loaded", img.all(16) + 16, lambda t: 0)
                    ln0 = img.all(2 * NCH)
                    if kind == "scan":
                        a = img.scan(NCH)
                        for t in range(NCH):
                            pe.wait_ge(s["ln_out"], ln0 + (t + 1))
                            if t < 2:
                                pe.wait_ge(s["ln_log"], ln0 + 4 * (t + 1))
                            else:
                                pe.wait_ge(s["padded"], a + (t - 1))
                                pe.wait_ge(s["gate_ready"], a + (t - 1))
                            for e in range(4):
                                mm = pe.matmul(PS[:, 4 * (t % 2) + e], wv("in_proj", e * C, C), XN[:, tok(t)],
                                               start=True, stop=True)
                                if e == 1:
                                    mm.then_inc(s["xx_ready"], 1)
                            mm.then_inc(s["z_ready"], 1)
                        pe.wait_ge(s["padded"], a + NCH)
                        pe.wait_ge(s["gate_ready"], a + NCH)
                        pe.wait_ge(s["border_zero"], img.scan(1) + 1)
                        pe.wait_ge(s["diagonals"], img.scan(1) + 1)
                        for t in range(NCH):
                            for tap in range(9):
                                dy, dx = divmod(tap, 3)
                                mm = pe.matmul(PS[:, t], DIAG[:, tap],
                                               PAD[:, 0, ROWS * t + dy:ROWS * (t + 1) + dy, dx:dx + HW],
                                               start=(tap == 0), stop=(tap == 8))
                            mm.then_inc(s["conv0_ready"], 1)
                        first = Chunk(img, 0, 0)
                        pe.wait_ge(s["x_half0"], a + NCH)
                        pe.wait_ge(s["x_half1"], img.scan(2) + 2)
                        for op in PE_SLOTS.values():
                            prepare(first, op)
                        pe.wait_ge(s["parts_ready"], first.i + 1)
                        spread(BB[:, 0], 0, 0).then_inc(s["b_ready"], 1)
                        spread(BB[:, 1], 1, 0).then_inc(s["b_ready"], 1)
                        spread(CB, N, 0).then_inc(s["c_ready"], 1)
                        scans(pe, img, chunk)
                        end = img.scan(STEPS) + STEPS
                        for n in range(N - LAG, N):
                            pe.wait_ge(s["readout_ready"], end - (N - 1 - n))
                            sum_states(n, YB, n % RING)
                        pe.wait_ge(s["y_merged"], img.scan(CHUNKS) + CHUNKS)
                        for t in range(NCH):
                            for h in range(DH):
                                mm = pe.matmul(PS[:, t], ones256, Y[:, h, tok(t)], start=(h == 0), stop=(h == 1))
                            mm.then_inc(s["on_mean"], 1)
                        for t in range(NCH):
                            pe.wait_ge(s["on_sq"], a + (t + 1))
                            for h in range(DH):
                                mm = pe.matmul(PS[:, t], ones256, SQ8[:, t, h], start=(h == 0), stop=(h == 1))
                            mm.then_inc(s["on_var"], 1)
                        for t in range(NCH):
                            pe.wait_ge(s["gated"], a + (t + 1))
                            for h in range(DH):
                                mm = pe.matmul(PS[:, t], wv("out_proj", h * C, C), Y[:, h, tok(t)],
                                               start=(h == 0), stop=(h == 1))
                            mm.then_inc(s["oproj"], 1)
                        layernorm(img, 1, "res_done", a, lambda t: t + 1)
                        ln1 = img.all(2 * NCH) + NCH
                        pe.wait_ge(s["ln_log"], ln1 + NCH)

                        def fc2(t):
                            pe.wait_ge(s["gelu_done"], img.scan(2 * NCH) + (2 * t + 2))
                            if t >= 2:
                                pe.wait_ge(s["out_ready"], img.all(NCH) + (t - 1))
                            for f in range(FF):
                                mm = pe.matmul(PS[:, 6 + t % 2], wv("fc2", f * C, C), GL[:, t % 2, f],
                                               start=(f == 0), stop=(f == FF - 1))
                            mm.then_inc(s["fc2_done"], 1)

                        for t in range(NCH):
                            pe.wait_ge(s["ln_out"], ln1 + (t + 1))
                            for p in range(2):
                                q = 2 * t + p
                                if q >= 3:
                                    pe.wait_ge(s["gelu_done"], img.scan(2 * NCH) + (q - 2))
                                for i in range(2):
                                    mm = pe.matmul(PS[:, 2 * (q % 3) + i], wv("fc1", (2 * p + i) * C, C), XN[:, tok(t)],
                                                   start=True, stop=True)
                                mm.then_inc(s["fc1_done"], 1)
                            if t:
                                fc2(t - 1)
                        fc2(NCH - 1)
                    else:
                        g = img.own(NCH)
                        for t in range(NCH):
                            pe.wait_ge(s["ln_out"], ln0 + (t + 1))
                            if t < 4:
                                pe.wait_ge(s["ln_log"], ln0 + 2 * (t + 1))
                            else:
                                pe.wait_ge(s["g_branch"], img.own(2 * NCH) + 2 * (t - 3))
                            for e in range(2):
                                mm = pe.matmul(PS[:, 2 * (t % 4) + e], wg_("w1", e * C, C), XN[:, tok(t)],
                                               start=True, stop=True)
                            mm.then_inc(s["g_w1"], 1)
                        pe.wait_ge(s["g_gap"], img.own(1) + 1)
                        pe.matmul(PS[:, 0, 0:1], wg_("wse"), SMALL[:, 8:9], start=True, stop=True).then_inc(s["g_att_ps"], 1)
                        pe.wait_ge(s["g_w2s"], img.own(1) + 1)
                        for t in range(NCH):
                            pe.matmul(PS[:, t], DIAG[:, 0], X0[:, 0, tok(t)], start=True, stop=True).then_inc(s["g_w2"], 1)
                        layernorm(img, 1, "g_res", g, lambda t: t + 1)
                        ln1 = img.all(2 * NCH) + NCH
                        pe.wait_ge(s["ln_log"], ln1 + NCH)

                        def wf2(t):
                            pe.wait_ge(s["g_c"], g + (t + 1))
                            if t >= 2:
                                pe.wait_ge(s["g_o"], g + (t - 1))
                            pe.matmul(PS[:, 6 + t % 2], wg_("wf2"), GL[:, t % 2, 1], start=True, stop=True).then_inc(s["g_wf2"], 1)

                        for t in range(NCH):
                            pe.wait_ge(s["ln_out"], ln1 + (t + 1))
                            if t >= 3:
                                pe.wait_ge(s["g_c"], g + (t - 2))
                            for e in range(2):
                                mm = pe.matmul(PS[:, 2 * (t % 3) + e], wg_("wf1", e * C, C), XN[:, tok(t)],
                                               start=True, stop=True)
                            mm.then_inc(s["g_wf1"], 1)
                            if t:
                                wf2(t - 1)
                        wf2(NCH - 1)

        @block.vector
        def _(dve):
            def layernorm(img, which, w, bias):
                base = img.all(2 * NCH) + which * NCH
                for t in range(NCH):
                    dve.wait_ge(s["ln_mean"], base + (t + 1))
                    dve.tensor_tensor(XN[:, tok(t)], XI[:, tok(t)], PS[:, t], ALU.subtract).then_inc(s["ln_cent"], 1)
                for t in range(NCH):
                    dve.wait_ge(s["ln_rstd"], base + (t + 1))
                    dve.tensor_tensor(XN[:, tok(t)], XN[:, tok(t)], RSTD[:, t], ALU.mult).then_inc(s["ln_norm"], 1)
                    dve.wait_ge(s["ln_norm"], base + (t + 1))
                    dve.tensor_scalar(XN[:, tok(t)], XN[:, tok(t)], w, bias, ALU.mult, ALU.add).then_inc(s["ln_out"], 1)

            def prepare(nxt, par, op):
                i = nxt.i
                if op == "rest":
                    dve.wait_ge(s["hi_ready"], i + 1)
                    dve.tensor_tensor(RAW[64:128], RAW[64:128], PARTS[64:128, par], ALU.subtract)\
                       .then_inc(s["rest_ready"], 1)
                if op == "low":
                    dve.wait_ge(s["mid_ready"], i + 1)
                    dve.tensor_tensor(PARTS[96:128, par], RAW[96:128], PARTS[96:128, par], ALU.subtract)\
                       .then_inc(s["parts_ready"], 1)
                if op == "round":
                    dve.wait_ge(s["e_ready"], i * DH + DH)
                    dve.tensor_scalar(ROUND[par], EXPV, 1.0, -1.0, ALU.add, ALU.add).then_inc(s["round_ready"], 1)
                if op == "delta":
                    dve.wait_ge(s["log1p_ready"], i + 1)
                    dve.tensor_tensor(DELTA[par], DELTA[par], LOGV, ALU.add).then_inc(s["delta_ready"], 1)
                if op == "input":
                    dve.wait_ge(s["delta_ready"], i + 1)
                    dve.tensor_tensor(DX[par], DELTA[par], nxt.X[:, :, nxt.tokens()], ALU.mult).then_inc(s["dx_ready"], 1)

            def scan_input(st, slot, par):
                dve.wait_ge(s["b_ready"], st + 1)
                dve.tensor_tensor(DBX[slot], DX[par], both(BB[:, slot]), ALU.mult).then_inc(s["input_ready"], 1)

            def merge(c, first):
                dve.wait_ge(s["ysum_done"], c.step + N)
                to, sums = c.out()
                if first:
                    for h in range(DH):
                        ins = dve.scalar_tensor_tensor(to[:, h], c.X[:, h, c.tokens()], DTOT[:, h:h + 1], sums[:, h],
                                                       ALU.mult, ALU.add)
                else:
                    for h in range(DH):
                        ins = dve.tensor_tensor(to[:, h], to[:, h], sums[:, h], ALU.add)
                ins.then_inc(s["y_merged"], 1)

            def chunk(c, prev, nxt, par):
                for n in range(N):
                    st = c.step + n
                    if n + 1 < N or nxt:
                        if n + 1 == N:
                            dve.wait_ge(s["dx_ready"], nxt.i + 1)
                        if prev or n >= 1:
                            dve.wait_ge(s["state_ready"], st * DH)
                        scan_input(st + 1, (n + 1) % 2, par if n + 1 < N else 1 - par)
                    dve.wait_ge(s["input_ready"], st + 1)
                    if prev or n >= 4:
                        dve.wait_ge(s["carry_ready"], st - 3)
                        dve.wait_ge(s["readout_ready"], st - 3)
                    for h in range(DH):
                        dve.wait_ge(s["decay_ready"], st * DH + (h + 1))
                        dve.tensor_tensor_scan(c.run(HS[n % RING][:, h]), c.run(DAB[:, h]), c.run(DBX[n % 2][:, h]),
                                               CARRY[:, n, h:h + 1], ALU.mult, ALU.add).then_inc(s["state_ready"], 1)
                    if n == MERGE and prev:
                        merge(prev, prev.k == DIRS[0])
                    if nxt and n in DVE_SLOTS:
                        prepare(nxt, 1 - par, DVE_SLOTS[n])

            dve.memset(ZERO[:, :], 0.0).then_inc(s["carry_cleared"], 1)
            dve.memset(CARRY[:, :, :], 0.0).then_inc(s["carry_cleared"], 1)
            dve.wait_ge(s["consts_loaded"], 32)
            for layer, (kind, _, _) in enumerate(layers):
                dve.wait_ge(s["weights_loaded"], 16 * (layer + 1))
                lay = Image(layer, 0)
                if kind == "scan":
                    dve.tensor_reduce(DTOT[:, :], wv("Ds").rearrange("p (k h) -> p h k", h=DH), AX_X, ALU.add)\
                       .then_inc(s["derived"], 1)
                    dve.wait_ge(s["a_exp"], lay.scan_layer + 1)
                    dve.tensor_scalar(ANEG[:, :], ANEG[:, :], -1.0, None, ALU.mult).then_inc(s["derived"], 0 + 1)
                else:
                    dve.tensor_tensor(SMALL[:, 0:2], wg_("b1"), wg_("wdw"), ALU.mult).then_inc(s["g_small"], 1)
                    dve.wait_ge(s["g_small"], 1)
                    dve.tensor_tensor(SMALL[:, 0:2], SMALL[:, 0:2], wg_("bdw"), ALU.add)
                    dve.tensor_tensor(SMALL[:, 2:3], wg_("beta"), wg_("b2"), ALU.mult)
                    dve.tensor_tensor(SMALL[:, 3:4], wg_("gamma"), wg_("bf2"), ALU.mult).then_inc(s["g_small"], 1)
                with dve.Fori(0, NB) as b:
                    img = Image(layer, b)
                    layernorm_w = wv if kind == "scan" else wg_
                    if kind == "scan":
                        dve.wait_ge(s["x_loaded"], img.all(16) + 16)
                        dve.memset(PAD[:, :, 0:PW:PW - 1, :], 0.0)
                        dve.memset(PAD[:, :, 1:PW - 1, 0:PW:PW - 1], 0.0).then_inc(s["border_zero"], 1)
                        for tap in range(9):
                            ins = dve.tensor_scalar(DIAG[:, tap], ident, wv("conv_w", tap, 1), None, ALU.mult)
                        ins.then_inc(s["diagonals"], 1)
                    layernorm(img, 0, layernorm_w("ln1_w"), layernorm_w("ln1_b"))
                    if kind == "scan":
                        a = img.scan(NCH)
                        for t in range(NCH):
                            dve.wait_ge(s["xx_ready"], a + (t + 1))
                            dve.tensor_copy(PAD[:, :, 1 + ROWS * t:1 + ROWS * (t + 1), 1:1 + HW],
                                            PS[:, 4 * (t % 2):4 * (t % 2) + 2].rearrange("p h (r c) -> p h r c", c=HW))\
                               .then_inc(s["padded"], 1)
                        conv = X0[:, 1].rearrange("p (r c) -> p r c", c=HW)
                        dve.wait_ge(s["padded"], a + NCH)
                        dve.wait_ge(s["border_zero"], img.scan(1) + 1)
                        for tap in range(9):
                            dy, dx = divmod(tap, 3)
                            window = PAD[:, 1, dy:dy + HW, dx:dx + HW]
                            w = wv("conv_w", 9 + tap, 1)
                            if tap:
                                dve.wait_ge(s["taps_done"], img.scan(9) + tap)
                                ins = dve.scalar_tensor_tensor(conv, window, w, conv, ALU.mult, ALU.add)
                            else:
                                ins = dve.tensor_scalar(conv, window, w, None, ALU.mult)
                            ins.then_inc(s["taps_done"], 1)
                        first = Chunk(img, 0, 0)
                        dve.wait_ge(s["x_half0"], a + NCH)
                        dve.wait_ge(s["x_half1"], img.scan(2) + 2)
                        for h in range(DH):
                            dve.tensor_copy(X1[:, h].rearrange("p (c r) -> p c r", r=HW),
                                            X0[:, h].rearrange("p (r c) -> p c r", c=HW)).then_inc(s["turned"], 1)
                        for op in DVE_SLOTS.values():
                            prepare(first, 0, op)
                        dve.wait_ge(s["dx_ready"], first.i + 1)
                        scan_input(first.step, 0, 0)
                        scans(dve, img, chunk)
                        merge(Chunk(img, K - 1, NCH - 1), False)
                        dve.wait_ge(s["y_merged"], img.scan(CHUNKS) + CHUNKS)
                        for t in range(NCH):
                            dve.wait_ge(s["on_mean"], a + (t + 1))
                            dve.tensor_tensor(Y[:, :, tok(t)], Y[:, :, tok(t)], both(PS[:, t]), ALU.subtract)\
                               .then_inc(s["on_cent"], 1)
                        for t in range(NCH):
                            dve.wait_ge(s["on_rstd"], a + (t + 1))
                            dve.tensor_tensor(Y[:, :, tok(t)], Y[:, :, tok(t)], both(RSTD[:, t]), ALU.mult)\
                               .then_inc(s["on_norm"], 1)
                        dve.wait_ge(s["residual_loaded"], img.scan(16) + 16)
                        for t in range(NCH):
                            dve.wait_ge(s["oproj"], a + (t + 1))
                            dve.tensor_tensor(XI[:, tok(t)], XI[:, tok(t)], PS[:, t], ALU.add).then_inc(s["res_done"], 1)
                        layernorm(img, 1, wv("ln2_w"), wv("ln2_b"))
                        for t in range(NCH):
                            dve.wait_ge(s["fc2_done"], a + (t + 1))
                            if t >= 2:
                                dve.wait_ge(s[f"out_stored{t % 2}"], (img.all(NCH // 2) + t // 2) * 16)
                            dve.scalar_tensor_tensor(OT[:, t % 2], PS[:, 6 + t % 2], wv("fc2_b"), XI[:, tok(t)],
                                                     ALU.add, ALU.add).then_inc(s["out_ready"], 1)
                    else:
                        g = img.own(NCH)
                        for t in range(NCH):
                            dve.wait_ge(s["g_branch"], img.own(2 * NCH) + (2 * t + 2))
                            dve.tensor_tensor(X0[:, 0, tok(t)], X0[:, 0, tok(t)], X0[:, 1, tok(t)], ALU.mult)\
                               .then_inc(s["g_mult"], 1)
                        dve.wait_ge(s["g_mult"], g + NCH)
                        dve.tensor_reduce(SMALL[:, 8:9], X0[:, 0], AX_X, ALU.add).then_inc(s["g_gap"], 1)
                        dve.wait_ge(s["g_att"], img.own(1) + 1)
                        dve.tensor_scalar(DIAG[:, 0], wg_("w2"), SMALL[:, 9:10], None, ALU.mult).then_inc(s["g_w2s"], 1)
                        for t in range(NCH):
                            dve.wait_ge(s["g_scaled"], g + (t + 1))
                            dve.tensor_tensor(XI[:, tok(t)], XI[:, tok(t)], X0[:, 1, tok(t)], ALU.add).then_inc(s["g_res"], 1)
                        layernorm(img, 1, wg_("ln2_w"), wg_("ln2_b"))

                        def result(t):
                            dve.wait_ge(s["g_o"], g + (t + 1))
                            if t >= 2:
                                dve.wait_ge(s[f"out_stored{t % 2}"], (img.all(NCH // 2) + t // 2) * 16)
                            dve.tensor_tensor(OT[:, t % 2], GL[:, t % 2, 2], XI[:, tok(t)], ALU.add).then_inc(s["out_ready"], 1)

                        for t in range(NCH):
                            dve.wait_ge(s["g_c1"], g + (t + 1))
                            if t >= 2:
                                dve.wait_ge(s["g_wf2"], g + (t - 1))
                            dve.scalar_tensor_tensor(GL[:, t % 2, 1], PS[:, 2 * (t % 3) + 1], wg_("bf1", 1, 1), GL[:, t % 2, 0],
                                                     ALU.add, ALU.mult).then_inc(s["g_c"], 1)
                            if t:
                                result(t - 1)
                        result(NCH - 1)

        @block.scalar
        def _(act):
            def layernorm(img, which, eps):
                base = img.all(2 * NCH) + which * NCH
                act.preload_act_table_set(LN_EXP)
                for t in range(NCH):
                    act.wait_ge(s["ln_cent"], base + (t + 1))
                    act.activation(SQ4[:, t], XN[:, tok(t)], ACT.Square).then_inc(s["ln_sq"], 1)
                for t in range(NCH):
                    act.wait_ge(s["ln_var"], base + (t + 1))
                    act.activation(RSTD[:, t], PS[:, t], ACT.Ln, bias=col(eps)).then_inc(s["ln_log"], 1)
                    act.wait_ge(s["ln_log"], base + (t + 1))
                    act.activation(RSTD[:, t], RSTD[:, t], ACT.Exp, scale=-0.5).then_inc(s["ln_rstd"], 1)

            def prepare(i, par, op, first=False):
                if op == "raw":
                    act.wait_ge(s["proj_ready"], i + 1)
                    if not first:
                        act.wait_ge(s["parts_ready"], i)
                    act.activation(RAW[:, :], PB, ACT.Identity, bias=col(K_ROW)).then_inc(s["raw_ready"], 1)
                if op == "hi":
                    act.wait_ge(s["raw_ready"], i + 1)
                    act.activation(PARTS[:, par], RAW[:, :], ACT.Copy).then_inc(s["hi_ready"], 1)
                if op == "mid":
                    act.wait_ge(s["rest_ready"], i + 1)
                    act.activation(PARTS[64:128, par], RAW[64:128], ACT.Copy).then_inc(s["mid_ready"], 1)
                h = 1 if op.endswith("1") else 0
                if op in ("abs0", "abs1"):
                    act.wait_ge(s["v_ready"], i * DH + (h + 1))
                    if h == 0 and not first:
                        act.wait_ge(s["log1p_ready"], i)
                    act.activation(EXPV[:, h], PB, ACT.Abs).then_inc(s["abs_done"], 1)
                if op in ("relu0", "relu1"):
                    act.activation(DELTA[par][:, h], PB, ACT.Relu).then_inc(s["v_used"], 1)
                if op in ("exp0", "exp1"):
                    act.wait_ge(s["abs_done"], i * DH + (h + 1))
                    act.activation(EXPV[:, h], EXPV[:, h], ACT.Exp, scale=-1.0).then_inc(s["e_ready"], 1)
                if op in ("log0", "log1"):
                    act.wait_ge(s["e_ready"], i * DH + (h + 1))
                    act.activation(LOGV[:, h], EXPV[:, h], ACT.Ln, bias=1.0).then_inc(s["ln_ready"], 1)

            def save(c, n, last_chunk):
                source = ZERO[:, :] if last_chunk else HS[n % RING][:, :, c.last()]
                act.activation(CARRY[:, n], source, ACT.Copy).then_inc(s["carry_ready"], 1)

            def chunk(c, prev, nxt, par):
                final = nxt is None or nxt.k != c.k
                for n in range(N):
                    st = c.step + n
                    if n == 0:
                        act.wait_ge(s["delta_ready"], c.i + 1)
                    for h in range(DH):
                        if prev or n:
                            act.wait_ge(s["state_ready"], st * DH + (h - 1))
                        a = (c.k * DH + h) * N + n
                        act.activation(DAB[:, h], DELTA[par][:, h], ACT.Exp, scale=ANEG[:, a:a + 1])\
                           .then_inc(s["decay_ready"], 1)
                    act.wait_ge(s["c_ready"], st + 1)
                    if prev or n >= RING:
                        act.wait_ge(s["readout_ready"], st - (RING - 1))
                    act.activation(CS[:, n % RING], CB, ACT.Copy).then_inc(s["c_copied"], 1)
                    if n:
                        save(c, n - 1, final)
                    elif prev:
                        save(prev, N - 1, prev.k != c.k)
                    if nxt:
                        for op in ACT_SLOTS.get(n, ()):
                            prepare(nxt.i, 1 - par, op)

            act.wait_ge(s["consts_loaded"], 32)
            act.wait_ge(s["carry_cleared"], 2)
            for layer, (kind, _, gelu) in enumerate(layers):
                act.wait_ge(s["weights_loaded"], 16 * (layer + 1))
                lay = Image(layer, 0)
                if kind == "scan":
                    act.activation(ANEG[:, :], wv("A_log"), ACT.Exp).then_inc(s["a_exp"], 1)
                else:
                    act.wait_ge(s["g_small"], 2)
                with act.Fori(0, NB) as b:
                    img = Image(layer, b)
                    layernorm(img, 0, K_EPS5 if kind == "scan" else K_EPS6)
                    if kind == "scan":
                        a = img.scan(NCH)
                        for t in range(NCH):
                            act.wait_ge(s["z_ready"], a + (t + 1))
                            if t >= 2:
                                act.wait_ge(s[f"gate_stored{t % 2}"], (img.scan(NCH // 2) + t // 2) * 16)
                            act.activation(SZT[t % 2], PS[:, 4 * (t % 2) + 2:4 * (t % 2) + 4], ACT.Silu)\
                               .then_inc(s["gate_ready"], 1)
                        for t in range(NCH):
                            act.wait_ge(s["conv0_ready"], a + (t + 1))
                            act.activation(X0[:, 0, tok(t)], PS[:, t], ACT.Silu, bias=wv("conv_b", 0, 1))\
                               .then_inc(s["x_half0"], 1)
                            if t == NCH - 3:
                                act.wait_ge(s["taps_done"], img.scan(9) + 9)
                                for i in range(2):
                                    part = X0[:, 1, i * L // 2:(i + 1) * L // 2]
                                    act.activation(part, part, ACT.Silu, bias=wv("conv_b", 1, 1)).then_inc(s["x_half1"], 1)
                        first = Chunk(img, 0, 0)
                        act.preload_act_table_set(LN_EXP)
                        for q in range(2):
                            act.wait_ge(s[f"gate_stored{q}"], (img.scan(NCH // 2) + NCH // 2) * 16)
                        for n in sorted(ACT_SLOTS):
                            for op in ACT_SLOTS[n]:
                                prepare(first.i, 0, op, True)
                        act.wait_ge(s["derived"], img.scan_layer * 2 + 2)
                        scans(act, img, chunk)
                        end = img.scan(STEPS) + STEPS
                        act.wait_ge(s["state_ready"], end * DH)
                        save(Chunk(img, K - 1, NCH - 1), N - 1, True)
                        for t in range(NCH):
                            act.wait_ge(s["on_cent"], a + (t + 1))
                            act.activation(SQ8[:, t], Y[:, :, tok(t)], ACT.Square).then_inc(s["on_sq"], 1)
                        for t in range(NCH):
                            act.wait_ge(s["on_var"], a + (t + 1))
                            act.activation(RSTD[:, t], PS[:, t], ACT.Ln, bias=col(K_EPS5)).then_inc(s["on_log"], 1)
                            act.wait_ge(s["on_log"], a + (t + 1))
                            act.activation(RSTD[:, t], RSTD[:, t], ACT.Exp, scale=-0.5).then_inc(s["on_rstd"], 1)
                        for t in range(NCH):
                            act.wait_ge(s["on_norm"], a + (t + 1))
                            for h in range(DH):
                                ins = act.activation(Y[:, h, tok(t)], Y[:, h, tok(t)], ACT.Identity,
                                                     bias=wv("onorm_b", h, 1), scale=wv("onorm_w", h, 1))
                            ins.then_inc(s["on_aff"], 1)
                        layernorm(img, 1, K_EPS5)
                        for t in range(NCH):
                            if t >= 2:
                                act.wait_ge(s["fc2_done"], a + (t - 1))
                            for p in range(2):
                                act.wait_ge(s["fc1_done"], img.scan(2 * NCH) + (2 * t + p + 1))
                                for i in range(2):
                                    f = 2 * p + i
                                    ins = act.activation(GL[:, t % 2, f], PS[:, 2 * ((2 * t + p) % 3) + i], gelu,
                                                         bias=wv("fc1_b", f, 1))
                                ins.then_inc(s["gelu_done"], 1)
                    else:
                        g = img.own(NCH)
                        for t in range(NCH):
                            act.wait_ge(s["g_w1"], g + (t + 1))
                            for e in range(2):
                                act.activation(X0[:, e, tok(t)], PS[:, 2 * (t % 4) + e], ACT.Identity,
                                               bias=SMALL[:, e:e + 1], scale=wg_("wdw", e, 1)).then_inc(s["g_branch"], 1)
                        act.wait_ge(s["g_att_ps"], img.own(1) + 1)
                        act.activation(SMALL[:, 9:10], PS[:, 0, 0:1], ACT.Identity, bias=wg_("bse"), scale=1.0 / L)\
                           .then_inc(s["g_att"], 1)
                        for t in range(NCH):
                            act.wait_ge(s["g_w2"], g + (t + 1))
                            act.activation(X0[:, 1, tok(t)], PS[:, t], ACT.Identity, bias=SMALL[:, 2:3], scale=wg_("beta"))\
                               .then_inc(s["g_scaled"], 1)
                        layernorm(img, 1, K_EPS6)

                        def scaled(t):
                            act.wait_ge(s["g_wf2"], g + (t + 1))
                            if t >= 2:
                                act.wait_ge(s["out_ready"], img.all(NCH) + (t - 1))
                            act.activation(GL[:, t % 2, 2], PS[:, 6 + t % 2], ACT.Identity, bias=SMALL[:, 3:4], scale=wg_("gamma"))\
                               .then_inc(s["g_o"], 1)

                        for t in range(NCH):
                            act.wait_ge(s["g_wf1"], g + (t + 1))
                            if t >= 2:
                                act.wait_ge(s["g_c"], g + (t - 1))
                            act.activation(GL[:, t % 2, 0], PS[:, 2 * (t % 3)], ACT.Identity, bias=wg_("bf1", 0, 1))\
                               .then_inc(s["g_c1"], 1)
                            if t:
                                scaled(t - 1)
                        scaled(NCH - 1)

        @block.gpsimd
        def _(pool):
            def prepare(i, par, op):
                if op == "error":
                    pool.wait_ge(s["round_ready"], i + 1)
                    pool.tensor_tensor(ROUND[par], EXPV, ROUND[par], ALU.subtract).then_inc(s["err_ready"], 1)
                if op == "log1p":
                    pool.wait_ge(s["ln_ready"], i * DH + DH)
                    pool.wait_ge(s["err_ready"], i + 1)
                    pool.tensor_tensor(LOGV, LOGV, ROUND[par], ALU.add).then_inc(s["log1p_ready"], 1)

            def chunk(c, prev, nxt, par):
                for n in range(N):
                    st = c.step + n
                    pool.wait_ge(s["c_copied"], st + 1)
                    if prev or n >= RING:
                        pool.wait_ge(s["ysum_done"], st - (RING - 1))
                    pool.wait_ge(s["state_ready"], st * DH + DH)
                    pool.tensor_tensor(HC[:, n % RING], HS[n % RING], both(CS[:, n % RING]), ALU.mult).then_inc(s["readout_ready"], 1)
                    if nxt and n in POOL_SLOTS:
                        prepare(nxt.i, 1 - par, POOL_SLOTS[n])

            for layer, (kind, _, _) in enumerate(layers):
                if kind != "scan":
                    continue
                with pool.Fori(0, NB) as b:
                    img = Image(layer, b)
                    a = img.scan(NCH)
                    for op in POOL_SLOTS.values():
                        prepare(Chunk(img, 0, 0).i, 0, op)
                    scans(pool, img, chunk)
                    pool.wait_ge(s["gates_loaded"], img.scan(16) + 16)
                    for t in range(NCH):
                        pool.wait_ge(s["on_aff"], a + (t + 1))
                        pool.tensor_tensor(Y[:, :, tok(t)], Y[:, :, tok(t)], X0[:, :, tok(t)], ALU.mult).then_inc(s["gated"], 1)


_V_NAMES = {0: ("ln1_w", "ln1_b", "dt_w", "dt_b", "A_log", "onorm_w", "onorm_b", "ln2_w", "ln2_b"),
            1: ("norm1_w", "norm1_b", "dt_projs_w", "dt_projs_b", "A_logs", "out_norm_w", "out_norm_b", "norm2_w", "norm2_b")}


def _cols(v):
    return np.ascontiguousarray(v.reshape(-1, P).T)


def _scan_weights(inputs, layer):
    names = _V_NAMES[min(layer, 1)]
    ln1w, ln1b, dtw, dtb, alog, onw, onb, ln2w, ln2b = (inputs[f"L{layer}_conv_{n}"] for n in names)
    g = {n: inputs[f"L{layer}_conv_{n}"] for n in ("in_proj_w", "conv_w", "conv_b", "x_proj_w", "Ds", "out_proj_w",
                                                   "fc1_w", "fc1_b", "fc2_w", "fc2_b")}
    flip = (lambda a: a) if layer == 0 else (lambda a: a.T)
    xp = g["x_proj_w"].reshape(K, R + 2 * N, DH, P).transpose(3, 0, 2, 1)
    dt, bc = xp[..., :R], xp[..., R:]
    gap = np.zeros((P, K, DH, 2 * N - R), np.float32)
    x_proj = np.concatenate([bc, dt, gap, bc, bc], axis=-1).reshape(P, -1)
    step = np.zeros((P, K, DH * P), np.float32)
    step[DT0:DT0 + R] = dtw.transpose(2, 0, 1)
    step[DT0 + R] = dtb
    parts = dict(
        in_proj=flip(g["in_proj_w"]), conv_w=g["conv_w"].reshape(DH, P, 9).transpose(1, 0, 2).reshape(P, -1),
        x_proj=x_proj, dt_w=step.reshape(P, -1),
        A_log=alog.reshape(K, DH, P, N).transpose(2, 0, 1, 3).reshape(P, -1),
        Ds=g["Ds"].reshape(K, DH, P).transpose(2, 0, 1).reshape(P, -1),
        onorm_w=_cols(onw), onorm_b=_cols(onb),
        out_proj=flip(g["out_proj_w"]).reshape(DH, P, C).transpose(1, 0, 2).reshape(P, -1),
        ln1_w=_cols(ln1w), ln1_b=_cols(ln1b), ln2_w=_cols(ln2w), ln2_b=_cols(ln2b),
        fc1=flip(g["fc1_w"]), fc1_b=_cols(g["fc1_b"]),
        fc2=flip(g["fc2_w"]).reshape(FF, P, C).transpose(1, 0, 2).reshape(P, -1), fc2_b=_cols(g["fc2_b"]),
        conv_b=_cols(g["conv_b"]))
    return np.ascontiguousarray(np.concatenate([parts[n] for n in V_COLS], axis=1))


def _gated_weights(inputs):
    g = {n: inputs[f"L2_conv_{n}"] for n in ("w1", "wse", "w2", "wf1", "wf2", "b1", "wdw", "bdw", "bse", "b2", "bf1", "bf2",
                                             "beta", "gamma", "ln1_scale", "ln1_bias", "ln2_scale", "ln2_bias")}
    g.update(ln1_w=g["ln1_scale"], ln1_b=g["ln1_bias"], ln2_w=g["ln2_scale"], ln2_b=g["ln2_bias"])
    mats = ("w1", "wse", "w2", "wf1", "wf2")
    return np.ascontiguousarray(np.concatenate([g[n] if n in mats else _cols(g[n]) for n in G_COLS], axis=1))


def _constants():
    c = np.zeros((P, KW), np.float32)
    c[:, K_ID:K_ID + P] = np.eye(P)
    c[:, K_128:K_128 + P] = 1.0 / P
    c[:, K_256:K_256 + P] = 1.0 / (DH * P)
    c[:, K_EPS5], c[:, K_EPS6] = 1e-5, 1e-6
    c[DT0 + R, K_ROW] = 1.0
    sel = np.zeros((P, 2 * N, P), np.float32)
    for row in range(2 * N):
        for part in (0, 64, 96):
            sel[part + row, row, :] = 1.0
    return c, sel


def kernel(**inputs):
    import concourse.bacc as _bacc
    from concourse.bass_utils import run_bass_kernel_spmd as _run
    inputs = {n: np.asarray(a) for n, a in inputs.items()}
    consts, sel = _constants()
    x = np.ascontiguousarray(inputs["x"].reshape(NB, L, C).transpose(0, 2, 1))
    arrays = {"in_x": x, "consts": consts, "sel": sel.astype(mybir.dt.np(BF16)),
              "w0": _scan_weights(inputs, 0), "w1": _scan_weights(inputs, 1), "wg": _gated_weights(inputs),
              "w3": _scan_weights(inputs, 3)}
    nc = _bacc.Bacc("TRN2", target_bir_lowering=False, num_devices=1)
    args = [nc.dram_tensor(n, a.shape, mybir.dt.from_np(a.dtype), kind="ExternalInput").ap() for n, a in arrays.items()]
    args.append(nc.dram_tensor("out_0", (NB, C, L), F32, kind="ExternalOutput").ap())
    program(nc, *args)
    r = _run(nc, [arrays], core_ids=[0])
    return np.ascontiguousarray(r.results[0]["out_0"].transpose(0, 2, 1)).reshape(NB, HW, HW, C)
```

```python
from contextlib import ExitStack

import numpy as np
import concourse.bass as bass
from concourse import mybir

F32 = mybir.dt.float32
BF16 = mybir.dt.bfloat16
ALU = mybir.AluOpType
ACT = mybir.ActivationFunctionType
AX_X = mybir.AxisListType.X

P = 128
NB, HW, C = 4, 64, 128
L = HW * HW
DH = 2
N, R, K = 16, 8, 4
CH = 512
NCH = L // CH
ROWS = CH // HW
PW = HW + 2
FF = 4
DIRS = (0, 2, 1, 3)
STEPS = N * NCH * K
CHUNKS = NCH * K
RING = 4
LAG = 4
PE_SLOTS = {0: "project", 2: "step0", 4: "step1", 8: "rest", 11: "tail"}
ACT_SLOTS = {1: ("raw",), 2: ("hi",), 3: ("abs0", "relu0"), 5: ("abs1", "relu1"), 6: ("exp0",), 7: ("exp1", "log0"),
             8: ("log1",), 10: ("mid",), 13: ("low",)}
DVE_SLOTS = {(8, 0): "round", (13, 1): "delta", (14, 0): "input"}
POOL_SLOTS = {8: "error", 10: "log1p"}
MERGE = 4
BASE = 14
TURN = 12
CONV_PE = 5
CONV_DVE = [(1, t, 2) for t in range(0, NCH, 2)] + [(0, CONV_PE, NCH - CONV_PE)]
TAPS = [9 * sum(n for _, _, n in CONV_DVE[:u]) for u in range(len(CONV_DVE) + 1)]
FINISH = (0, "pe0", "raw", 1, "pe1", "abs0", "relu0", 2, "abs1", "relu1", "hi", "pe2", "exp0", "exp1", "log0", "log1",
          3, "mid", "pe3", "low", "pe4", 4)
X_ORDER = [f for f in FINISH if f in range(len(CONV_DVE)) or str(f).startswith("pe")]
PE_FIRST = {(1, 3): "project", (2, 0): "step0", (2, 7): "step1", (3, 2): "rest", (3, 8): "tail"}
LAST_TAPS = {3: "round", 8: "delta"}
LN_EXP = "natural_log_exp_and_others"
DT0 = 32

V_COLS = {}
_at = 0
for _name, _n in (("in_proj", 4 * C), ("conv_w", DH * 9), ("x_proj", K * DH * P), ("dt_w", K * DH * P),
                  ("A_log", K * DH * N), ("Ds", K * DH), ("onorm_w", DH), ("onorm_b", DH), ("out_proj", DH * C),
                  ("ln1_w", 1), ("ln1_b", 1), ("ln2_w", 1), ("ln2_b", 1), ("fc1", FF * C), ("fc1_b", FF),
                  ("fc2", FF * C), ("fc2_b", 1), ("conv_b", DH)):
    V_COLS[_name] = (_at, _at + _n)
    _at += _n
VW = _at
G_COLS = {}
_at = 0
for _name, _n in (("w1", 2 * C), ("wse", C), ("w2", C), ("wf1", 2 * C), ("wf2", C), ("b1", 2), ("wdw", 2), ("bdw", 2),
                  ("bse", 1), ("b2", 1), ("bf1", 2), ("bf2", 1), ("beta", 1), ("gamma", 1),
                  ("ln1_w", 1), ("ln1_b", 1), ("ln2_w", 1), ("ln2_b", 1)):
    G_COLS[_name] = (_at, _at + _n)
    _at += _n
GW = _at
K_ID, K_128, K_256, K_EPS5, K_EPS6, K_ROW = 0, P, 2 * P, 3 * P, 3 * P + 1, 3 * P + 2
KW = 3 * P + 3


def program(nc, x_in, consts, sel_in, w0, w1, wg, w3, out):
    ctx = ExitStack()
    with ctx:
        def sb(name, shape, dt=F32):
            return ctx.enter_context(nc.sbuf_tensor(name, shape, dt))

        def sem(name):
            return ctx.enter_context(nc.semaphore(name))

        layers = [("scan", w0, ACT.Gelu), ("scan", w1, ACT.Gelu_apprx_tanh), ("gated", wg, None),
                  ("scan", w3, ACT.Gelu_apprx_tanh)]
        hidden = [nc.dram_tensor(f"hidden{i}", [NB, P, L], F32).ap() for i in range(3)]
        gates = nc.dram_tensor("gates", [P, DH, L], F32).ap()
        sources = [x_in, *hidden]
        targets = [*hidden, out]

        X0 = sb("X0", [P, DH, L])
        X1 = sb("X1", [P, DH, L])
        YP = sb("YP", [P, DH * PW * PW])
        W = sb("W", [P, VW])
        KC = sb("KC", [P, KW])
        SEL = sb("SEL", [P, 2 * N, P], BF16)
        ANEG = sb("ANEG", [P, K * DH * N])
        DTOT = sb("DTOT", [P, DH])
        DSUM = sb("DSUM", [P, DH, P])
        MINUS = sb("MINUS", [P, P], BF16)
        MINUS2 = sb("MINUS2", [P, P], BF16)
        SMALL = sb("SMALL", [P, 16])
        WK = sb("WK", [P, 12 * 2 * CH])
        HC = sb("HC", [P, RING, DH, CH])
        CS = sb("CS", [P, RING, CH])
        DIAG = CS[:, :, :].rearrange("p s (t c) -> p (s t) c", c=P)
        PARTS = sb("PARTS", [P, 2, CH], BF16)
        RAW = sb("RAW", [P, CH])
        CARRY = sb("CARRY", [P, N, DH])
        ZERO = sb("ZERO", [P, DH])
        PS = ctx.enter_context(nc.psum_tensor("PS", [P, 8, CH], F32))

        def work(i):
            return WK[:, 2 * CH * i:2 * CH * (i + 1)].rearrange("p (h l) -> p h l", h=DH)

        DELTA = [work(0), work(1)]
        DX = [work(2), work(3)]
        EXPV, LOGV = work(4), work(5)
        DBX = [work(6), work(7)]
        HS = [work(8 + i) for i in range(RING)]
        ROUND = DX
        PAD = YP[:, :].rearrange("p (h r c) -> p h r c", h=DH, r=PW)
        Y = YP[:, 0:DH * L].rearrange("p (h l) -> p h l", h=DH)
        YT = YP[:, 0:DH * L].rearrange("p (h r c) -> p h c r", h=DH, r=HW)
        SQ8 = WK[:, 0:NCH * 2 * CH].rearrange("p (t h l) -> p t h l", t=NCH, h=DH)
        SQ4 = YP[:, 0:L].rearrange("p (t l) -> p t l", t=NCH)
        RSTD = WK[:, 2 * L:3 * L].rearrange("p (t l) -> p t l", t=NCH)
        GL = WK[:, 0:2 * FF * CH].rearrange("p (s f l) -> p s f l", s=2, f=FF)
        OT = WK[:, 2 * FF * CH:2 * FF * CH + 2 * CH].rearrange("p (s l) -> p s l", s=2)
        SZT = [work(0), work(1)]
        XIN = {"scan": X0[:, 0], "gated": Y[:, 1]}
        XI, XN = X1[:, 0, :], X1[:, 1, :]
        YB, DAB, BB, CB, PB = PS[:, 0:2], PS[:, 2:4], PS[:, 4:6], PS[:, 6], PS[:, 7]

        ident, ones128, ones256 = KC[:, K_ID:K_ID + P], KC[:, K_128:K_128 + P], KC[:, K_256:K_256 + P]

        def col(i):
            return KC[:, i:i + 1]

        def wv(name, a=0, n=None):
            lo, hi = V_COLS[name]
            return W[:, lo + a:hi if n is None else lo + a + n]

        def wg_(name, a=0, n=None):
            lo, hi = G_COLS[name]
            return W[:, lo + a:hi if n is None else lo + a + n]

        def tok(t):
            return slice(t * CH, (t + 1) * CH)

        def both(ap):
            return ap.rearrange("p (o l) -> p o l", o=1).to_broadcast([P, DH, CH])

        s = {name: sem(name) for name in (
            "consts_loaded", "weights_loaded", "x_loaded", "gates_loaded", "residual_loaded",
            "gate_stored0", "gate_stored1", "out_stored0", "out_stored1",
            "derived", "diagonals", "carry_cleared", "a_exp",
            "ln_mean", "ln_cent", "ln_sq", "ln_var", "ln_log", "ln_rstd", "ln_norm", "ln_out",
            "border_zero", "xx_ready", "z_ready", "gate_ready", "padded", "conv0_ready", "taps_done", "x_ready",
            "turned",
            "proj_ready", "raw_ready", "hi_ready", "rest_ready", "mid_ready", "tail_ready", "parts_ready", "v_ready", "v_used",
            "abs_done", "e_ready", "ln_ready", "round_ready", "err_ready", "log1p_ready", "delta_ready", "dx_ready",
            "b_ready", "c_ready", "decay_ready", "c_copied", "input_ready", "state_ready", "carry_ready",
            "readout_ready", "ysum_done", "y_merged",
            "on_half", "on_mean", "on_cent", "on_sq", "on_sum", "on_var", "on_log", "on_rstd", "on_norm", "gated", "oproj",
            "res_done", "fc1_done", "gelu_done", "fc2_done", "out_ready",
            "g_small", "g_w1", "g_branch", "g_mult", "g_gap", "g_att_ps", "g_att", "g_w2s", "g_w2", "g_scaled",
            "g_res", "g_wf1", "g_c1", "g_c", "g_wf2", "g_o")}

        class Image:

            def __init__(self, layer, b):
                self.layer, self.b = layer, b
                self.scan_layer = {0: 0, 1: 1, 3: 2}.get(layer, 0)

            def all(self, per):
                return self.b * per + self.layer * NB * per

            def scan(self, per):
                return self.b * per + self.scan_layer * NB * per

            def results(self, t):
                return self.all(NCH) + NCH + t

            def own(self, per):
                return self.b * per

        class Chunk:

            def __init__(self, img, ki, j):
                self.k = DIRS[ki]
                self.o, self.back = self.k % 2, self.k // 2
                self.pos = j * -1 + (NCH - 1) if self.back else j
                self.i = img.scan(CHUNKS) + ki * NCH + j
                self.step = img.scan(STEPS) + (ki * NCH + j) * N
                self.X = X1 if self.o else X0
                self.turned = img.scan(NCH) + NCH

            def tokens(self):
                if isinstance(self.pos, int):
                    return slice(self.pos * CH, (self.pos + 1) * CH)
                return bass.ds(self.pos * CH, CH)

            def last(self):
                return 0 if self.back else CH - 1

            def run(self, ap):
                return ap[:, ::-1] if self.back else ap

            def out(self):
                if not self.o:
                    return Y[:, :, self.tokens()]
                cols = (slice(self.pos * ROWS, (self.pos + 1) * ROWS) if isinstance(self.pos, int)
                        else bass.ds(self.pos * ROWS, ROWS))
                return YT[:, :, cols, :]

            def sums(self):
                return YB.rearrange("p h (c r) -> p h c r", r=HW) if self.o else YB

        def scans(engine, img, body):
            for ki in range(K):
                before = Chunk(img, ki - 1, NCH - 1) if ki else None
                after = Chunk(img, ki + 1, 0) if ki + 1 < K else None
                body(Chunk(img, ki, 0), before, Chunk(img, ki, 1), 0)
                with engine.Fori(0, NCH // 2 - 1) as j:
                    for u in (1, 2):
                        body(Chunk(img, ki, 2 * j + u), Chunk(img, ki, 2 * j + (u - 1)),
                             Chunk(img, ki, 2 * j + (u + 1)), u % 2)
                body(Chunk(img, ki, NCH - 1), Chunk(img, ki, NCH - 2), after, 1)

        block = ctx.enter_context(nc.Block())

        @block.sync
        def _(sp):
            sp.dma_start(KC[:, :], consts).then_inc(s["consts_loaded"], 16)
            sp.dma_start(SEL[:, :, :], sel_in).then_inc(s["consts_loaded"], 16)
            for layer, (kind, weights, _) in enumerate(layers):
                src, dst = sources[layer], targets[layer]

                def load(images, b, to, ready):
                    sp.dma_start(to, images[bass.ds(b, 1)].rearrange("o p l -> p (o l)")).then_inc(s[ready], 16)

                def stored(img):
                    for q in range(2):
                        sp.wait_ge(s[f"out_stored{q}"], img.all(NCH // 2) * 16)

                def image(b, more):
                    img = Image(layer, b)
                    if not isinstance(b, int) or b > 0:
                        stored(img)
                    if kind == "gated":
                        load(src, b, XI, "residual_loaded")
                    else:
                        for t in range(NCH):
                            sp.wait_ge(s["gate_ready"], img.scan(NCH) + (t + 1))
                            sp.dma_start(gates[:, :, tok(t)], SZT[t % 2]).then_inc(s[f"gate_stored{t % 2}"], 16)
                        for q in range(2):
                            sp.wait_ge(s[f"gate_stored{q}"], (img.scan(NCH // 2) + NCH // 2) * 16)
                        sp.wait_ge(s["y_merged"], img.scan(CHUNKS) + 2 * NCH)
                        sp.dma_start(X0[:, :, :], gates).then_inc(s["gates_loaded"], 16)
                        sp.wait_ge(s["y_merged"], img.scan(CHUNKS) + CHUNKS)
                        load(src, b, XI, "residual_loaded")
                    for t in range(NCH):
                        sp.wait_ge(s["out_ready"], img.results(t + 1))
                        sp.dma_start(dst[bass.ds(b, 1), :, tok(t)].rearrange("o p l -> p (o l)"),
                                     OT[:, t % 2]).then_inc(s[f"out_stored{t % 2}"], 16)
                        if more and t == 0:
                            load(src[1:NB], b, XIN[kind], "x_loaded")

                if layer:
                    stored(Image(layer, 0))
                load(src, 0, XIN[kind], "x_loaded")
                sp.dma_start(W[:, 0:VW if kind == "scan" else GW], weights).then_inc(s["weights_loaded"], 16)
                image(0, True)
                with sp.Fori(1, NB - 1) as b:
                    image(b, True)
                image(NB - 1, False)
            for q in range(2):
                sp.wait_ge(s[f"out_stored{q}"], 16 * len(layers) * NB * NCH // 2)

        @block.tensor
        def _(pe):
            def layernorm(img, which, source, ready, per, count):
                base = img.all(2 * NCH) + which * NCH
                for t in range(NCH):
                    pe.wait_ge(s[ready], per + count(t))
                    pe.matmul(PS[:, t], ones128, source[:, tok(t)], start=True, stop=True).then_inc(s["ln_mean"], 1)
                for t in range(NCH):
                    pe.wait_ge(s["ln_sq"], base + (t + 1))
                    pe.matmul(PS[:, t], ones128, SQ4[:, t], start=True, stop=True).then_inc(s["ln_var"], 1)

            def project(nxt):
                for h in range(DH):
                    mm = pe.matmul(PB, wv("x_proj", (nxt.k * DH + h) * P, P), nxt.X[:, h, nxt.tokens()],
                                   start=(h == 0), stop=(h == 1))
                mm.then_inc(s["proj_ready"], 1)

            def prepare(nxt, par, op):
                if op == "project":
                    project(nxt)
                if op == "rest":
                    pe.wait_ge(s["v_used"], nxt.i * DH + DH)
                    pe.wait_ge(s["hi_ready"], nxt.i + 1)
                    pe.matmul(PB, ident, RAW[:, :], start=True, stop=False)
                    pe.matmul(PB, MINUS[:, :], PARTS[:, par], start=False, stop=True).then_inc(s["rest_ready"], 1)
                if op == "tail":
                    pe.wait_ge(s["mid_ready"], nxt.i + 1)
                    pe.matmul(PB, ident, RAW[:, :], start=True, stop=False)
                    pe.matmul(PB, MINUS2[:, :], PARTS[:, par], start=False, stop=True).then_inc(s["tail_ready"], 1)
                if op == "step0":
                    pe.wait_ge(s["raw_ready"], nxt.i + 1)
                    step_size(nxt, 0)
                if op == "step1":
                    pe.wait_ge(s["v_used"], nxt.i * DH + 1)
                    step_size(nxt, 1)

            def step_size(nxt, h):
                pe.matmul(PB, wv("dt_w", (nxt.k * DH + h) * P, P)[DT0:DT0 + R + 1], RAW[DT0:DT0 + R + 1],
                          start=True, stop=True).then_inc(s["v_ready"], 1)

            def spread(bank, row, parity):
                return pe.matmul(bank, SEL[:, row], PARTS[:, parity], start=True, stop=True)

            def sum_base(c, first):
                for h in range(DH):
                    if first:
                        pe.matmul(YB[:, h], DSUM[:, h], X0[:, h, c.tokens()], start=False, stop=False)
                    else:
                        pe.matmul(c.sums()[:, h], ident, c.out()[:, h], start=False, stop=False)

            def sum_states(n, slot):
                for h in range(DH):
                    mm = pe.matmul(YB[:, h], ident, HC[:, slot, h], start=(n == 0), stop=(n == N - 1))
                mm.then_inc(s["ysum_done"], 1)

            def chunk(c, prev, nxt, par):
                for n in range(N):
                    st = c.step + n
                    if n + 2 < N or nxt:
                        pe.wait_ge(s["input_ready"], st * DH + DH)
                        if n + 2 == N:
                            pe.wait_ge(s["parts_ready"], c.i + 2)
                        m = (n + 2) % N
                        spread(BB[:, n % 2], m, par if n + 2 < N else 1 - par).then_inc(s["b_ready"], 1)
                    if n + 1 < N or nxt:
                        pe.wait_ge(s["c_copied"], st + 1)
                        m = (n + 1) % N
                        spread(CB, N + m, par if n + 1 < N else 1 - par).then_inc(s["c_ready"], 1)
                    if nxt and n in PE_SLOTS:
                        if PE_SLOTS[n] == "project":
                            if nxt.o and not c.o:
                                pe.wait_ge(s["turned"], c.turned)
                            pe.wait_ge(s["v_used"], c.i * DH + DH)
                        prepare(nxt, 1 - par, PE_SLOTS[n])
                    if n >= LAG or prev:
                        if n == LAG and prev:
                            pe.wait_ge(s["y_merged"], c.i)
                        pe.wait_ge(s["readout_ready"], st - (LAG - 1))
                        sum_states((n - LAG) % N, (n - LAG) % RING)
                    if n == BASE:
                        sum_base(c, c.k == DIRS[0])

            pe.wait_ge(s["consts_loaded"], 32)
            for layer, (kind, _, _) in enumerate(layers):
                pe.wait_ge(s["weights_loaded"], 16 * (layer + 1))
                if kind == "scan":
                    pe.wait_ge(s["derived"], Image(layer, 0).scan_layer * 7 + 7)
                with pe.Fori(0, NB) as b:
                    img = Image(layer, b)
                    pe.wait_ge(s["out_ready"], img.results(0))
                    layernorm(img, 0, XIN[kind], "x_loaded", img.all(16) + 16, lambda t: 0)
                    ln0 = img.all(2 * NCH)
                    if kind == "scan":
                        a = img.scan(NCH)
                        for t in range(NCH):
                            pe.wait_ge(s["ln_out"], ln0 + (t + 1))
                            if t < 2:
                                pe.wait_ge(s["ln_log"], ln0 + 4 * (t + 1))
                            else:
                                pe.wait_ge(s["padded"], a + (t - 1))
                                pe.wait_ge(s["gate_ready"], a + (t - 1))
                            for e in range(4):
                                mm = pe.matmul(PS[:, 4 * (t % 2) + e], wv("in_proj", e * C, C), XN[:, tok(t)],
                                               start=True, stop=True)
                                if e == 1:
                                    mm.then_inc(s["xx_ready"], 1)
                            mm.then_inc(s["z_ready"], 1)
                        pe.wait_ge(s["padded"], a + NCH - 1)
                        pe.wait_ge(s["gate_ready"], a + NCH - 1)
                        pe.wait_ge(s["border_zero"], img.scan(1) + 1)
                        pe.wait_ge(s["diagonals"], img.scan(1) + 1)
                        first, x = Chunk(img, 0, 0), img.scan(len(X_ORDER))
                        for t in range(CONV_PE):
                            if t >= 4:
                                pe.wait_ge(s["x_ready"], x + (X_ORDER.index(f"pe{t - 4}") + 1))
                            for tap in range(9):
                                dy, dx = divmod(tap, 3)
                                mm = pe.matmul(PS[:, t % 4], DIAG[:, tap],
                                               PAD[:, 0, ROWS * t + dy:ROWS * (t + 1) + dy, dx:dx + HW],
                                               start=(tap == 0), stop=(tap == 8))
                                if tap == 8:
                                    mm.then_inc(s["conv0_ready"], 1)
                                op = PE_FIRST.get((t, tap))
                                if op == "project":
                                    pe.wait_ge(s["gate_ready"], a + NCH)
                                    pe.wait_ge(s["x_ready"], x + (max(X_ORDER.index(0), X_ORDER.index("pe0")) + 1))
                                if op:
                                    prepare(first, 0, op)
                        pe.wait_ge(s["parts_ready"], first.i + 1)
                        spread(BB[:, 0], 0, 0).then_inc(s["b_ready"], 1)
                        spread(BB[:, 1], 1, 0).then_inc(s["b_ready"], 1)
                        spread(CB, N, 0).then_inc(s["c_ready"], 1)
                        pe.wait_ge(s["x_ready"], x + len(X_ORDER))
                        scans(pe, img, chunk)
                        end = img.scan(STEPS) + STEPS
                        for n in range(N - LAG, N):
                            pe.wait_ge(s["readout_ready"], end - (N - 1 - n))
                            sum_states(n, n % RING)
                        for t in range(NCH):
                            pe.wait_ge(s["on_half"], a + (t + 1))
                            pe.matmul(PS[:, t], ones256, SQ8[:, t, 0], start=True, stop=True).then_inc(s["on_mean"], 1)
                        for t in range(NCH):
                            pe.wait_ge(s["on_sum"], a + (t + 1))
                            pe.matmul(PS[:, t], ones256, SQ8[:, t, 0], start=True, stop=True).then_inc(s["on_var"], 1)
                        for t in range(NCH):
                            for h in range(DH):
                                pe.wait_ge(s["gated"], img.scan(NCH * DH) + (t * DH + h + 1))
                                mm = pe.matmul(PS[:, t], wv("out_proj", h * C, C), Y[:, h, tok(t)],
                                               start=(h == 0), stop=(h == 1))
                            mm.then_inc(s["oproj"], 1)
                        layernorm(img, 1, XI, "res_done", a, lambda t: t + 1)
                        ln1 = img.all(2 * NCH) + NCH

                        def fc2(t):
                            pe.wait_ge(s["gelu_done"], img.scan(2 * NCH) + (2 * t + 2))
                            if t >= 2:
                                pe.wait_ge(s["out_ready"], img.results(t - 1))
                            elif t == 0:
                                pe.wait_ge(s["ln_log"], ln1 + NCH)
                            for f in range(FF):
                                mm = pe.matmul(PS[:, 6 + t % 2], wv("fc2", f * C, C), GL[:, t % 2, f],
                                               start=(f == 0), stop=(f == FF - 1))
                            mm.then_inc(s["fc2_done"], 1)

                        for t in range(NCH):
                            pe.wait_ge(s["ln_out"], ln1 + (t + 1))
                            for p in range(2):
                                q = 2 * t + p
                                if q < 3:
                                    pe.wait_ge(s["ln_log"], ln1 + 2 * (q + 1))
                                else:
                                    pe.wait_ge(s["gelu_done"], img.scan(2 * NCH) + (q - 2))
                                for i in range(2):
                                    mm = pe.matmul(PS[:, 2 * (q % 3) + i], wv("fc1", (2 * p + i) * C, C), XN[:, tok(t)],
                                                   start=True, stop=True)
                                mm.then_inc(s["fc1_done"], 1)
                            if t:
                                fc2(t - 1)
                        fc2(NCH - 1)
                    else:
                        g = img.own(NCH)
                        for t in range(NCH):
                            pe.wait_ge(s["ln_out"], ln0 + (t + 1))
                            if t < 4:
                                pe.wait_ge(s["ln_log"], ln0 + 2 * (t + 1))
                            else:
                                pe.wait_ge(s["g_branch"], img.own(2 * NCH) + 2 * (t - 3))
                            for e in range(2):
                                mm = pe.matmul(PS[:, 2 * (t % 4) + e], wg_("w1", e * C, C), XN[:, tok(t)],
                                               start=True, stop=True)
                            mm.then_inc(s["g_w1"], 1)
                        pe.wait_ge(s["g_gap"], img.own(1) + 1)
                        pe.matmul(PS[:, 0, 0:1], wg_("wse"), SMALL[:, 8:9], start=True, stop=True).then_inc(s["g_att_ps"], 1)
                        pe.wait_ge(s["g_w2s"], img.own(1) + 1)
                        for t in range(NCH):
                            pe.matmul(PS[:, t], DIAG[:, 0], X0[:, 0, tok(t)], start=True, stop=True).then_inc(s["g_w2"], 1)
                        layernorm(img, 1, XI, "g_res", g, lambda t: t + 1)
                        ln1 = img.all(2 * NCH) + NCH
                        pe.wait_ge(s["ln_log"], ln1 + NCH)

                        def wf2(t):
                            pe.wait_ge(s["g_c"], g + (t + 1))
                            if t >= 2:
                                pe.wait_ge(s["g_o"], g + (t - 1))
                            pe.matmul(PS[:, 6 + t % 2], wg_("wf2"), GL[:, t % 2, 1], start=True, stop=True).then_inc(s["g_wf2"], 1)

                        for t in range(NCH):
                            pe.wait_ge(s["ln_out"], ln1 + (t + 1))
                            if t >= 3:
                                pe.wait_ge(s["g_c"], g + (t - 2))
                            for e in range(2):
                                mm = pe.matmul(PS[:, 2 * (t % 3) + e], wg_("wf1", e * C, C), XN[:, tok(t)],
                                               start=True, stop=True)
                            mm.then_inc(s["g_wf1"], 1)
                            if t:
                                wf2(t - 1)
                        wf2(NCH - 1)

        @block.vector
        def _(dve):
            def layernorm(img, which, source, w, bias):
                base = img.all(2 * NCH) + which * NCH
                for t in range(NCH):
                    dve.wait_ge(s["ln_mean"], base + (t + 1))
                    dve.tensor_tensor(XN[:, tok(t)], source[:, tok(t)], PS[:, t], ALU.subtract).then_inc(s["ln_cent"], 1)
                for t in range(NCH):
                    dve.wait_ge(s["ln_rstd"], base + (t + 1))
                    dve.tensor_tensor(XN[:, tok(t)], XN[:, tok(t)], RSTD[:, t], ALU.mult).then_inc(s["ln_norm"], 1)
                    dve.wait_ge(s["ln_norm"], base + (t + 1))
                    dve.tensor_scalar(XN[:, tok(t)], XN[:, tok(t)], w, bias, ALU.mult, ALU.add).then_inc(s["ln_out"], 1)

            def prepare(nxt, par, op):
                i = nxt.i
                if op == "round":
                    dve.wait_ge(s["e_ready"], i * DH + DH)
                    dve.tensor_scalar(ROUND[par], EXPV, 1.0, -1.0, ALU.add, ALU.add).then_inc(s["round_ready"], 1)
                if op == "delta":
                    dve.wait_ge(s["log1p_ready"], i + 1)
                    dve.tensor_tensor(DELTA[par], DELTA[par], LOGV, ALU.add).then_inc(s["delta_ready"], 1)
                if op == "input":
                    dve.wait_ge(s["delta_ready"], i + 1)
                    dve.tensor_tensor(DX[par], DELTA[par], nxt.X[:, :, nxt.tokens()], ALU.mult).then_inc(s["dx_ready"], 1)

            def scan_input(st, slot, par, h):
                if h == 0:
                    dve.wait_ge(s["b_ready"], st + 1)
                dve.tensor_tensor(DBX[slot][:, h], DX[par][:, h], BB[:, slot], ALU.mult).then_inc(s["input_ready"], 1)

            def chunk(c, prev, nxt, par):
                for n in range(N):
                    st = c.step + n
                    for h in range(DH):
                        if n + 1 < N or nxt:
                            if n + 1 == N and h == 0:
                                dve.wait_ge(s["dx_ready"], nxt.i + 1)
                            if prev or n >= 1:
                                dve.wait_ge(s["state_ready"], st * DH + (h - 1))
                            scan_input(st + 1, (n + 1) % 2, par if n + 1 < N else 1 - par, h)
                        dve.wait_ge(s["input_ready"], st * DH + (h + 1))
                        if h == 0 and (prev or n >= RING):
                            dve.wait_ge(s["carry_ready"], st - (RING - 1))
                            dve.wait_ge(s["readout_ready"], st - (RING - 1))
                        dve.wait_ge(s["decay_ready"], st * DH + (h + 1))
                        dve.tensor_tensor_scan(c.run(HS[n % RING][:, h]), c.run(DAB[:, h]), c.run(DBX[n % 2][:, h]),
                                               CARRY[:, n, h:h + 1], ALU.mult, ALU.add).then_inc(s["state_ready"], 1)
                        if nxt and (n, h) in DVE_SLOTS:
                            prepare(nxt, 1 - par, DVE_SLOTS[n, h])

            dve.memset(ZERO[:, :], 0.0).then_inc(s["carry_cleared"], 1)
            dve.memset(CARRY[:, :, :], 0.0).then_inc(s["carry_cleared"], 1)
            dve.memset(SMALL[:, :], 0.0).then_inc(s["out_ready"], NCH)
            dve.wait_ge(s["consts_loaded"], 32)
            for layer, (kind, _, _) in enumerate(layers):
                dve.wait_ge(s["weights_loaded"], 16 * (layer + 1))
                lay = Image(layer, 0)
                if kind == "scan":
                    dve.tensor_reduce(DTOT[:, :], wv("Ds").rearrange("p (k h) -> p h k", h=DH), AX_X, ALU.add)\
                       .then_inc(s["derived"], 1)
                    dve.wait_ge(s["a_exp"], lay.scan_layer + 1)
                    dve.tensor_scalar(ANEG[:, :], ANEG[:, :], -1.0, None, ALU.mult).then_inc(s["derived"], 1)
                    dve.wait_ge(s["derived"], lay.scan_layer * 7 + 2)
                    for h in range(DH):
                        dve.tensor_scalar(DSUM[:, h], ident, DTOT[:, h:h + 1], None, ALU.mult).then_inc(s["derived"], 1)
                    dve.tensor_scalar(MINUS[:, :], ident, -1.0, None, ALU.mult).then_inc(s["derived"], 1)
                    dve.tensor_scalar(MINUS2[:, 0:96], ident[:, 0:96], -1.0, None, ALU.mult)
                    dve.tensor_scalar(MINUS2[:, 96:P], ident[:, 96:P], -1.0, None, ALU.mult).then_inc(s["derived"], 1)
                    dve.wait_ge(s["derived"], lay.scan_layer * 7 + 6)
                    dve.scalar_tensor_tensor(MINUS2[:, 96:P], ident[:, 64:96], -1.0, MINUS2[:, 96:P], ALU.mult, ALU.add)\
                       .then_inc(s["derived"], 1)
                else:
                    dve.tensor_tensor(SMALL[:, 0:2], wg_("b1"), wg_("wdw"), ALU.mult).then_inc(s["g_small"], 1)
                    dve.wait_ge(s["g_small"], 1)
                    dve.tensor_tensor(SMALL[:, 0:2], SMALL[:, 0:2], wg_("bdw"), ALU.add)
                    dve.tensor_tensor(SMALL[:, 2:3], wg_("beta"), wg_("b2"), ALU.mult)
                    dve.tensor_tensor(SMALL[:, 3:4], wg_("gamma"), wg_("bf2"), ALU.mult).then_inc(s["g_small"], 1)
                with dve.Fori(0, NB) as b:
                    img = Image(layer, b)
                    layernorm_w = wv if kind == "scan" else wg_
                    layernorm(img, 0, XIN[kind], layernorm_w("ln1_w"), layernorm_w("ln1_b"))
                    if kind == "scan":
                        a = img.scan(NCH)
                        dve.memset(PAD[:, :, 0:PW:PW - 1, :], 0.0)
                        dve.memset(PAD[:, :, 1:PW - 1, 0:PW:PW - 1], 0.0).then_inc(s["border_zero"], 1)
                        for tap in range(9):
                            ins = dve.tensor_scalar(DIAG[:, tap], ident, wv("conv_w", tap, 1), None, ALU.mult)
                        ins.then_inc(s["diagonals"], 1)
                        first, taps = Chunk(img, 0, 0), img.scan(TAPS[-1])
                        dve.wait_ge(s["border_zero"], img.scan(1) + 1)
                        for u, (half, t0, parts) in enumerate(CONV_DVE):
                            dve.wait_ge(s["padded"], a + min(t0 + parts + 1, NCH))
                            for tap in range(9):
                                dy, dx = divmod(tap, 3)
                                w = wv("conv_w", 9 * half + tap, 1)
                                for i in range(parts):
                                    t = t0 + i
                                    conv = X0[:, half, tok(t)].rearrange("p (r c) -> p r c", c=HW)
                                    window = PAD[:, half, ROWS * t + dy:ROWS * (t + 1) + dy, dx:dx + HW]
                                    if tap:
                                        dve.wait_ge(s["taps_done"], taps + (TAPS[u] + parts * (tap - 1) + i + 1))
                                        ins = dve.scalar_tensor_tensor(conv, window, w, conv, ALU.mult, ALU.add)
                                    else:
                                        ins = dve.tensor_scalar(conv, window, w, None, ALU.mult)
                                    ins.then_inc(s["taps_done"], 1)
                                if u == len(CONV_DVE) - 1 and tap in LAST_TAPS:
                                    prepare(first, 0, LAST_TAPS[tap])
                        prepare(first, 0, "input")
                        dve.wait_ge(s["dx_ready"], first.i + 1)
                        for h in range(DH):
                            scan_input(first.step, 0, 0, h)
                        dve.wait_ge(s["x_ready"], img.scan(len(X_ORDER)) + len(X_ORDER))
                        scans(dve, img, chunk)
                        dve.wait_ge(s["y_merged"], img.scan(CHUNKS) + CHUNKS)
                        for t in range(NCH):
                            dve.wait_ge(s["on_mean"], a + (t + 1))
                            dve.tensor_tensor(Y[:, :, tok(t)], Y[:, :, tok(t)], both(PS[:, t]), ALU.subtract)\
                               .then_inc(s["on_cent"], 1)
                        dve.wait_ge(s["gates_loaded"], img.scan(16) + 16)
                        for t in range(NCH):
                            dve.wait_ge(s["on_rstd"], a + (t + 1))
                            for h in range(DH):
                                dve.scalar_tensor_tensor(Y[:, h, tok(t)], Y[:, h, tok(t)], wv("onorm_w", h, 1), RSTD[:, t],
                                                         ALU.mult, ALU.mult).then_inc(s["on_norm"], 1)
                            for h in range(DH):
                                dve.wait_ge(s["on_norm"], img.scan(NCH * DH) + (t * DH + h + 1))
                                dve.scalar_tensor_tensor(Y[:, h, tok(t)], Y[:, h, tok(t)], wv("onorm_b", h, 1), X0[:, h, tok(t)],
                                                         ALU.add, ALU.mult).then_inc(s["gated"], 1)
                        dve.wait_ge(s["residual_loaded"], img.all(16) + 16)
                        for t in range(NCH):
                            dve.wait_ge(s["oproj"], a + (t + 1))
                            dve.tensor_tensor(XI[:, tok(t)], XI[:, tok(t)], PS[:, t], ALU.add).then_inc(s["res_done"], 1)
                        layernorm(img, 1, XI, wv("ln2_w"), wv("ln2_b"))
                        for t in range(NCH):
                            dve.wait_ge(s["fc2_done"], a + (t + 1))
                            if t >= 2:
                                dve.wait_ge(s[f"out_stored{t % 2}"], (img.all(NCH // 2) + t // 2) * 16)
                            dve.scalar_tensor_tensor(OT[:, t % 2], PS[:, 6 + t % 2], wv("fc2_b"), XI[:, tok(t)],
                                                     ALU.add, ALU.add).then_inc(s["out_ready"], 1)
                    else:
                        g = img.own(NCH)
                        for t in range(NCH):
                            dve.wait_ge(s["g_branch"], img.own(2 * NCH) + (2 * t + 2))
                            dve.tensor_tensor(X0[:, 0, tok(t)], X0[:, 0, tok(t)], X0[:, 1, tok(t)], ALU.mult)\
                               .then_inc(s["g_mult"], 1)
                        dve.wait_ge(s["g_mult"], g + NCH)
                        dve.tensor_reduce(SMALL[:, 8:9], X0[:, 0], AX_X, ALU.add).then_inc(s["g_gap"], 1)
                        dve.wait_ge(s["g_att"], img.own(1) + 1)
                        dve.tensor_scalar(DIAG[:, 0], wg_("w2"), SMALL[:, 9:10], None, ALU.mult).then_inc(s["g_w2s"], 1)
                        dve.wait_ge(s["residual_loaded"], img.all(16) + 16)
                        for t in range(NCH):
                            dve.wait_ge(s["g_scaled"], g + (t + 1))
                            dve.tensor_tensor(XI[:, tok(t)], XI[:, tok(t)], X0[:, 1, tok(t)], ALU.add).then_inc(s["g_res"], 1)
                        layernorm(img, 1, XI, wg_("ln2_w"), wg_("ln2_b"))

                        def result(t):
                            dve.wait_ge(s["g_o"], g + (t + 1))
                            if t >= 2:
                                dve.wait_ge(s[f"out_stored{t % 2}"], (img.all(NCH // 2) + t // 2) * 16)
                            dve.tensor_tensor(OT[:, t % 2], GL[:, t % 2, 2], XI[:, tok(t)], ALU.add).then_inc(s["out_ready"], 1)

                        for t in range(NCH):
                            dve.wait_ge(s["g_c1"], g + (t + 1))
                            if t >= 2:
                                dve.wait_ge(s["g_wf2"], g + (t - 1))
                            dve.scalar_tensor_tensor(GL[:, t % 2, 1], PS[:, 2 * (t % 3) + 1], wg_("bf1", 1, 1), GL[:, t % 2, 0],
                                                     ALU.add, ALU.mult).then_inc(s["g_c"], 1)
                            if t:
                                result(t - 1)
                        result(NCH - 1)

        @block.scalar
        def _(act):
            def layernorm(img, which, eps):
                base = img.all(2 * NCH) + which * NCH
                act.preload_act_table_set(LN_EXP)
                for t in range(NCH):
                    act.wait_ge(s["ln_cent"], base + (t + 1))
                    act.activation(SQ4[:, t], XN[:, tok(t)], ACT.Square).then_inc(s["ln_sq"], 1)
                for t in range(NCH):
                    act.wait_ge(s["ln_var"], base + (t + 1))
                    act.activation(RSTD[:, t], PS[:, t], ACT.Ln, bias=col(eps)).then_inc(s["ln_log"], 1)
                    act.wait_ge(s["ln_log"], base + (t + 1))
                    act.activation(RSTD[:, t], RSTD[:, t], ACT.Exp, scale=-0.5).then_inc(s["ln_rstd"], 1)

            def prepare(i, par, op, first=False):
                if op == "raw":
                    act.wait_ge(s["proj_ready"], i + 1)
                    act.activation(RAW[:, :], PB, ACT.Identity, bias=col(K_ROW)).then_inc(s["raw_ready"], 1)
                if op == "hi":
                    act.wait_ge(s["raw_ready"], i + 1)
                    act.activation(PARTS[:, par], RAW[:, :], ACT.Copy).then_inc(s["hi_ready"], 1)
                if op == "mid":
                    act.wait_ge(s["rest_ready"], i + 1)
                    act.activation(PARTS[64:96, par], PB[64:96], ACT.Copy).then_inc(s["mid_ready"], 1)
                if op == "low":
                    act.wait_ge(s["tail_ready"], i + 1)
                    act.activation(PARTS[96:128, par], PB[96:128], ACT.Copy).then_inc(s["parts_ready"], 1)
                h = 1 if op.endswith("1") else 0
                if op in ("abs0", "abs1"):
                    act.wait_ge(s["v_ready"], i * DH + (h + 1))
                    if h == 0 and not first:
                        act.wait_ge(s["log1p_ready"], i)
                    act.activation(EXPV[:, h], PB, ACT.Abs).then_inc(s["abs_done"], 1)
                if op in ("relu0", "relu1"):
                    act.activation(DELTA[par][:, h], PB, ACT.Relu).then_inc(s["v_used"], 1)
                if op in ("exp0", "exp1"):
                    act.wait_ge(s["abs_done"], i * DH + (h + 1))
                    act.activation(EXPV[:, h], EXPV[:, h], ACT.Exp, scale=-1.0).then_inc(s["e_ready"], 1)
                if op in ("log0", "log1"):
                    act.wait_ge(s["e_ready"], i * DH + (h + 1))
                    act.activation(LOGV[:, h], EXPV[:, h], ACT.Ln, bias=1.0).then_inc(s["ln_ready"], 1)

            def save(c, n, last_chunk):
                source = ZERO[:, :] if last_chunk else HS[n % RING][:, :, c.last()]
                act.activation(CARRY[:, n], source, ACT.Copy).then_inc(s["carry_ready"], 1)

            def take_sums(c):
                act.activation(c.out(), c.sums(), ACT.Copy).then_inc(s["y_merged"], 1)

            def chunk(c, prev, nxt, par):
                final = nxt is None or nxt.k != c.k
                for n in range(N):
                    st = c.step + n
                    act.wait_ge(s["c_ready"], st + 1)
                    if prev or n >= RING:
                        act.wait_ge(s["readout_ready"], st - (RING - 1))
                    act.activation(CS[:, n % RING], CB, ACT.Copy).then_inc(s["c_copied"], 1)
                    if n == 0:
                        act.wait_ge(s["delta_ready"], c.i + 1)
                    for h in range(DH):
                        if prev or n:
                            act.wait_ge(s["state_ready"], st * DH + (h - 1))
                        a = (c.k * DH + h) * N + n
                        act.activation(DAB[:, h], DELTA[par][:, h], ACT.Exp, scale=ANEG[:, a:a + 1])\
                           .then_inc(s["decay_ready"], 1)
                    if n == MERGE and prev:
                        act.wait_ge(s["ysum_done"], c.step)
                    if n:
                        save(c, n - 1, final)
                    elif prev:
                        save(prev, N - 1, prev.k != c.k)
                    if n == MERGE and prev:
                        take_sums(prev)
                    if nxt:
                        for op in ACT_SLOTS.get(n, ()):
                            prepare(nxt.i, 1 - par, op)
                    if n == TURN and c.k == DIRS[0]:
                        cols = c.pos * ROWS
                        cols = slice(cols, cols + ROWS) if isinstance(c.pos, int) else bass.ds(cols, ROWS)
                        act.activation(X1[:, :, c.tokens()].rearrange("p h (c r) -> p h c r", r=HW),
                                       X0[:, :, :].rearrange("p h (r c) -> p h c r", c=HW)[:, :, cols, :], ACT.Copy)\
                           .then_inc(s["turned"], 1)

            act.wait_ge(s["consts_loaded"], 32)
            act.wait_ge(s["carry_cleared"], 2)
            for layer, (kind, _, gelu) in enumerate(layers):
                act.wait_ge(s["weights_loaded"], 16 * (layer + 1))
                lay = Image(layer, 0)
                if kind == "scan":
                    act.activation(ANEG[:, :], wv("A_log"), ACT.Exp).then_inc(s["a_exp"], 1)
                else:
                    act.wait_ge(s["g_small"], 2)
                with act.Fori(0, NB) as b:
                    img = Image(layer, b)
                    layernorm(img, 0, K_EPS5 if kind == "scan" else K_EPS6)
                    if kind == "scan":
                        a = img.scan(NCH)
                        for t in range(NCH):
                            bank = 4 * (t % 2)
                            act.wait_ge(s["xx_ready"], a + (t + 1))
                            act.activation(PAD[:, :, 1 + ROWS * t:1 + ROWS * (t + 1), 1:1 + HW],
                                           PS[:, bank:bank + 2].rearrange("p h (r c) -> p h r c", c=HW), ACT.Copy)\
                               .then_inc(s["padded"], 1)
                            act.wait_ge(s["z_ready"], a + (t + 1))
                            if t >= 2:
                                act.wait_ge(s[f"gate_stored{t % 2}"], (img.scan(NCH // 2) + t // 2) * 16)
                            act.activation(SZT[t % 2], PS[:, bank + 2:bank + 4], ACT.Silu).then_inc(s["gate_ready"], 1)
                        first = Chunk(img, 0, 0)
                        for what in FINISH:
                            if what in range(len(CONV_DVE)):
                                half, t, parts = CONV_DVE[what]
                                act.wait_ge(s["taps_done"], img.scan(TAPS[-1]) + TAPS[what + 1])
                                part = X0[:, half, t * CH:(t + parts) * CH]
                                act.activation(part, part, ACT.Silu, bias=wv("conv_b", half, 1)).then_inc(s["x_ready"], 1)
                            elif what.startswith("pe"):
                                t = int(what[2:])
                                act.wait_ge(s["conv0_ready"], img.scan(CONV_PE) + (t + 1))
                                act.activation(X0[:, 0, tok(t)], PS[:, t % 4], ACT.Silu, bias=wv("conv_b", 0, 1))\
                                   .then_inc(s["x_ready"], 1)
                            else:
                                if what == "abs0":
                                    for q in range(2):
                                        act.wait_ge(s[f"gate_stored{q}"], (img.scan(NCH // 2) + NCH // 2) * 16)
                                if what == "exp0":
                                    act.preload_act_table_set(LN_EXP)
                                prepare(first.i, 0, what, True)
                        act.preload_act_table_set(LN_EXP)
                        act.wait_ge(s["x_ready"], img.scan(len(X_ORDER)) + len(X_ORDER))
                        act.wait_ge(s["derived"], img.scan_layer * 7 + 7)
                        scans(act, img, chunk)
                        end = img.scan(STEPS) + STEPS
                        act.wait_ge(s["state_ready"], end * DH)
                        save(Chunk(img, K - 1, NCH - 1), N - 1, True)
                        act.wait_ge(s["ysum_done"], end)
                        take_sums(Chunk(img, K - 1, NCH - 1))
                        for t in range(NCH):
                            act.wait_ge(s["on_cent"], a + (t + 1))
                            act.activation(SQ8[:, t], Y[:, :, tok(t)], ACT.Square).then_inc(s["on_sq"], 1)
                        for t in range(NCH):
                            act.wait_ge(s["on_var"], a + (t + 1))
                            act.activation(RSTD[:, t], PS[:, t], ACT.Ln, bias=col(K_EPS5)).then_inc(s["on_log"], 1)
                            act.wait_ge(s["on_log"], a + (t + 1))
                            act.activation(RSTD[:, t], RSTD[:, t], ACT.Exp, scale=-0.5).then_inc(s["on_rstd"], 1)
                        layernorm(img, 1, K_EPS5)
                        for t in range(NCH):
                            if t >= 2:
                                act.wait_ge(s["fc2_done"], a + (t - 1))
                            for p in range(2):
                                act.wait_ge(s["fc1_done"], img.scan(2 * NCH) + (2 * t + p + 1))
                                for i in range(2):
                                    f = 2 * p + i
                                    ins = act.activation(GL[:, t % 2, f], PS[:, 2 * ((2 * t + p) % 3) + i], gelu,
                                                         bias=wv("fc1_b", f, 1))
                                ins.then_inc(s["gelu_done"], 1)
                    else:
                        g = img.own(NCH)
                        for t in range(NCH):
                            act.wait_ge(s["g_w1"], g + (t + 1))
                            for e in range(2):
                                act.activation(X0[:, e, tok(t)], PS[:, 2 * (t % 4) + e], ACT.Identity,
                                               bias=SMALL[:, e:e + 1], scale=wg_("wdw", e, 1)).then_inc(s["g_branch"], 1)
                        act.wait_ge(s["g_att_ps"], img.own(1) + 1)
                        act.activation(SMALL[:, 9:10], PS[:, 0, 0:1], ACT.Identity, bias=wg_("bse"), scale=1.0 / L)\
                           .then_inc(s["g_att"], 1)
                        for t in range(NCH):
                            act.wait_ge(s["g_w2"], g + (t + 1))
                            act.activation(X0[:, 1, tok(t)], PS[:, t], ACT.Identity, bias=SMALL[:, 2:3], scale=wg_("beta"))\
                               .then_inc(s["g_scaled"], 1)
                        layernorm(img, 1, K_EPS6)

                        def scaled(t):
                            act.wait_ge(s["g_wf2"], g + (t + 1))
                            if t >= 2:
                                act.wait_ge(s["out_ready"], img.results(t - 1))
                            act.activation(GL[:, t % 2, 2], PS[:, 6 + t % 2], ACT.Identity, bias=SMALL[:, 3:4], scale=wg_("gamma"))\
                               .then_inc(s["g_o"], 1)

                        for t in range(NCH):
                            act.wait_ge(s["g_wf1"], g + (t + 1))
                            if t >= 2:
                                act.wait_ge(s["g_c"], g + (t - 1))
                            act.activation(GL[:, t % 2, 0], PS[:, 2 * (t % 3)], ACT.Identity, bias=wg_("bf1", 0, 1))\
                               .then_inc(s["g_c1"], 1)
                            if t:
                                scaled(t - 1)
                        scaled(NCH - 1)

        @block.gpsimd
        def _(pool):
            def prepare(i, par, op):
                if op == "error":
                    pool.wait_ge(s["round_ready"], i + 1)
                    pool.tensor_tensor(ROUND[par], EXPV, ROUND[par], ALU.subtract).then_inc(s["err_ready"], 1)
                if op == "log1p":
                    pool.wait_ge(s["ln_ready"], i * DH + DH)
                    pool.wait_ge(s["err_ready"], i + 1)
                    pool.tensor_tensor(LOGV, LOGV, ROUND[par], ALU.add).then_inc(s["log1p_ready"], 1)

            def chunk(c, prev, nxt, par):
                for n in range(N):
                    st = c.step + n
                    pool.wait_ge(s["c_copied"], st + 1)
                    if prev or n >= RING:
                        pool.wait_ge(s["ysum_done"], st - (RING - 1))
                    pool.wait_ge(s["state_ready"], st * DH + DH)
                    pool.tensor_tensor(HC[:, n % RING], HS[n % RING], both(CS[:, n % RING]), ALU.mult).then_inc(s["readout_ready"], 1)
                    if nxt and n in POOL_SLOTS:
                        prepare(nxt.i, 1 - par, POOL_SLOTS[n])

            for layer, (kind, _, _) in enumerate(layers):
                if kind != "scan":
                    continue
                with pool.Fori(0, NB) as b:
                    img = Image(layer, b)
                    a = img.scan(NCH)
                    for op in POOL_SLOTS.values():
                        prepare(Chunk(img, 0, 0).i, 0, op)
                    scans(pool, img, chunk)
                    pool.wait_ge(s["y_merged"], img.scan(CHUNKS) + CHUNKS)
                    for t in range(NCH):
                        pool.tensor_tensor(SQ8[:, t, 0], Y[:, 0, tok(t)], Y[:, 1, tok(t)], ALU.add).then_inc(s["on_half"], 1)
                    for t in range(NCH):
                        pool.wait_ge(s["on_sq"], a + (t + 1))
                        pool.tensor_tensor(SQ8[:, t, 0], SQ8[:, t, 0], SQ8[:, t, 1], ALU.add).then_inc(s["on_sum"], 1)


_V_NAMES = {0: ("ln1_w", "ln1_b", "dt_w", "dt_b", "A_log", "onorm_w", "onorm_b", "ln2_w", "ln2_b"),
            1: ("norm1_w", "norm1_b", "dt_projs_w", "dt_projs_b", "A_logs", "out_norm_w", "out_norm_b", "norm2_w", "norm2_b")}


def _cols(v):
    return np.ascontiguousarray(v.reshape(-1, P).T)


def _scan_weights(inputs, layer):
    names = _V_NAMES[min(layer, 1)]
    ln1w, ln1b, dtw, dtb, alog, onw, onb, ln2w, ln2b = (inputs[f"L{layer}_conv_{n}"] for n in names)
    g = {n: inputs[f"L{layer}_conv_{n}"] for n in ("in_proj_w", "conv_w", "conv_b", "x_proj_w", "Ds", "out_proj_w",
                                                   "fc1_w", "fc1_b", "fc2_w", "fc2_b")}
    flip = (lambda a: a) if layer == 0 else (lambda a: a.T)
    xp = g["x_proj_w"].reshape(K, R + 2 * N, DH, P).transpose(3, 0, 2, 1)
    dt, bc = xp[..., :R], xp[..., R:]
    gap = np.zeros((P, K, DH, 2 * N - R), np.float32)
    x_proj = np.concatenate([bc, dt, gap, bc, bc], axis=-1).reshape(P, -1)
    step = np.zeros((P, K, DH * P), np.float32)
    step[DT0:DT0 + R] = dtw.transpose(2, 0, 1)
    step[DT0 + R] = dtb
    parts = dict(
        in_proj=flip(g["in_proj_w"]), conv_w=g["conv_w"].reshape(DH, P, 9).transpose(1, 0, 2).reshape(P, -1),
        x_proj=x_proj, dt_w=step.reshape(P, -1),
        A_log=alog.reshape(K, DH, P, N).transpose(2, 0, 1, 3).reshape(P, -1),
        Ds=g["Ds"].reshape(K, DH, P).transpose(2, 0, 1).reshape(P, -1),
        onorm_w=_cols(onw), onorm_b=_cols(onb),
        out_proj=flip(g["out_proj_w"]).reshape(DH, P, C).transpose(1, 0, 2).reshape(P, -1),
        ln1_w=_cols(ln1w), ln1_b=_cols(ln1b), ln2_w=_cols(ln2w), ln2_b=_cols(ln2b),
        fc1=flip(g["fc1_w"]), fc1_b=_cols(g["fc1_b"]),
        fc2=flip(g["fc2_w"]).reshape(FF, P, C).transpose(1, 0, 2).reshape(P, -1), fc2_b=_cols(g["fc2_b"]),
        conv_b=_cols(g["conv_b"]))
    return np.ascontiguousarray(np.concatenate([parts[n] for n in V_COLS], axis=1))


def _gated_weights(inputs):
    g = {n: inputs[f"L2_conv_{n}"] for n in ("w1", "wse", "w2", "wf1", "wf2", "b1", "wdw", "bdw", "bse", "b2", "bf1", "bf2",
                                             "beta", "gamma", "ln1_scale", "ln1_bias", "ln2_scale", "ln2_bias")}
    g.update(ln1_w=g["ln1_scale"], ln1_b=g["ln1_bias"], ln2_w=g["ln2_scale"], ln2_b=g["ln2_bias"])
    mats = ("w1", "wse", "w2", "wf1", "wf2")
    return np.ascontiguousarray(np.concatenate([g[n] if n in mats else _cols(g[n]) for n in G_COLS], axis=1))


def _constants():
    c = np.zeros((P, KW), np.float32)
    c[:, K_ID:K_ID + P] = np.eye(P)
    c[:, K_128:K_128 + P] = 1.0 / P
    c[:, K_256:K_256 + P] = 1.0 / (DH * P)
    c[:, K_EPS5], c[:, K_EPS6] = 1e-5, 1e-6
    c[DT0 + R, K_ROW] = 1.0
    sel = np.zeros((P, 2 * N, P), np.float32)
    for row in range(2 * N):
        for part in (0, 64, 96):
            sel[part + row, row, :] = 1.0
    return c, sel


def kernel(**inputs):
    import concourse.bacc as _bacc
    from concourse.bass_utils import run_bass_kernel_spmd as _run
    inputs = {n: np.asarray(a) for n, a in inputs.items()}
    consts, sel = _constants()
    x = np.ascontiguousarray(inputs["x"].reshape(NB, L, C).transpose(0, 2, 1))
    arrays = {"in_x": x, "consts": consts, "sel": sel.astype(mybir.dt.np(BF16)),
              "w0": _scan_weights(inputs, 0), "w1": _scan_weights(inputs, 1), "wg": _gated_weights(inputs),
              "w3": _scan_weights(inputs, 3)}
    nc = _bacc.Bacc("TRN2", target_bir_lowering=False, num_devices=1)
    args = [nc.dram_tensor(n, a.shape, mybir.dt.from_np(a.dtype), kind="ExternalInput").ap() for n, a in arrays.items()]
    args.append(nc.dram_tensor("out_0", (NB, C, L), F32, kind="ExternalOutput").ap())
    program(nc, *args)
    r = _run(nc, [arrays], core_ids=[0])
    return np.ascontiguousarray(r.results[0]["out_0"].transpose(0, 2, 1)).reshape(NB, HW, HW, C)
```
